# Optimizing a Trainium2 kernel written in Bass

```python
import numpy as np
import jax
import jax.numpy as jnp

def _softmax(x, axis=-1):
    return jax.nn.softmax(x, axis=axis)

def _gelu(x):
    return jax.nn.gelu(x, approximate=True)

def _silu(x):
    return jax.nn.silu(x)

def _sigmoid(x):
    return jax.nn.sigmoid(x)

def _layernorm(x, axis=-1, eps=1e-05):
    m = jnp.mean(x, axis=axis, keepdims=True)
    v = jnp.var(x, axis=axis, keepdims=True)
    return (x - m) / jnp.sqrt(v + eps)

def _scatter_add(tgt, idx, src, axis=0):
    return tgt.at[idx].add(src)

def _segment_sum(src, seg, n):
    return jax.ops.segment_sum(src, seg, n)
kernel_name = 'mk_lm_tower_d2_tok_ids1024_r4_35c69e'

def setup_inputs(seed: int=0):
    np.random.seed(seed)
    _w = jnp.asarray

    def _rec_inputs():
        import jax
        import jax.numpy as jnp
        _rk = jax.random.key(seed)
        x = jax.random.randint(jax.random.fold_in(_rk, 1), (2, 1024), 0, 31983, jnp.int32)
        return x
    x = _rec_inputs()

    def _L0_tok_setup():
        import jax, jax.numpy as jnp
        import numpy as np
        VOCAB = 8000
        FEATURES = 256
        key = jax.random.key(seed)
        k1, k2 = jax.random.split(key)
        input_ids = jax.random.randint(k1, (2, 512), 0, VOCAB, dtype=jnp.int32)
        embedding = jax.random.normal(k2, (VOCAB, FEATURES), dtype=jnp.float32) * 0.02
        return {'input_ids': input_ids, 'embedding': embedding}
    _L0_tok_all = _L0_tok_setup()
    _L0_tok_in = {k: v for k, v in _L0_tok_all.items() if k in ('embedding',)}
    del _L0_tok_all

    def _L0_attn_setup():
        import jax, jax.numpy as jnp
        import numpy as np
        N_EMBD = 256
        N_HEAD = 16
        HEAD_DIM = N_EMBD // N_HEAD
        KV_RANK = 64
        Q_RANK = 128
        ROPE_DIM = 32
        B, T = (2, 512)
        EPS = 1e-06

        def _rope_tables(T, dim):
            inv_freq = 1.0 / 10000.0 ** (np.arange(0, dim, 2, dtype=np.float32) / dim)
            t = np.arange(T, dtype=np.float32)
            freqs = np.outer(t, inv_freq)
            emb = np.concatenate([freqs, freqs], -1)
            return (jnp.asarray(np.cos(emb)), jnp.asarray(np.sin(emb)))

        def _apply_rope(x, cos, sin):
            d2 = x.shape[-1] // 2
            x1, x2 = (x[..., :d2], x[..., d2:])
            rot = jnp.concatenate([-x2, x1], axis=-1)
            return x * cos[None, None, :, :] + rot * sin[None, None, :, :]
        key = jax.random.key(seed)
        ks = jax.random.split(key, 10)

        def w(k, fan_in, fan_out):
            return jax.random.normal(k, (fan_in, fan_out), dtype=jnp.float32) * fan_in ** (-0.5)
        return {'x': jax.random.normal(ks[0], (B, T, N_EMBD), dtype=jnp.float32), 'W_kv': w(ks[1], N_EMBD, KV_RANK), 'g_kv': jnp.ones((KV_RANK,), dtype=jnp.float32), 'W_kdec': w(ks[2], KV_RANK, N_HEAD * HEAD_DIM), 'W_vdec': w(ks[3], KV_RANK, N_HEAD * HEAD_DIM), 'W_q': w(ks[4], N_EMBD, Q_RANK), 'W_qdec': w(ks[5], Q_RANK, N_HEAD * HEAD_DIM), 'W_krope': w(ks[6], N_EMBD, N_HEAD * ROPE_DIM), 'W_qrope': w(ks[7], Q_RANK, N_HEAD * ROPE_DIM), 'W_o': w(ks[8], N_HEAD * HEAD_DIM, N_EMBD)}
    _L0_attn_all = _L0_attn_setup()
    _L0_attn_in = {k: v for k, v in _L0_attn_all.items() if k in ('W_kv', 'g_kv', 'W_kdec', 'W_vdec', 'W_q', 'W_qdec', 'W_krope', 'W_qrope', 'W_o')}
    del _L0_attn_all

    def _L0_ffn_setup():
        import jax, jax.numpy as jnp
        import numpy as np
        DIM = 256
        DEPTH = 6
        HEADS = 16
        DIM_HEAD = 64
        WINDOW = 64
        INNER = HEADS * DIM_HEAD
        DIM_INNER = int(DIM * 4 * 2 / 3)
        QK_SCALE = 8.0

        def shift_tokens(t):
            a, s = jnp.split(t, 2, -1)
            s = jnp.pad(s, ((0, 0), (1, 0), (0, 0)))[:, :-1]
            return jnp.concatenate([a, s], -1)

        def l2norm(t):
            return t / jnp.maximum(jnp.linalg.norm(t, axis=-1, keepdims=True), 1e-12)

        def rotate_half(x):
            x1, x2 = jnp.split(x, 2, -1)
            return jnp.concatenate([-x2, x1], -1)

        def rotary_tables(n):
            half = jnp.arange(0, DIM_HEAD, 2, dtype=jnp.float32)
            inv_freq = 1.0 / 10000.0 ** (half / DIM_HEAD)
            t = jnp.arange(n, dtype=jnp.float32)
            freqs = t[:, None] * inv_freq[None, :]
            freqs = jnp.concatenate([freqs, freqs], -1)
            base_scale = (half + 0.4 * DIM_HEAD) / (1.4 * DIM_HEAD)
            power = (t - n // 2) / (WINDOW // 2)
            scale = base_scale[None, :] ** power[:, None]
            scale = jnp.concatenate([scale, scale], -1)
            return (freqs, scale)

        def local_attention(q, k, v):
            b, h, n, d = q.shape
            w = WINDOW
            nw = n // w
            bq = q.reshape(b, h, nw, w, d)
            bk = k.reshape(b, h, nw, w, d)
            bv = v.reshape(b, h, nw, w, d)

            def look(t):
                p = jnp.pad(t, ((0, 0), (0, 0), (1, 0), (0, 0), (0, 0)))
                return jnp.concatenate([p[:, :, :nw], p[:, :, 1:]], axis=3)
            bk2, bv2 = (look(bk), look(bv))
            seq = jnp.arange(n).reshape(nw, w)
            seq_p = jnp.pad(seq, ((1, 0), (0, 0)), constant_values=-1)
            jt = jnp.concatenate([seq_p[:nw], seq_p[1:]], axis=1)
            it = seq[:, :, None]
            jb = jt[:, None, :]
            mask = (it < jb) | (it > jb + w) | (jb == -1)
            sim = jnp.einsum('bhwie,bhwje->bhwij', bq, bk2) * QK_SCALE
            sim = jnp.where(mask, -jnp.finfo(sim.dtype).max, sim)
            attn = jax.nn.softmax(sim, -1)
            out = jnp.einsum('bhwij,bhwje->bhwie', attn, bv2)
            return out.reshape(b, h, n, d)

        def attn_layer(x, Wqkv, qs, ksc, Wo):
            b, n, _ = x.shape
            qkv = x @ Wqkv
            q, k, v = jnp.split(qkv, 3, -1)
            sh = lambda t: t.reshape(b, n, HEADS, DIM_HEAD).transpose(0, 2, 1, 3)
            q, k, v = (sh(q), sh(k), sh(v))
            q = l2norm(q) * qs
            k = l2norm(k) * ksc
            freqs, scale = rotary_tables(n)
            cos, sin = (jnp.cos(freqs), jnp.sin(freqs))
            q = q * cos * scale + rotate_half(q) * sin * scale
            inv = 1.0 / scale
            k = k * cos * inv + rotate_half(k) * sin * inv
            out = local_attention(q, k, v)
            out = out.transpose(0, 2, 1, 3).reshape(b, n, INNER)
            return out @ Wo

        def ffn_layer(x, g, bln, W1, b1, W2, b2):
            mu = x.mean(-1, keepdims=True)
            var = ((x - mu) ** 2).mean(-1, keepdims=True)
            xn = (x - mu) / jnp.sqrt(var + 1e-05) * g + bln
            hg = xn @ W1 + b1
            a, gate = jnp.split(hg, 2, -1)
            return a * jax.nn.gelu(gate, approximate=False) @ W2 + b2
        key = jax.random.key(seed)
        ks = jax.random.split(key, 8)
        B, N = (2, 512)
        init = lambda k, shape: jax.random.normal(k, shape, jnp.float32) * 0.02
        return {'x': jax.random.normal(ks[0], (B, N, DIM), jnp.float32), 'Wqkv': init(ks[1], (DEPTH, DIM, 3 * INNER)), 'q_scale': jnp.ones((DEPTH, DIM_HEAD), jnp.float32), 'k_scale': jnp.ones((DEPTH, DIM_HEAD), jnp.float32), 'Wo': init(ks[2], (DEPTH, INNER, DIM)), 'ln_g': jnp.ones((DEPTH, DIM), jnp.float32), 'ln_b': jnp.zeros((DEPTH, DIM), jnp.float32), 'W1': init(ks[3], (DEPTH, DIM, 2 * DIM_INNER)), 'b1': jnp.zeros((DEPTH, 2 * DIM_INNER), jnp.float32), 'W2': init(ks[4], (DEPTH, DIM_INNER, DIM)), 'b2': jnp.zeros((DEPTH, DIM), jnp.float32)}
    _L0_ffn_all = _L0_ffn_setup()
    _L0_ffn_in = {k: v for k, v in _L0_ffn_all.items() if k in ('Wqkv', 'q_scale', 'k_scale', 'Wo', 'ln_g', 'ln_b', 'W1', 'b1', 'W2', 'b2')}
    del _L0_ffn_all

    def _L1_attn_setup():
        import jax, jax.numpy as jnp
        import numpy as np
        D_MODEL = 256
        N_HEADS = 4
        KEY_DIM = 256
        VALUE_DIM = 512
        DK = KEY_DIM // N_HEADS
        DV = VALUE_DIM // N_HEADS
        LOW_RANK = 16
        GATE_NORM = 16.0
        EPS = 1e-05

        def _gla_scan(q, k, v, gk):
            B, H, L, dk = q.shape
            dv = v.shape[-1]
            qs = jnp.moveaxis(q, 2, 0)
            ks_ = jnp.moveaxis(k, 2, 0)
            vs = jnp.moveaxis(v, 2, 0)
            gs = jnp.moveaxis(gk, 2, 0)

            def step(S, inp):
                q_t, k_t, v_t, g_t = inp
                S = S * jnp.exp(g_t)[..., None] + k_t[..., None] * v_t[..., None, :]
                o_t = jnp.einsum('bhk,bhkv->bhv', q_t, S)
                return (S, o_t)
            S0 = jnp.zeros((B, H, dk, dv), q.dtype)
            _, os = jax.lax.scan(step, S0, (qs, ks_, vs, gs))
            return jnp.moveaxis(os, 0, 2)
        key = jax.random.key(seed)
        ks = jax.random.split(key, 10)
        B, L = (2, 512)
        gain = 2.0 ** (-2.5)

        def xavier(k, shape, g=gain):
            fan_in, fan_out = (shape[0], shape[1])
            a = g * np.sqrt(6.0 / (fan_in + fan_out))
            return jax.random.uniform(k, shape, jnp.float32, -a, a)
        return {'x': jax.random.normal(ks[0], (B, L, D_MODEL), jnp.float32), 'Wq': xavier(ks[1], (D_MODEL, KEY_DIM)), 'Wk': xavier(ks[2], (D_MODEL, KEY_DIM)), 'Wv': xavier(ks[3], (D_MODEL, VALUE_DIM)), 'Wg': xavier(ks[4], (D_MODEL, VALUE_DIM)), 'gk_w1': xavier(ks[5], (D_MODEL, LOW_RANK)), 'gk_w2': xavier(ks[6], (LOW_RANK, KEY_DIM)), 'gk_b2': jnp.zeros((KEY_DIM,), jnp.float32), 'g_norm_w': jnp.ones((DV,), jnp.float32), 'Wo': xavier(ks[7], (VALUE_DIM, D_MODEL))}
    _L1_attn_all = _L1_attn_setup()
    _L1_attn_in = {k: v for k, v in _L1_attn_all.items() if k in ('Wq', 'Wk', 'Wv', 'Wg', 'gk_w1', 'gk_w2', 'gk_b2', 'g_norm_w', 'Wo')}
    del _L1_attn_all

    def _L1_ffn_setup():
        import jax, jax.numpy as jnp
        import numpy as np
        from jax import lax
        DIM = 256
        INTER = 128
        N_EXPERTS = 16
        TOPK = 4
        ROUTE_SCALE = 2.5
        VOCAB = 8000

        def _silu_and_mul(gu):
            gate, up = jnp.split(gu, 2, axis=-1)
            return jax.nn.silu(gate) * up
        key = jax.random.key(seed)
        ks = jax.random.split(key, 8)
        x = jax.random.normal(ks[0], (2, 128, DIM), dtype=jnp.float32)
        input_ids = jax.random.randint(ks[1], (2, 128), 0, VOCAB)
        s = 0.02
        gate_w = jax.random.normal(ks[2], (N_EXPERTS, DIM), dtype=jnp.float32) * s
        gate_b = jax.random.normal(ks[3], (N_EXPERTS,), dtype=jnp.float32) * s
        w13 = jax.random.normal(ks[4], (N_EXPERTS, 2 * INTER, DIM), dtype=jnp.float32) * s
        w2 = jax.random.normal(ks[5], (N_EXPERTS, DIM, INTER), dtype=jnp.float32) * s
        w13_s = jax.random.normal(ks[6], (2 * INTER, DIM), dtype=jnp.float32) * s
        w2_s = jax.random.normal(ks[7], (DIM, INTER), dtype=jnp.float32) * s
        return {'x': x, 'input_ids': input_ids, 'gate_w': gate_w, 'gate_b': gate_b, 'w13': w13, 'w2': w2, 'w13_s': w13_s, 'w2_s': w2_s}
    _L1_ffn_all = _L1_ffn_setup()
    _L1_ffn_in = {k: v for k, v in _L1_ffn_all.items() if k in ('input_ids', 'gate_w', 'gate_b', 'w13', 'w2', 'w13_s', 'w2_s')}
    del _L1_ffn_all
    return {'x': x, 'L0_tok_embedding': _L0_tok_in['embedding'], 'L0_attn_W_kv': _L0_attn_in['W_kv'], 'L0_attn_g_kv': _L0_attn_in['g_kv'], 'L0_attn_W_kdec': _L0_attn_in['W_kdec'], 'L0_attn_W_vdec': _L0_attn_in['W_vdec'], 'L0_attn_W_q': _L0_attn_in['W_q'], 'L0_attn_W_qdec': _L0_attn_in['W_qdec'], 'L0_attn_W_krope': _L0_attn_in['W_krope'], 'L0_attn_W_qrope': _L0_attn_in['W_qrope'], 'L0_attn_W_o': _L0_attn_in['W_o'], 'L0_ffn_Wqkv': _L0_ffn_in['Wqkv'], 'L0_ffn_q_scale': _L0_ffn_in['q_scale'], 'L0_ffn_k_scale': _L0_ffn_in['k_scale'], 'L0_ffn_Wo': _L0_ffn_in['Wo'], 'L0_ffn_ln_g': _L0_ffn_in['ln_g'], 'L0_ffn_ln_b': _L0_ffn_in['ln_b'], 'L0_ffn_W1': _L0_ffn_in['W1'], 'L0_ffn_b1': _L0_ffn_in['b1'], 'L0_ffn_W2': _L0_ffn_in['W2'], 'L0_ffn_b2': _L0_ffn_in['b2'], 'L1_attn_Wq': _L1_attn_in['Wq'], 'L1_attn_Wk': _L1_attn_in['Wk'], 'L1_attn_Wv': _L1_attn_in['Wv'], 'L1_attn_Wg': _L1_attn_in['Wg'], 'L1_attn_gk_w1': _L1_attn_in['gk_w1'], 'L1_attn_gk_w2': _L1_attn_in['gk_w2'], 'L1_attn_gk_b2': _L1_attn_in['gk_b2'], 'L1_attn_g_norm_w': _L1_attn_in['g_norm_w'], 'L1_attn_Wo': _L1_attn_in['Wo'], 'L1_ffn_input_ids': _L1_ffn_in['input_ids'], 'L1_ffn_gate_w': _L1_ffn_in['gate_w'], 'L1_ffn_gate_b': _L1_ffn_in['gate_b'], 'L1_ffn_w13': _L1_ffn_in['w13'], 'L1_ffn_w2': _L1_ffn_in['w2'], 'L1_ffn_w13_s': _L1_ffn_in['w13_s'], 'L1_ffn_w2_s': _L1_ffn_in['w2_s']}

def reference(x, L0_tok_embedding, L0_attn_W_kv, L0_attn_g_kv, L0_attn_W_kdec, L0_attn_W_vdec, L0_attn_W_q, L0_attn_W_qdec, L0_attn_W_krope, L0_attn_W_qrope, L0_attn_W_o, L0_ffn_Wqkv, L0_ffn_q_scale, L0_ffn_k_scale, L0_ffn_Wo, L0_ffn_ln_g, L0_ffn_ln_b, L0_ffn_W1, L0_ffn_b1, L0_ffn_W2, L0_ffn_b2, L1_attn_Wq, L1_attn_Wk, L1_attn_Wv, L1_attn_Wg, L1_attn_gk_w1, L1_attn_gk_w2, L1_attn_gk_b2, L1_attn_g_norm_w, L1_attn_Wo, L1_ffn_input_ids, L1_ffn_gate_w, L1_ffn_gate_b, L1_ffn_w13, L1_ffn_w2, L1_ffn_w13_s, L1_ffn_w2_s):
    import jax
    import jax.numpy as jnp

    def _L0_tok_ref(input_ids, embedding):
        import jax, jax.numpy as jnp
        import numpy as np
        VOCAB = 8000
        FEATURES = 256
        iota = jax.lax.iota(jnp.int32, VOCAB)
        one_hot = (input_ids[..., None] == iota).astype(embedding.dtype)
        return jnp.dot(one_hot, embedding)

    def _L0_attn_ref(x, W_kv, g_kv, W_kdec, W_vdec, W_q, W_qdec, W_krope, W_qrope, W_o):
        import jax, jax.numpy as jnp
        import numpy as np
        N_EMBD = 256
        N_HEAD = 16
        HEAD_DIM = N_EMBD // N_HEAD
        KV_RANK = 64
        Q_RANK = 128
        ROPE_DIM = 32
        B, T = (2, 512)
        EPS = 1e-06

        def _rope_tables(T, dim):
            inv_freq = 1.0 / 10000.0 ** (np.arange(0, dim, 2, dtype=np.float32) / dim)
            t = np.arange(T, dtype=np.float32)
            freqs = np.outer(t, inv_freq)
            emb = np.concatenate([freqs, freqs], -1)
            return (jnp.asarray(np.cos(emb)), jnp.asarray(np.sin(emb)))

        def _apply_rope(x, cos, sin):
            d2 = x.shape[-1] // 2
            x1, x2 = (x[..., :d2], x[..., d2:])
            rot = jnp.concatenate([-x2, x1], axis=-1)
            return x * cos[None, None, :, :] + rot * sin[None, None, :, :]
        Bx, Tx, C = x.shape
        kv_c = x @ W_kv
        kv_c = kv_c * jax.lax.rsqrt(jnp.mean(kv_c * kv_c, axis=-1, keepdims=True) + EPS) * g_kv
        q_c = x @ W_q

        def heads(y, d):
            return y.reshape(Bx, Tx, N_HEAD, d).transpose(0, 2, 1, 3)
        k_content = heads(kv_c @ W_kdec, HEAD_DIM)
        v = heads(kv_c @ W_vdec, HEAD_DIM)
        q_content = heads(q_c @ W_qdec, HEAD_DIM)
        k_rope = heads(x @ W_krope, ROPE_DIM)
        q_rope = heads(q_c @ W_qrope, ROPE_DIM)
        cos, sin = _rope_tables(Tx, ROPE_DIM)
        q_rope = _apply_rope(q_rope, cos, sin)
        k_rope = _apply_rope(k_rope, cos, sin)
        q = jnp.concatenate([q_content, q_rope], axis=-1)
        k = jnp.concatenate([k_content, k_rope], axis=-1)
        scale = 1.0 / jnp.sqrt(jnp.float32(q.shape[-1]))
        scores = jnp.einsum('bhqd,bhkd->bhqk', q, k) * scale
        causal = jnp.tril(jnp.ones((Tx, Tx), dtype=bool))
        scores = jnp.where(causal[None, None], scores, jnp.float32(-jnp.inf))
        attn = jax.nn.softmax(scores, axis=-1)
        out = jnp.einsum('bhqk,bhkd->bhqd', attn, v)
        out = out.transpose(0, 2, 1, 3).reshape(Bx, Tx, N_HEAD * HEAD_DIM)
        return out @ W_o

    def _L0_ffn_ref(x, Wqkv, q_scale, k_scale, Wo, ln_g, ln_b, W1, b1, W2, b2):
        import jax, jax.numpy as jnp
        import numpy as np
        DIM = 256
        DEPTH = 6
        HEADS = 16
        DIM_HEAD = 64
        WINDOW = 64
        INNER = HEADS * DIM_HEAD
        DIM_INNER = int(DIM * 4 * 2 / 3)
        QK_SCALE = 8.0

        def shift_tokens(t):
            a, s = jnp.split(t, 2, -1)
            s = jnp.pad(s, ((0, 0), (1, 0), (0, 0)))[:, :-1]
            return jnp.concatenate([a, s], -1)

        def l2norm(t):
            return t / jnp.maximum(jnp.linalg.norm(t, axis=-1, keepdims=True), 1e-12)

        def rotate_half(x):
            x1, x2 = jnp.split(x, 2, -1)
            return jnp.concatenate([-x2, x1], -1)

        def rotary_tables(n):
            half = jnp.arange(0, DIM_HEAD, 2, dtype=jnp.float32)
            inv_freq = 1.0 / 10000.0 ** (half / DIM_HEAD)
            t = jnp.arange(n, dtype=jnp.float32)
            freqs = t[:, None] * inv_freq[None, :]
            freqs = jnp.concatenate([freqs, freqs], -1)
            base_scale = (half + 0.4 * DIM_HEAD) / (1.4 * DIM_HEAD)
            power = (t - n // 2) / (WINDOW // 2)
            scale = base_scale[None, :] ** power[:, None]
            scale = jnp.concatenate([scale, scale], -1)
            return (freqs, scale)

        def local_attention(q, k, v):
            b, h, n, d = q.shape
            w = WINDOW
            nw = n // w
            bq = q.reshape(b, h, nw, w, d)
            bk = k.reshape(b, h, nw, w, d)
            bv = v.reshape(b, h, nw, w, d)

            def look(t):
                p = jnp.pad(t, ((0, 0), (0, 0), (1, 0), (0, 0), (0, 0)))
                return jnp.concatenate([p[:, :, :nw], p[:, :, 1:]], axis=3)
            bk2, bv2 = (look(bk), look(bv))
            seq = jnp.arange(n).reshape(nw, w)
            seq_p = jnp.pad(seq, ((1, 0), (0, 0)), constant_values=-1)
            jt = jnp.concatenate([seq_p[:nw], seq_p[1:]], axis=1)
            it = seq[:, :, None]
            jb = jt[:, None, :]
            mask = (it < jb) | (it > jb + w) | (jb == -1)
            sim = jnp.einsum('bhwie,bhwje->bhwij', bq, bk2) * QK_SCALE
            sim = jnp.where(mask, -jnp.finfo(sim.dtype).max, sim)
            attn = jax.nn.softmax(sim, -1)
            out = jnp.einsum('bhwij,bhwje->bhwie', attn, bv2)
            return out.reshape(b, h, n, d)

        def attn_layer(x, Wqkv, qs, ksc, Wo):
            b, n, _ = x.shape
            qkv = x @ Wqkv
            q, k, v = jnp.split(qkv, 3, -1)
            sh = lambda t: t.reshape(b, n, HEADS, DIM_HEAD).transpose(0, 2, 1, 3)
            q, k, v = (sh(q), sh(k), sh(v))
            q = l2norm(q) * qs
            k = l2norm(k) * ksc
            freqs, scale = rotary_tables(n)
            cos, sin = (jnp.cos(freqs), jnp.sin(freqs))
            q = q * cos * scale + rotate_half(q) * sin * scale
            inv = 1.0 / scale
            k = k * cos * inv + rotate_half(k) * sin * inv
            out = local_attention(q, k, v)
            out = out.transpose(0, 2, 1, 3).reshape(b, n, INNER)
            return out @ Wo

        def ffn_layer(x, g, bln, W1, b1, W2, b2):
            mu = x.mean(-1, keepdims=True)
            var = ((x - mu) ** 2).mean(-1, keepdims=True)
            xn = (x - mu) / jnp.sqrt(var + 1e-05) * g + bln
            hg = xn @ W1 + b1
            a, gate = jnp.split(hg, 2, -1)
            return a * jax.nn.gelu(gate, approximate=False) @ W2 + b2
        for i in range(DEPTH):
            x = attn_layer(shift_tokens(x), Wqkv[i], q_scale[i], k_scale[i], Wo[i]) + x
            x = ffn_layer(shift_tokens(x), ln_g[i], ln_b[i], W1[i], b1[i], W2[i], b2[i]) + x
        return x

    def _L1_attn_ref(x, Wq, Wk, Wv, Wg, gk_w1, gk_w2, gk_b2, g_norm_w, Wo):
        import jax, jax.numpy as jnp
        import numpy as np
        D_MODEL = 256
        N_HEADS = 4
        KEY_DIM = 256
        VALUE_DIM = 512
        DK = KEY_DIM // N_HEADS
        DV = VALUE_DIM // N_HEADS
        LOW_RANK = 16
        GATE_NORM = 16.0
        EPS = 1e-05

        def _gla_scan(q, k, v, gk):
            B, H, L, dk = q.shape
            dv = v.shape[-1]
            qs = jnp.moveaxis(q, 2, 0)
            ks_ = jnp.moveaxis(k, 2, 0)
            vs = jnp.moveaxis(v, 2, 0)
            gs = jnp.moveaxis(gk, 2, 0)

            def step(S, inp):
                q_t, k_t, v_t, g_t = inp
                S = S * jnp.exp(g_t)[..., None] + k_t[..., None] * v_t[..., None, :]
                o_t = jnp.einsum('bhk,bhkv->bhv', q_t, S)
                return (S, o_t)
            S0 = jnp.zeros((B, H, dk, dv), q.dtype)
            _, os = jax.lax.scan(step, S0, (qs, ks_, vs, gs))
            return jnp.moveaxis(os, 0, 2)
        B, L, _ = x.shape
        scale = DK ** (-0.5)

        def heads(t, d):
            return t.reshape(B, L, N_HEADS, d).transpose(0, 2, 1, 3)
        q = heads(x @ Wq, DK) * scale
        k = heads(x @ Wk, DK)
        v = heads(x @ Wv, DV)
        gk = heads(jax.nn.log_sigmoid(x @ gk_w1 @ gk_w2 + gk_b2) / GATE_NORM, DK)
        o = _gla_scan(q, k, v, gk)
        o = o.transpose(0, 2, 1, 3)
        g = (x @ Wg).reshape(B, L, N_HEADS, DV)
        rms = o * jax.lax.rsqrt(jnp.mean(o * o, axis=-1, keepdims=True) + EPS)
        o = rms * g_norm_w * (g * jax.nn.sigmoid(g))
        o = o.reshape(B, L, VALUE_DIM)
        return o @ Wo

    def _L1_ffn_ref(x, input_ids, gate_w, gate_b, w13, w2, w13_s, w2_s):
        import jax, jax.numpy as jnp
        import numpy as np
        from jax import lax
        DIM = 256
        INTER = 128
        N_EXPERTS = 16
        TOPK = 4
        ROUTE_SCALE = 2.5
        VOCAB = 8000

        def _silu_and_mul(gu):
            gate, up = jnp.split(gu, 2, axis=-1)
            return jax.nn.silu(gate) * up
        B, S, D = x.shape
        xt = x.reshape(-1, D)
        T = xt.shape[0]
        scores = jax.nn.sigmoid(xt.astype(jnp.float32) @ gate_w.T)
        biased = scores + gate_b
        _, idx = lax.top_k(biased, TOPK)
        w = jnp.take_along_axis(scores, idx, axis=-1)
        w = w / jnp.sum(w, axis=-1, keepdims=True)
        w = w * ROUTE_SCALE
        comb = jnp.zeros((T, N_EXPERTS), jnp.float32)
        comb = comb.at[jnp.arange(T)[:, None], idx].add(w)
        comb = comb.astype(x.dtype)

        def expert_body(y, args):
            w13_e, w2_e, c_e = args
            h = _silu_and_mul(xt @ w13_e.T)
            return (y + c_e[:, None] * (h @ w2_e.T), None)
        y, _ = lax.scan(expert_body, jnp.zeros_like(xt), (w13, w2, comb.T))
        y = y + _silu_and_mul(xt @ w13_s.T) @ w2_s.T
        return y.astype(x.dtype).reshape(B, S, D)
    h = _L0_tok_ref(x, L0_tok_embedding)
    h = h + _L0_attn_ref(_layernorm(h, axis=-1), L0_attn_W_kv, L0_attn_g_kv, L0_attn_W_kdec, L0_attn_W_vdec, L0_attn_W_q, L0_attn_W_qdec, L0_attn_W_krope, L0_attn_W_qrope, L0_attn_W_o)
    h = h + _L0_ffn_ref(_layernorm(h, axis=-1), L0_ffn_Wqkv, L0_ffn_q_scale, L0_ffn_k_scale, L0_ffn_Wo, L0_ffn_ln_g, L0_ffn_ln_b, L0_ffn_W1, L0_ffn_b1, L0_ffn_W2, L0_ffn_b2)
    h = h + _L1_attn_ref(_layernorm(h, axis=-1), L1_attn_Wq, L1_attn_Wk, L1_attn_Wv, L1_attn_Wg, L1_attn_gk_w1, L1_attn_gk_w2, L1_attn_gk_b2, L1_attn_g_norm_w, L1_attn_Wo)
    h = h + _L1_ffn_ref(_layernorm(h, axis=-1), L1_ffn_input_ids, L1_ffn_gate_w, L1_ffn_gate_b, L1_ffn_w13, L1_ffn_w2, L1_ffn_w13_s, L1_ffn_w2_s)
    return h

_drawn_inputs = setup_inputs


def setup_inputs(seed=0):
    import zlib

    import numpy as np

    out = dict(_drawn_inputs(seed))
    spreads = {'L0_attn_g_kv': (1.0, 0.2),
     'L0_ffn_q_scale': (1.0, 0.6),
     'L0_ffn_k_scale': (1.0, 0.6),
     'L0_ffn_ln_g': (1.0, 0.6),
     'L0_ffn_ln_b': (0.0, 0.765),
     'L0_ffn_b1': (0.0, 0.1),
     'L0_ffn_b2': (0.0, 0.1),
     'L1_attn_gk_b2': (0.0, 0.8),
     'L1_attn_g_norm_w': (1.0, 0.6)}
    factors = {'L1_attn_Wq': 4.201,
     'L1_attn_Wk': 4.317,
     'L1_attn_Wv': 4.084,
     'L1_attn_Wg': 4.143,
     'L1_attn_gk_w1': 8.0,
     'L1_attn_gk_w2': 8.0,
     'L1_attn_Wo': 4.189,
     'L1_ffn_gate_w': 5.275,
     'L1_ffn_gate_b': 8.0,
     'L1_ffn_w13': 4.437,
     'L1_ffn_w2': 4.407,
     'L1_ffn_w13_s': 5.659,
     'L1_ffn_w2_s': 6.075}
    for name, (base, spread) in spreads.items():
        noise = np.random.default_rng([zlib.crc32(name.encode()), seed]).standard_normal(out[name].shape)
        drawn = base * np.exp(spread * noise) if base else spread * noise
        out[name] = jnp.asarray(drawn.astype(out[name].dtype))
    for name, factor in factors.items():
        out[name] = (out[name] * factor).astype(out[name].dtype)
    return out
```

```python
from contextlib import ExitStack

import concourse.bass as bass
from concourse import mybir

F32 = mybir.dt.float32
ALU = mybir.AluOpType
ACT = mybir.ActivationFunctionType
AX = mybir.AxisListType.X
P = 128


def tower_consts(TILES):
    import numpy as np
    P, HD, WIN = 128, 64, 64
    T = TILES * P
    f32 = np.float32
    half = np.arange(0, HD, 2, dtype=f32)
    inv_freq = (f32(1.0) / np.power(f32(10000.0), half / f32(HD))).astype(f32)
    t = np.arange(T, dtype=f32)
    freqs = t[:, None] * inv_freq[None, :]
    freqs = np.concatenate([freqs, freqs], -1)
    base = (half + f32(0.4 * HD)) / f32(1.4 * HD)
    power = (t - T // 2) / f32(WIN // 2)
    scale = np.power(base[None, :], power[:, None]).astype(f32)
    scale = np.concatenate([scale, scale], -1)
    inv = (f32(1.0) / scale).astype(f32)
    sign = np.where(np.arange(HD) < HD // 2, -1.0, 1.0).astype(f32)
    cos, sin = np.cos(freqs), np.sin(freqs) * sign
    QK_SCALE = 8.0
    trig = np.stack([np.stack([cos * scale * QK_SCALE, sin * scale * QK_SCALE], 1), np.stack([cos * inv, sin * inv], 1)], 1)
    trig = trig.reshape(TILES, P, 4 * HD).astype(f32)
    i = np.arange(P)[:, None]
    c = np.arange(WIN + P)[None, :]
    ok = (i <= c) & (c <= i + WIN)
    mask = np.repeat(np.where(ok, 0.0, -1e30)[None], TILES, 0)
    mask[0, :, :WIN] = -1e30
    before, own = mask[:, :, :WIN], mask[:, :, WIN:]
    keep = np.ones((TILES, P, 1))
    keep[TILES - 1] = 0.0
    band = np.concatenate([own, before, before, own, keep], -1).astype(f32)
    ident = np.eye(P, dtype=f32)
    shift = np.zeros((2, P, P), f32)
    shift[0, np.arange(P - 1), np.arange(1, P)] = 1.0
    shift[1, P - 1, 0] = 1.0
    return ident, trig, band, shift


def mla_consts(T):
    import numpy as np
    f32 = np.float32
    dim = 32
    inv_freq = 1.0 / 10000.0 ** (np.arange(0, dim, 2, dtype=f32) / dim)
    freqs = np.outer(np.arange(T, dtype=f32), inv_freq)
    emb = np.concatenate([freqs, freqs], -1)
    sign = np.where(np.arange(dim) < dim // 2, -1.0, 1.0).astype(f32)
    rope = np.stack([np.cos(emb), np.sin(emb) * sign], 1).astype(f32)
    causal = np.where(np.arange(128)[None, :] <= np.arange(128)[:, None], 0.0, -1e30).astype(f32)
    return rope, causal


def mla_project(nc, ids_dram, emb_dram, ident_dram, rope_dram, w_x_dram, g_kv_dram, w_kvdec_dram, w_q_dram,
                emb, qT_all, kT_all, v_all):
    VOCAB, D = emb_dram.shape
    KC = D // P
    RANK = w_kvdec_dram.shape[0]
    QRANK = w_q_dram.shape[0]
    HEADS, CONT, ROPE, SLOT = 16, 16, 32, 64
    RH = ROPE // 2
    PAIRS = HEADS // 2
    KR = HEADS * ROPE
    HC = HEADS * CONT
    NB = 2
    TILES = ids_dram.shape[1] // NB
    VD = CONT + 1

    with ExitStack() as ctx:
        ctx.enter_context(nc.cleanup_on_exit())
        def sb(name, shape, dt=F32):
            return ctx.enter_context(nc.sbuf_tensor("mp_" + name, shape, dt))

        def sem(name):
            return nc.alloc_semaphore("mp_" + name)

        bank = [ctx.enter_context(nc.psum_tensor(f"mp_bank{j}", [P, 512], F32)) for j in range(8)]
        ident = sb("ident", [P, P])
        rope = sb("rope", [P, TILES, 2, ROPE])
        w_x = sb("w_x", [P, KC, KR + RANK + QRANK])
        w_kvdec = sb("w_kvdec", [RANK, 2 * HC])
        w_q = sb("w_q", [P, KR + HC])
        g_kv = sb("g_kv", [P, RANK])
        minus_half = sb("minus_half", [P, 1])
        ids = sb("ids", [P, NB * TILES], mybir.dt.int32)
        idsf = sb("idsf", [P, NB * TILES])
        below = sb("below", [P, NB * TILES])
        rows = sb("rows", [P, NB * TILES], mybir.dt.int32)
        stats = [sb(f"stats{b}", [P, 6]) for b in range(NB)]
        mv = [sb(f"mv{b}", [P, 2]) for b in range(NB)]
        ve = [sb(f"ve{b}", [P, 1]) for b in range(NB)]
        rstd = [sb(f"rstd{b}", [P, 1]) for b in range(NB)]
        xn = [sb(f"xn{b}", [P, D]) for b in range(NB)]
        xT = [sb(f"xT{b}", [P, KC, P]) for b in range(NB)]
        sq = [sb(f"sq{b}", [P, RANK]) for b in range(NB)]
        ssum = [sb(f"ssum{b}", [P, 1]) for b in range(NB)]
        ms = [sb(f"ms{b}", [P, 1]) for b in range(NB)]
        rms = [sb(f"rms{b}", [P, 1]) for b in range(NB)]
        comp = [sb(f"comp{b}", [P, RANK + QRANK]) for b in range(NB)]
        compT = [sb(f"compT{b}", [P, 2, P]) for b in range(NB)]
        packed = sb("packed", [P, 2, HEADS, SLOT])
        cross = sb("cross", [P, 2, HEADS, ROPE])

        USES = [2, 1, 1, 1, 1, 1, 2, 2]
        full = [sem(f"full{j}") for j in range(8)]
        drained = [sem(f"drained{j}") for j in range(8)]
        const_in, ready, ids_in, rows_ready, gathered = (sem("const_in"), sem("ready"), sem("ids_in"),
                                                         sem("rows_ready"), sem("gathered"))
        ONES = ["stats_ready", "mv_ready", "ve_ready", "rstd_ready", "xn_ready", "squared", "ms_ready", "rms_ready",
                "comp_ready"]
        s = {n: sem(n) for n in ONES}
        TWOS = ["crossed", "straight", "packed_ready"]
        s.update({n: sem(n) for n in TWOS})
        id_step, act_gate, dve_gate = sem("id_step"), sem("act_gate"), sem("dve_gate")

        def nth(per, k, pos=0):
            return per * (k + 2) + pos + 1

        def in0(i, use):
            return 4 * (i + 1) + use + 1

        block = ctx.enter_context(nc.Block())

        @block.sync
        def _(sp):
            for j in range(8):
                sp.sem_inc(full[j], 2 * USES[j])
                sp.sem_inc(drained[j], 2 * USES[j])
            for n in ONES:
                sp.sem_inc(s[n], 2)
            for n in TWOS:
                sp.sem_inc(s[n], 4)
            sp.dma_start(ids[:, :], ids_dram).then_inc(ids_in, 16)
            for dst, src in ((ident[:, :], ident_dram),
                             (rope[:, :, :, :], rope_dram.rearrange("(i p) a d -> p i a d", p=P)),
                             (w_x[:, :, :], w_x_dram.rearrange("(c p) n -> p c n", p=P)),
                             (w_kvdec[:, :], w_kvdec_dram), (w_q[:, :], w_q_dram),
                             (g_kv[:, :], g_kv_dram.partition_broadcast(P))):
                sp.dma_start(dst, src).then_inc(const_in, 16)

        @block.vector
        def _(dve):
            nc.vector.memset(minus_half[:, :], -0.5)
            nc.vector.memset(v_all[:, :, :, :], 1.0)
            nc.vector.memset(packed[:, :, :, :], 0.0)
            nc.vector.memset(emb[:, :, :], 0.0).then_inc(ready, 1)
            dve.wait_ge(ids_in, 16)
            nc.vector.tensor_copy(idsf[:, :], ids[:, :]).then_inc(id_step, 1)
            dve.wait_ge(id_step, 1)
            nc.vector.tensor_scalar(idsf[:, :], idsf[:, :], float(VOCAB), -1.0, ALU.min, ALU.max).then_inc(id_step, 1)
            dve.wait_ge(id_step, 2)
            nc.vector.tensor_scalar(below[:, :], idsf[:, :], 0.0, float(VOCAB + 1), ALU.is_lt, ALU.mult)\
                .then_inc(id_step, 1)
            dve.wait_ge(id_step, 3)
            nc.vector.tensor_tensor(rows[:, :], idsf[:, :], below[:, :], ALU.add).then_inc(rows_ready, 1)
            dve.wait_ge(const_in, 96)
            dve.wait_ge(gathered, 16 * NB * TILES)

            def norm(i, b):
                k = 2 * i + b
                src = emb[:, bass.ds(b * TILES + i, 1), :].rearrange("p a d -> p (a d)")
                nc.vector.bn_stats(stats[b][:, :], src).then_inc(s["stats_ready"], 1)
                dve.wait_ge(s["stats_ready"], nth(1, k))
                dve.sem_inc(dve_gate, 1)
                nc.vector.bn_aggr(mv[b][:, :], stats[b][:, :]).then_inc(s["mv_ready"], 1)
                dve.wait_ge(s["mv_ready"], nth(1, k))
                nc.vector.tensor_scalar(ve[b][:, :], mv[b][:, 1:2], 1e-5, None, ALU.add).then_inc(s["ve_ready"], 1)
                dve.wait_ge(s["rstd_ready"], nth(1, k))
                dve.wait_ge(full[0], in0(i - 1, b))
                dve.sem_inc(dve_gate, 1)
                nc.vector.tensor_scalar(xn[b][:, :], src, mv[b][:, 0:1], rstd[b][:, :], ALU.subtract, ALU.mult)\
                    .then_inc(s["xn_ready"], 1)

            def compress(i, b):
                k = 2 * i + b
                dve.wait_ge(s["squared"], nth(1, k))
                nc.vector.tensor_scalar(ms[b][:, :], ssum[b][:, :], 1.0 / RANK, 1e-6, ALU.mult, ALU.add)\
                    .then_inc(s["ms_ready"], 1)
                dve.wait_ge(s["rms_ready"], nth(1, k))
                dve.wait_ge(full[0], in0(i - 1, 2 + b))
                nc.vector.scalar_tensor_tensor(comp[b][:, 0:RANK], bank[2][:, 0:RANK], rms[b][:, :], g_kv[:, :],
                                               ALU.mult, ALU.mult)
                nc.vector.tensor_copy(comp[b][:, RANK:RANK + QRANK], bank[2][:, RANK:RANK + QRANK])\
                    .then_inc(drained[2], 1)

            def rotate(i, b, h):
                k = 2 * i + b
                j = (4, 1)[h]
                src = bank[j][:, :].rearrange("p (n d) -> p n d", d=ROPE)
                dve.wait_ge(full[6 + h], nth(2, k - 1, 1))
                dve.wait_ge(full[j], nth(1, k))
                dve.sem_inc(dve_gate, 1)
                cos = rope[:, bass.ds(i, 1), 0, :].to_broadcast([P, HEADS, ROPE])
                nc.vector.tensor_tensor(packed[:, h, :, CONT:CONT + ROPE], src, cos, ALU.mult)\
                    .then_inc(s["straight"], 1)
                for first, other in ((0, RH), (RH, 0)):
                    sin = rope[:, bass.ds(i, 1), 1, first:first + RH].to_broadcast([P, HEADS, RH])
                    last = nc.vector.tensor_tensor(cross[:, h, :, first:first + RH], src[:, :, other:other + RH], sin,
                                                   ALU.mult)
                last.then_inc(drained[j], 1)
                dve.wait_ge(drained[j], nth(1, k))
                nc.vector.tensor_tensor(packed[:, h, :, CONT:CONT + ROPE], packed[:, h, :, CONT:CONT + ROPE],
                                        cross[:, h, :, :], ALU.add).then_inc(s["packed_ready"], 1)

            with dve.Fori(0, TILES) as i:
                for b in range(NB):
                    norm(i, b)
                for b in range(NB):
                    compress(i, b)
                for b in range(NB):
                    rotate(i, b, 1)
                    rotate(i, b, 0)
                    for g in range(2):
                        dve.wait_ge(full[7], nth(2, 2 * i + b, g))
                        dve.sem_inc(dve_gate, 1)
                        nc.vector.tensor_copy(kT_all[:, b * PAIRS + 4 * g:b * PAIRS + 4 * g + 4, bass.ds(i * P, P)],
                                              bank[7][:, :].rearrange("p (n t) -> p n t", t=P)).then_inc(drained[7], 1)

        @block.gpsimd
        def _(pool):
            pool.wait_ge(ready, 1)
            pool.wait_ge(rows_ready, 1)
            for g in range(NB * TILES):
                pool.indirect_dma_start(
                    out=emb[:, g, :], out_offset=None, in_=emb_dram,
                    in_offset=bass.IndirectOffsetOnAxis(ap=rows[:, g:g + 1].bitcast(mybir.dt.uint32), axis=0),
                    bounds_check=VOCAB - 1, oob_is_err=False).then_inc(gathered, 16)
            with pool.Fori(0, TILES) as i:
                for b in range(NB):
                    pool.wait_ge(s["ve_ready"], nth(1, 2 * i + b))
                    nc.gpsimd.tensor_tensor(rstd[b][:, :], ve[b][:, :], minus_half[:, :], ALU.pow)\
                        .then_inc(s["rstd_ready"], 1)
                for b in range(NB):
                    pool.wait_ge(s["ms_ready"], nth(1, 2 * i + b))
                    nc.gpsimd.tensor_tensor(rms[b][:, :], ms[b][:, :], minus_half[:, :], ALU.pow)\
                        .then_inc(s["rms_ready"], 1)

        @block.tensor
        def _(pe):
            def mm(out, lhsT, rhs, start, stop):
                return nc.tensor.matmul(out, lhsT, rhs, start=start, stop=stop)

            pe.wait_ge(const_in, 96)
            with pe.Fori(0, TILES) as i:
                for b in range(NB):
                    pe.wait_ge(s["xn_ready"], nth(1, 2 * i + b))
                    pe.wait_ge(drained[0], in0(i, b) - 1)
                    for c in range(KC):
                        last = nc.tensor.transpose(bank[0][:, c * P:(c + 1) * P], xn[b][:, c * P:(c + 1) * P],
                                                   ident[:, :])
                    last.then_inc(full[0], 1)
                for b in range(NB):
                    k = 2 * i + b
                    pe.wait_ge(drained[0], in0(i, b))
                    for j, cols in ((2, slice(KR, KR + RANK + QRANK)), (1, slice(0, KR))):
                        pe.wait_ge(drained[j], nth(1, k - 1))
                        for c in range(KC):
                            last = mm(bank[j][:, 0:cols.stop - cols.start], xT[b][:, c, :], w_x[:, c, cols],
                                      c == 0, c == KC - 1)
                        last.then_inc(full[j], 1)
                for b in range(NB):
                    pe.wait_ge(drained[2], nth(1, 2 * i + b))
                    pe.wait_ge(drained[0], in0(i, 2 + b) - 1)
                    nc.tensor.transpose(bank[0][:, P:2 * P], comp[b][:, RANK:RANK + QRANK], ident[:, :])
                    nc.tensor.transpose(bank[0][0:RANK, 0:P], comp[b][:, 0:RANK], ident[:, :]).then_inc(full[0], 1)
                for b in range(NB):
                    k = 2 * i + b
                    pe.wait_ge(drained[0], in0(i, 2 + b))
                    for j, x, w in ((3, compT[b][0:RANK, 0, :], w_kvdec[:, :]), (4, compT[b][:, 1, :], w_q[:, 0:KR]),
                                    (5, compT[b][:, 1, :], w_q[:, KR:KR + HC])):
                        pe.wait_ge(drained[j], nth(1, k - 1))
                        mm(bank[j][:, 0:w.shape[1]], x, w, True, True).then_inc(full[j], 1)
                    for h, content, pos in ((1, 3, 0), (0, 5, 1)):
                        pe.wait_ge(s["packed_ready"], nth(2, k, pos))
                        pe.wait_ge(drained[content], nth(1, k))
                        for g in range(2):
                            pe.wait_ge(drained[6 + h], nth(2, k, g) - 1)
                            for n in range(4):
                                a = 2 * (4 * g + n)
                                last = nc.tensor.transpose(bank[6 + h][:, n * P:(n + 1) * P],
                                                           packed[:, h, a:a + 2, :].rearrange("p n d -> p (n d)"),
                                                           ident[:, :])
                            last.then_inc(full[6 + h], 1)

        @block.scalar
        def _(act):
            act.wait_ge(ready, 1)
            with act.Fori(0, TILES) as i:
                for b in range(NB):
                    act.wait_ge(full[0], in0(i, b))
                    nc.scalar.copy(xT[b][:, :, :].rearrange("p c t -> p (c t)"), bank[0][:, 0:KC * P])\
                        .then_inc(drained[0], 1)
                for b in range(NB):
                    act.wait_ge(full[2], nth(1, 2 * i + b))
                    nc.scalar.activation(sq[b][:, :], bank[2][:, 0:RANK], ACT.Square, accum_out=ssum[b][:, :])\
                        .then_inc(s["squared"], 1)
                for b in range(NB):
                    act.wait_ge(full[0], in0(i, 2 + b))
                    nc.scalar.copy(compT[b][0:RANK, 0, :], bank[0][0:RANK, 0:P])
                    nc.scalar.copy(compT[b][:, 1, :], bank[0][:, P:2 * P]).then_inc(drained[0], 1)
                for b in range(NB):
                    k = 2 * i + b
                    act.wait_ge(full[3], nth(1, k))
                    act.wait_ge(full[7], nth(2, k - 1, 1))
                    act.sem_inc(act_gate, 1)
                    nc.scalar.copy(packed[:, 1, :, 0:CONT], bank[3][:, 0:HC].rearrange("p (n d) -> p n d", d=CONT))
                    values = v_all[:, b * PAIRS:(b + 1) * PAIRS, bass.ds(i, 1), :]\
                        .rearrange("p n a (e d) -> p (n a) e d", d=VD)
                    nc.scalar.copy(values[:, :, :, 0:CONT],
                                   bank[3][:, HC:2 * HC].rearrange("p (n e d) -> p n e d", e=2, d=CONT))\
                        .then_inc(drained[3], 1)
                    act.wait_ge(full[5], nth(1, k))
                    act.wait_ge(full[6], nth(2, k - 1, 1))
                    nc.scalar.copy(packed[:, 0, :, 0:CONT], bank[5][:, 0:HC].rearrange("p (n d) -> p n d", d=CONT))\
                        .then_inc(drained[5], 1)
                    for g in range(2):
                        act.wait_ge(full[6], nth(2, k, g))
                        act.sem_inc(act_gate, 1)
                        nc.scalar.copy(qT_all[:, b * PAIRS + 4 * g:b * PAIRS + 4 * g + 4, bass.ds(i * P, P)],
                                       bank[6][:, :].rearrange("p (n t) -> p n t", t=P)).then_inc(drained[6], 1)


def mla_attend(nc, ident_dram, causal_dram, qT_all, kT_all, v_all, o_all):
    PAIRS, T = qT_all.shape[1] // 2, qT_all.shape[2]
    ITERS = 2 * PAIRS
    TILES = T // P
    HALF_T = T // 2
    VD = v_all.shape[3] // 2
    CONT = VD - 1
    D = o_all.shape[2]
    SCALE = 48 ** -0.5
    UNITS = 2 * TILES

    with ExitStack() as ctx:
        ctx.enter_context(nc.cleanup_on_exit())
        def sb(name, shape, dt=F32):
            return ctx.enter_context(nc.sbuf_tensor("ma_" + name, shape, dt))

        def sem(name):
            return nc.alloc_semaphore("ma_" + name)

        ident = sb("ident", [P, P])
        causal = sb("causal", [P, P])
        qz = [sb(f"qz{e}", [P, T]) for e in range(2)]
        mx = [sb(f"mx{e}", [P, 1]) for e in range(2)]
        bias = [sb(f"bias{e}", [P, 1]) for e in range(2)]
        probs = [sb(f"probs{e}", [P, T]) for e in range(2)]
        pT = [sb(f"pT{j}", [P, 4, P]) for j in range(4)]
        rec = sb("rec", [P, 2])
        s_bank = [ctx.enter_context(nc.psum_tensor(f"ma_s{e}", [P, T], F32)) for e in range(2)]
        t_bank = [ctx.enter_context(nc.psum_tensor(f"ma_t{j}", [P, 512], F32)) for j in range(2)]
        o_bank = [ctx.enter_context(nc.psum_tensor(f"ma_o{j}", [P, 512], F32)) for j in range(2)]

        const_in, zeroed = sem("const_in"), sem("zeroed")
        q_in = [sem(f"q_in{j}") for j in range(2)]
        s_full, exp_done = [sem(f"s_full{e}") for e in range(2)], [sem(f"exp_done{e}") for e in range(2)]
        masked, mx_ready, bias_ready = ([sem(f"masked{e}") for e in range(2)], [sem(f"mx_ready{e}") for e in range(2)],
                                        [sem(f"bias_ready{e}") for e in range(2)])
        t_full, t_drained = [sem(f"t_full{j}") for j in range(2)], [sem(f"t_drained{j}") for j in range(2)]
        o_full, o_drained = [sem(f"o_full{j}") for j in range(2)], [sem(f"o_drained{j}") for j in range(2)]
        o_ready, rec_ready = sem("o_ready"), sem("rec_ready")
        dve_gate, sp_gate = sem("dve_gate"), sem("sp_gate")

        GROUPS = []
        for unit in range(UNITS):
            for first in range(0, unit // 2 + 1, 4):
                GROUPS.append((unit, first, min(4, unit // 2 + 1 - first)))
        IN_BANK = len(GROUPS) // 2
        assert len(GROUPS) % 4 == 0
        OB = TILES // 2

        def count(per, it, pos):
            return per * (it + 1) + pos + 1

        def within(it):
            if isinstance(it, int):
                return it
            return nc.s_assert_within(it, 0, ITERS - 1, skip_runtime_bounds_check_because="a pair's number")

        def ahead(it, following, unit, do):
            if unit + 2 < UNITS:
                do(it, unit + 2)
            elif following is not None:
                do(following, unit + 2 - UNITS)

        def groups_of(unit):
            return [g for g, (u, _, _) in enumerate(GROUPS) if u == unit]

        block = ctx.enter_context(nc.Block())

        @block.sync
        def _(sp):
            for e in range(2):
                for s in (s_full[e], exp_done[e], masked[e], mx_ready[e], bias_ready[e]):
                    sp.sem_inc(s, TILES)
                for s in (t_full[e], t_drained[e]):
                    sp.sem_inc(s, IN_BANK)
                for s in (o_full[e], o_drained[e]):
                    sp.sem_inc(s, OB)
            sp.sem_inc(rec_ready, TILES)
            sp.dma_start(ident[:, :], ident_dram).then_inc(const_in, 16)
            sp.dma_start(causal[:, :], causal_dram).then_inc(const_in, 16)
            sp.wait_ge(zeroed, 1)
            with sp.Fori(0, ITERS) as it:
                for j in range(2):
                    for e in range(2):
                        sp.wait_ge(s_full[e], count(TILES, it - 1, (j + 1) * TILES // 2 - 1))
                    sp.sem_inc(sp_gate, 1)
                    for e in range(2):
                        rows = slice(64 * e, 64 * e + 64)
                        sp.dma_start(qz[e][rows, j * HALF_T:(j + 1) * HALF_T],
                                     qT_all[rows, bass.ds(it, 1), j * HALF_T:(j + 1) * HALF_T]
                                     .rearrange("p a t -> p (a t)")).then_inc(q_in[j], 16)
            for j in range(2):
                sp.wait_ge(q_in[j], 32 * ITERS)

        @block.tensor
        def _(pe):
            def scores(it, unit):
                qt, e = unit // 2, unit % 2
                if e == 0 and qt in (0, TILES // 2):
                    pe.wait_ge(q_in[qt // (TILES // 2)], 32 * (it + 1))
                pe.wait_ge(exp_done[e], count(TILES, it, qt) - 1)
                for first in range(0, (qt + 1) * P, 512):
                    n = min(512, (qt + 1) * P - first)
                    last = nc.tensor.matmul(s_bank[e][:, first:first + n], qz[e][:, qt * P:(qt + 1) * P],
                                            kT_all[:, bass.ds(within(it), 1), first:first + n].rearrange("p a t -> p (a t)"),
                                            start=True, stop=True)
                last.then_inc(s_full[e], 1)

            def transpose_probs(it, unit):
                qt, e = unit // 2, unit % 2
                pe.wait_ge(exp_done[e], count(TILES, it, qt))
                for g in groups_of(unit):
                    _, first, n = GROUPS[g]
                    pe.wait_ge(t_drained[g % 2], count(IN_BANK, it, g // 2) - 1)
                    for a in range(n):
                        last = nc.tensor.transpose(t_bank[g % 2][:, a * P:(a + 1) * P],
                                                   probs[e][:, (first + a) * P:(first + a + 1) * P], ident[:, :])
                    last.then_inc(t_full[g % 2], 1)

            def weigh(it, unit):
                qt, e = unit // 2, unit % 2
                if e == 0:
                    pe.wait_ge(o_drained[qt % 2], count(OB, it, qt // 2) - 1)
                for g in groups_of(unit):
                    _, first, n = GROUPS[g]
                    pe.wait_ge(t_drained[g % 2], count(IN_BANK, it, g // 2))
                    for a in range(n):
                        kt = first + a
                        last = nc.tensor.matmul(o_bank[qt % 2][:, e * VD:(e + 1) * VD], pT[g % 4][:, a, :],
                                                v_all[:, bass.ds(within(it), 1), kt, e * VD:(e + 1) * VD]
                                                .rearrange("p a d -> p (a d)"), start=kt == 0, stop=kt == qt)
                if e == 1:
                    last.then_inc(o_full[qt % 2], 1)

            def pair(it, following):
                for unit in range(UNITS):
                    ahead(it, following, unit, scores)
                    transpose_probs(it, unit)
                    if unit:
                        weigh(it, unit - 1)
                weigh(it, UNITS - 1)

            pe.wait_ge(const_in, 32)
            scores(0, 0)
            scores(0, 1)
            with pe.Fori(0, ITERS - 1) as it:
                pair(it, it + 1)
            pair(ITERS - 1, None)

        @block.vector
        def _(dve):
            def stats(it, unit):
                qt, e = unit // 2, unit % 2
                own = s_bank[e][:, qt * P:(qt + 1) * P]
                dve.wait_ge(s_full[e], count(TILES, it, qt))
                nc.vector.tensor_tensor(own, own, causal[:, :], ALU.add).then_inc(masked[e], 1)
                dve.wait_ge(masked[e], count(TILES, it, qt))
                nc.vector.tensor_reduce(mx[e][:, :], s_bank[e][:, 0:(qt + 1) * P], AX, ALU.max).then_inc(mx_ready[e], 1)
                dve.wait_ge(exp_done[e], count(TILES, it, qt) - 1)
                dve.wait_ge(mx_ready[e], count(TILES, it, qt))
                nc.vector.tensor_scalar(bias[e][:, :], mx[e][:, :], -SCALE, None, ALU.mult).then_inc(bias_ready[e], 1)

            nc.vector.memset(qz[0][:, :], 0.0)
            nc.vector.memset(qz[1][:, :], 0.0).then_inc(zeroed, 1)
            dve.wait_ge(const_in, 32)
            def keep_o(it, qt):
                got = o_bank[qt % 2][:, 0:2 * VD].rearrange("p (e d) -> p e d", d=VD)
                before = (it, qt - 1) if qt else (it - 1, TILES - 1)
                dve.wait_ge(o_drained[before[1] % 2], count(OB, before[0], before[1] // 2))
                dve.wait_ge(o_full[qt % 2], count(OB, it, qt // 2))
                nc.vector.reciprocal(rec[:, :].unsqueeze(2), got[:, :, CONT:VD]).then_inc(rec_ready, 1)
                at = (it >> 3) * (TILES * D) + (it & 7) * (2 * CONT) + qt * D
                if not isinstance(it, int):
                    at = nc.s_assert_within(at, 0, 2 * TILES * D - 2 * CONT,
                                            skip_runtime_bounds_check_because="a pair's columns")
                dve.wait_ge(rec_ready, count(TILES, it, qt))
                dve.sem_inc(dve_gate, 1)
                nc.vector.tensor_tensor(
                    o_all[:, :, :].rearrange("p a d -> p (a d)")[:, bass.ds(at, 2 * CONT)]
                    .rearrange("p (e d) -> p e d", d=CONT), got[:, :, 0:CONT],
                    rec[:, :].unsqueeze(2).to_broadcast([P, 2, CONT]), ALU.mult).then_inc(o_drained[qt % 2], 1)

            def pair(it, following):
                for unit in range(UNITS):
                    ahead(it, following, unit, stats)
                    for g in groups_of(unit):
                        if g % 2 == 0:
                            n = GROUPS[g][2]
                            dve.wait_ge(t_full[0], count(IN_BANK, it, g // 2))
                            nc.vector.tensor_copy(pT[g % 4][:, 0:n, :].rearrange("p a t -> p (a t)"),
                                                  t_bank[0][:, 0:n * P]).then_inc(t_drained[0], 1)
                    if unit >= 2 and unit % 2 == 0:
                        keep_o(it, unit // 2 - 1)
                keep_o(it, TILES - 1)

            stats(0, 0)
            stats(0, 1)
            with dve.Fori(0, ITERS - 1) as it:
                pair(it, it + 1)
            pair(ITERS - 1, None)

        @block.scalar
        def _(act):
            def exponent(it, unit):
                qt, e = unit // 2, unit % 2
                before = (it, unit - 2) if unit >= 2 else (it - 1, UNITS - 2 + unit)
                g = groups_of(before[1])[-1]
                act.wait_ge(t_full[g % 2], count(IN_BANK, before[0], g // 2))
                act.wait_ge(bias_ready[e], count(TILES, it, qt))
                nc.scalar.activation(probs[e][:, 0:(qt + 1) * P], s_bank[e][:, 0:(qt + 1) * P], ACT.Exp,
                                     bias=bias[e][:, :], scale=SCALE).then_inc(exp_done[e], 1)

            def pair(it, following):
                for unit in range(UNITS):
                    ahead(it, following, unit, exponent)
                    for g in groups_of(unit):
                        if g % 2 == 1:
                            n = GROUPS[g][2]
                            act.wait_ge(t_full[1], count(IN_BANK, it, g // 2))
                            nc.scalar.copy(pT[g % 4][:, 0:n, :].rearrange("p a t -> p (a t)"),
                                           t_bank[1][:, 0:n * P]).then_inc(t_drained[1], 1)

            exponent(0, 0)
            exponent(0, 1)
            with act.Fori(0, ITERS - 1) as it:
                pair(it, it + 1)
            pair(ITERS - 1, None)


def mla_output(nc, ident_dram, o_all, emb, wo_dram, h1_dram, tower_in):
    D = wo_dram.shape[0]
    KC = D // P
    NB = 2
    TILES = emb.shape[1] // NB

    with ExitStack() as ctx:
        ctx.enter_context(nc.cleanup_on_exit())
        def sb(name, shape, dt=F32):
            return ctx.enter_context(nc.sbuf_tensor("mo_" + name, shape, dt))

        def sem(name):
            return nc.alloc_semaphore("mo_" + name)

        ident = sb("ident", [P, P])
        wo = sb("wo", [P, KC, D])
        minus_half = sb("minus_half", [P, 1])
        o = [sb(f"o{b}", [P, D]) for b in range(NB)]
        oT = [sb(f"oT{b}", [P, KC, P]) for b in range(NB)]
        h1 = [sb(f"h1{b}", [P, D]) for b in range(NB)]
        stats = [sb(f"stats{b}", [P, 6]) for b in range(NB)]
        mv = [sb(f"mv{b}", [P, 2]) for b in range(NB)]
        ve = [sb(f"ve{b}", [P, 1]) for b in range(NB)]
        rstd = [sb(f"rstd{b}", [P, 1]) for b in range(NB)]
        xn = [sb(f"xn{b}", [P, D]) for b in range(NB)]
        t_bank = [ctx.enter_context(nc.psum_tensor(f"mo_t{b}", [P, 512], F32)) for b in range(NB)]
        w_bank = [ctx.enter_context(nc.psum_tensor(f"mo_w{b}", [P, 512], F32)) for b in range(NB)]
        const_in, root_ready = sem("const_in"), sem("root_ready")
        NAMES = ["o_copied", "t_full", "t_drained", "w_full", "h1_ready", "stats_ready", "mv_ready", "ve_ready",
                 "rstd_ready", "xn_ready"]
        s = [{n: sem(f"{n}{b}") for n in NAMES} for b in range(NB)]
        h1_stored, xn_stored = [[sem(f"{n}{b}") for b in range(NB)] for n in ("h1_stored", "xn_stored")]
        act_gate, dve_gate, sp_gate = sem("act_gate"), sem("dve_gate"), sem("sp_gate")

        def now(i):
            return i + 2

        block = ctx.enter_context(nc.Block())

        @block.sync
        def _(sp):
            for b in range(NB):
                for n in NAMES:
                    sp.sem_inc(s[b][n], 1)
                sp.sem_inc(h1_stored[b], 16)
                sp.sem_inc(xn_stored[b], 16)
            sp.dma_start(ident[:, :], ident_dram).then_inc(const_in, 16)
            sp.dma_start(wo[:, :, :], wo_dram.rearrange("(c p) n -> p c n", p=P)).then_inc(const_in, 16)
            with sp.Fori(0, TILES) as i:
                for b in range(NB):
                    sp.wait_ge(h1_stored[b], 16 * (i + 1))
                    sp.sem_inc(sp_gate, 1)
                    sp.wait_ge(s[b]["h1_ready"], now(i))
                    sp.sem_inc(sp_gate, 1)
                    sp.dma_start(h1_dram[b, bass.ds(i * P, P), :], h1[b][:, :]).then_inc(h1_stored[b], 16)
                    sp.wait_ge(xn_stored[b], 16 * (i + 1))
                    sp.sem_inc(sp_gate, 1)
                    sp.wait_ge(s[b]["xn_ready"], now(i))
                    sp.sem_inc(sp_gate, 1)
                    sp.dma_start(tower_in[b, bass.ds(i * P, P), :], xn[b][:, :]).then_inc(xn_stored[b], 16)
            for b in range(NB):
                sp.wait_ge(h1_stored[b], 16 * (TILES + 1))
                sp.wait_ge(xn_stored[b], 16 * (TILES + 1))

        @block.scalar
        def _(act):
            with act.Fori(0, TILES) as i:
                for b in range(NB):
                    act.wait_ge(s[b]["t_full"], now(i - 1))
                    act.sem_inc(act_gate, 1)
                    nc.scalar.copy(o[b][:, :], o_all[:, bass.ds(b * TILES + i, 1), :].rearrange("p a d -> p (a d)"))\
                        .then_inc(s[b]["o_copied"], 1)
                for b in range(NB):
                    act.wait_ge(s[b]["t_full"], now(i))
                    nc.scalar.copy(oT[b][:, :, :].rearrange("p c t -> p (c t)"), t_bank[b][:, 0:D])\
                        .then_inc(s[b]["t_drained"], 1)

        @block.tensor
        def _(pe):
            pe.wait_ge(const_in, 32)
            with pe.Fori(0, TILES) as i:
                for b in range(NB):
                    pe.wait_ge(s[b]["o_copied"], now(i))
                    for c in range(KC):
                        last = nc.tensor.transpose(t_bank[b][:, c * P:(c + 1) * P], o[b][:, c * P:(c + 1) * P],
                                                   ident[:, :])
                    last.then_inc(s[b]["t_full"], 1)
                for b in range(NB):
                    pe.wait_ge(s[b]["t_drained"], now(i))
                    pe.wait_ge(s[b]["h1_ready"], now(i - 1))
                    for c in range(KC):
                        last = nc.tensor.matmul(w_bank[b][:, 0:D], oT[b][:, c, :], wo[:, c, :], start=c == 0,
                                                stop=c == KC - 1)
                    last.then_inc(s[b]["w_full"], 1)

        @block.vector
        def _(dve):
            nc.vector.memset(minus_half[:, :], -0.5).then_inc(root_ready, 1)
            with dve.Fori(0, TILES) as i:
                for b in range(NB):
                    dve.wait_ge(h1_stored[b], 16 * (i + 1))
                    dve.wait_ge(s[b]["xn_ready"], now(i - 1))
                    dve.wait_ge(s[b]["w_full"], now(i))
                    dve.sem_inc(dve_gate, 1)
                    nc.vector.tensor_tensor(h1[b][:, :], w_bank[b][:, 0:D],
                                            emb[:, bass.ds(b * TILES + i, 1), :].rearrange("p a d -> p (a d)"),
                                            ALU.add).then_inc(s[b]["h1_ready"], 1)
                for b in range(NB):
                    dve.wait_ge(s[b]["h1_ready"], now(i))
                    dve.sem_inc(dve_gate, 1)
                    nc.vector.bn_stats(stats[b][:, :], h1[b][:, :]).then_inc(s[b]["stats_ready"], 1)
                for b in range(NB):
                    dve.wait_ge(s[b]["stats_ready"], now(i))
                    dve.sem_inc(dve_gate, 1)
                    nc.vector.bn_aggr(mv[b][:, :], stats[b][:, :]).then_inc(s[b]["mv_ready"], 1)
                for b in range(NB):
                    dve.wait_ge(s[b]["mv_ready"], now(i))
                    nc.vector.tensor_scalar(ve[b][:, :], mv[b][:, 1:2], 1e-5, None, ALU.add)\
                        .then_inc(s[b]["ve_ready"], 1)
                for b in range(NB):
                    dve.wait_ge(s[b]["rstd_ready"], now(i))
                    dve.wait_ge(xn_stored[b], 16 * (i + 1))
                    nc.vector.tensor_scalar(xn[b][:, :], h1[b][:, :], mv[b][:, 0:1], rstd[b][:, :], ALU.subtract,
                                            ALU.mult).then_inc(s[b]["xn_ready"], 1)

        @block.gpsimd
        def _(pool):
            pool.wait_ge(root_ready, 1)
            with pool.Fori(0, TILES) as i:
                for b in range(NB):
                    pool.wait_ge(s[b]["ve_ready"], now(i))
                    nc.gpsimd.tensor_tensor(rstd[b][:, :], ve[b][:, :], minus_half[:, :], ALU.pow)\
                        .then_inc(s[b]["rstd_ready"], 1)


def mla_stage(nc, ids, embedding, ident, rope, causal, w_x, g_kv, w_kvdec, w_q, wo, h1_dram, tower_in):
    PAIRS, T = 8, h1_dram.shape[1]
    TILES = T // P
    with ExitStack() as ctx:
        emb = ctx.enter_context(nc.sbuf_tensor("emb_rows", [P, 2 * TILES, 256], F32))
        with ExitStack() as inner:
            qT_all = inner.enter_context(nc.sbuf_tensor("qT_all", [P, 2 * PAIRS, T], F32))
            kT_all = inner.enter_context(nc.sbuf_tensor("kT_all", [P, 2 * PAIRS, T], F32))
            v_all = inner.enter_context(nc.sbuf_tensor("v_all", [P, 2 * PAIRS, TILES, 34], F32))
            mla_project(nc, ids, embedding, ident, rope, w_x, g_kv, w_kvdec, w_q, emb, qT_all, kT_all, v_all)
            o_all = inner.enter_context(nc.sbuf_tensor("o_all", [P, 2 * TILES, 256], F32))
            mla_attend(nc, ident, causal, qT_all, kT_all, v_all, o_all)
            mla_output(nc, ident, o_all, emb, wo, h1_dram, tower_in)


def local_tower(nc, ident_dram, trig_dram, band_dram, shift_dram, h_dram, scale_dram, wqkv_dram, wo_dram,
                lng_dram, lnb_dram, w1_dram, b1_dram, w2_dram, b2_dram):
    LAYERS, D, QKV = wqkv_dram.shape
    F2 = w1_dram.shape[2]
    F = F2 // 2
    HALF = F // 2
    HD, WIN = 64, 64
    INNER = QKV // 3
    HEADS = INNER // HD
    PAIRS = HEADS // 2
    KC = D // P
    NB, ROWS = h_dram.shape[1], h_dram.shape[2]
    TILES = (ROWS - 1) // P
    ITERS = LAYERS * TILES
    TILE_BITS = TILES.bit_length() - 1
    assert TILES == 1 << TILE_BITS and NB == 2
    KEYS = WIN + P
    OWN, BEFORE = (0, P + 2 * WIN), P
    FC = (F + P - 1) // P
    FTAIL = F - (FC - 1) * P
    OC = INNER // P
    h_rows = h_dram.rearrange("l b t d -> (l b t) d")

    def within(value, most):
        if isinstance(value, int):
            return value
        return nc.s_assert_within(value, 0, most,
                                  skip_runtime_bounds_check_because="layer and tile come from one count")

    with ExitStack() as ctx:
        ctx.enter_context(nc.cleanup_on_exit())
        def sb(name, shape):
            return ctx.enter_context(nc.sbuf_tensor("lt_" + name, shape, F32))

        def pb(name):
            return ctx.enter_context(nc.psum_tensor("lt_" + name, [P, 512], F32))

        def sem(name):
            return nc.alloc_semaphore("lt_" + name)

        ident = sb("ident", [P, P])
        shift = sb("shift", [P, 2, P])
        wqkv = sb("wqkv", [P, 2 * KC * QKV])
        wo = sb("wo", [P, OC, D])
        w1 = sb("w1", [P, KC, F2])
        w2 = sb("w2", [P, FC, D])
        b1 = sb("b1", [P, F2])
        b2 = sb("b2", [P, D])
        lng = sb("lng", [P, KC])
        lnb = sb("lnb", [P, KC])
        scales = sb("scales", [P, LAYERS, 2, HD])
        trig = sb("trig", [P, 2, 2, HD])
        rot_c = sb("rot_c", [P, 2, HD])
        rot_s = sb("rot_s", [P, 2, HD])
        band = sb("band", [P, 2 * KEYS + 1])
        minus_half = sb("minus_half", [P, HEADS])
        x = [sb(f"x{b}", [P, D]) for b in range(NB)]
        xs = [sb(f"xs{b}", [P, D]) for b in range(NB)]
        xsT = [sb(f"xsT{b}", [P, KC, P]) for b in range(NB)]
        raw = [sb(f"raw{b}", [P, 2, HEADS, HD]) for b in range(NB)]
        qT = [sb(f"qT{b}", [P, PAIRS, P]) for b in range(NB)]
        kT = [sb(f"kT{b}", [P, PAIRS, 2 * KEYS]) for b in range(NB)]
        v = [sb(f"v{b}", [P, HEADS, HD + 1]) for b in range(NB)]
        v_prev = [sb(f"v_prev{b}", [P, HEADS, HD + 1]) for b in range(NB)]
        x1 = [sb(f"x1{b}", [P, D]) for b in range(NB)]
        x1_prev = [sb(f"x1_prev{b}", [P, P]) for b in range(NB)]
        out_tile = [sb(f"out_tile{b}", [P, D]) for b in range(NB)]
        turn_c = sb("turn_c", [P, 2, HEADS, HD])
        turn_s = sb("turn_s", [P, 2, HEADS, HD])
        ss = sb("ss", [P, 2, HEADS])
        rn = sb("rn", [P, 2, HEADS])
        sm = sb("sm", [P, 4, 2 * KEYS])
        minus_max = sb("minus_max", [P, 4, 2])
        pT = sb("pT", [P, 4, P])
        pT_prev = sb("pT_prev", [P, 2, P])
        rec = sb("rec", [P, 4])
        o = sb("o", [P, HEADS, HD])
        oT = sb("oT", [P, OC, P])
        stats = sb("stats", [P, 2, 6])
        mv = sb("mv", [P, 2])
        ve = sb("ve", [P, 1])
        rstd = sb("rstd", [P, 1])
        yn = sb("yn", [P, D])
        yT = sb("yT", [P, KC, P])
        gate = sb("gate", [P, F])
        ff = sb("ff", [P, FC * P])
        fT = sb("fT", [P, FC, P])

        a_bank = [pb("a0"), pb("a1")]
        s_bank = [pb("s0"), pb("s1")]
        p_bank = [pb("p0"), pb("p1")]
        o_bank = [pb("o0"), pb("o1")]

        a_full, a_drained = [sem("a0_full"), sem("a1_full")], [sem("a0_drained"), sem("a1_drained")]
        s_full, s_drained = [sem("s0_full"), sem("s1_full")], [sem("s0_drained"), sem("s1_drained")]
        p_full, p_drained = [sem("p0_full"), sem("p1_full")], [sem("p0_drained"), sem("p1_drained")]
        o_full, o_drained = [sem("o0_full"), sem("o1_full")], [sem("o0_drained"), sem("o1_drained")]
        const_in, consts_set = sem("const_in"), sem("consts_set")
        wqkv_in, wo_in, wff_in = sem("wqkv_in"), sem("wo_in"), sem("wff_in")
        xs_in = [sem(f"xs_in{b}") for b in range(NB)]
        x_in = [sem(f"x_in{b}") for b in range(NB)]
        trig_in, band_in = sem("trig_in"), sem("band_in")
        h_stored = [sem(f"h_stored{b}") for b in range(NB)]
        rot_ready = sem("rot_ready")
        ss_ready, rn_ready, turn_s_ready, turned = sem("ss_ready"), sem("rn_ready"), sem("turn_s_ready"), sem("turned")
        mx_ready, probs_ready = sem("mx_ready"), sem("probs_ready")
        ve_ready, rstd_ready = sem("ve_ready"), sem("rstd_ready")
        x1_kept, gelu_ready, ff_ready = sem("x1_kept"), sem("gelu_ready"), sem("ff_ready")
        squares_summed, c_turned, added = sem("squares_summed"), sem("c_turned"), sem("added")
        v_moved, k_moved = sem("v_moved"), sem("k_moved")
        rec_ready, stats_ready, mv_ready = sem("rec_ready"), sem("stats_ready"), sem("mv_ready")
        act_gate, dve_gate, pool_gate, sp_gate = sem("act_gate"), sem("dve_gate"), sem("pool_gate"), sem("sp_gate")

        COUNTS = [(s_full, 4), (s_drained, 4), (p_full, 7), (p_drained, 7), (o_full, 5), (o_drained, 5)]
        ONES = [(ss_ready, 2), (rn_ready, 2), (turn_s_ready, 2), (turned, 2), (mx_ready, PAIRS),
                (probs_ready, PAIRS), (ve_ready, 1), (rstd_ready, 1), (x1_kept, 1), (gelu_ready, 2),
                (ff_ready, 2), (squares_summed, 2), (c_turned, 2), (added, 2), (rec_ready, 4), (stats_ready, 2),
                (mv_ready, 1), (v_moved, 1), (k_moved, 1)]
        A_USES = 11
        XT, PROJ, TR = 0, (1, 2, 3, 4, 5, 8), (6, 7, 9, 10)
        PROBS_USE, OT_USE, SHIFT_USE, HT_USE = ((0, 1, 2, 4), (0, 1, 2, 3)), (3, 4), 5, 6
        WO_USE = 2

        def nth(per, k, pos=0):
            return per * (k + 2) + pos + 1

        def a_use(u, b, pos):
            n = A_USES * b + pos
            return n % 2, A_USES * (u + 1) + n // 2 + 1

        block = ctx.enter_context(nc.Block())

        @block.sync
        def _(sp):
            for banks, n in COUNTS:
                for s in banks:
                    sp.sem_inc(s, 2 * n)
            for s in a_full + a_drained:
                sp.sem_inc(s, A_USES)
            for s, n in ONES:
                sp.sem_inc(s, 2 * n)
            sp.sem_inc(rot_ready, 1)
            for s in h_stored:
                sp.sem_inc(s, 16)
            sp.dma_start(ident[:, :], ident_dram).then_inc(const_in, 16)
            sp.dma_start(shift[:, :, :], shift_dram.rearrange("a p q -> p a q")).then_inc(const_in, 16)
            sp.dma_start(scales[:, :, :, :].rearrange("p l a d -> p (l a d)"),
                         scale_dram.rearrange("l a d -> (l a d)").partition_broadcast(P)).then_inc(const_in, 16)

            def load_wqkv(l, parity):
                sp.dma_start(wqkv[:, bass.ds(parity * (KC * QKV), KC * QKV)].rearrange("p (c n) -> p c n", c=KC),
                             wqkv_dram[bass.ds(l, 1), :, :].rearrange("l (c p) n -> p (l c) n", p=P)).then_inc(wqkv_in, 16)

            def row(u, b, first):
                at = ((u >> TILE_BITS) * NB + b) * ROWS + (u & (TILES - 1)) * P + first
                return within(at, (LAYERS + 1) * NB * ROWS - P)

            def load_xs(u, b):
                sp.dma_start(xs[b][:, 0:P], h_rows[bass.ds(row(u, b, 1), P), 0:P]).then_inc(xs_in[b], 16)
                sp.dma_start(xs[b][:, P:D], h_rows[bass.ds(row(u, b, 0), P), P:D]).then_inc(xs_in[b], 16)

            def load_x(u, b):
                sp.dma_start(x[b][:, :], h_rows[bass.ds(row(u, b, 1), P), :]).then_inc(x_in[b], 16)

            def load_trig(u):
                sp.dma_start(trig[:, :, :, :].rearrange("p a c d -> p (a c d)"),
                             trig_dram[bass.ds(u & (TILES - 1), 1), :, :].rearrange("t p n -> p (t n)")).then_inc(trig_in, 16)

            def load_band(u):
                sp.dma_start(band[:, :], band_dram[bass.ds(u & (TILES - 1), 1), :, :].rearrange("t p n -> p (t n)"))\
                    .then_inc(band_in, 16)

            load_wqkv(0, 0)
            for b in range(NB):
                load_xs(0, b)
            load_trig(0)
            load_band(0)
            for b in range(NB):
                load_x(0, b)

            def layer(l, last):
                sp.dma_start(wo[:, :, :], wo_dram[bass.ds(l, 1), :, :].rearrange("l (c p) n -> p (l c) n", p=P))\
                    .then_inc(wo_in, 16)
                sp.dma_start(w1[:, :, :], w1_dram[bass.ds(l, 1), :, :].rearrange("l (c p) n -> p (l c) n", p=P))\
                    .then_inc(wff_in, 16)
                w2_l = w2_dram[bass.ds(l, 1), :, :]
                sp.wait_ge(consts_set, 1)
                sp.dma_start(w2[:, 0:FC - 1, :], w2_l[:, 0:(FC - 1) * P, :].rearrange("l (c p) n -> p (l c) n", p=P))\
                    .then_inc(wff_in, 16)
                sp.dma_start(w2[0:FTAIL, FC - 1, :], w2_l[:, (FC - 1) * P:F, :].rearrange("l p n -> p (l n)"))\
                    .then_inc(wff_in, 16)
                sp.dma_start(b1[:, :], b1_dram[bass.ds(l, 1), :].rearrange("l n -> (l n)").partition_broadcast(P))\
                    .then_inc(wff_in, 16)
                sp.dma_start(b2[:, :], b2_dram[bass.ds(l, 1), :].rearrange("l n -> (l n)").partition_broadcast(P))\
                    .then_inc(wff_in, 16)
                with nc.allow_non_contiguous_dma(reason="256 gains and biases, one to a partition"):
                    sp.dma_start(lng[:, :], lng_dram[bass.ds(l, 1), :].rearrange("l (c p) -> p (l c)", p=P))\
                        .then_inc(wff_in, 16)
                    sp.dma_start(lnb[:, :], lnb_dram[bass.ds(l, 1), :].rearrange("l (c p) -> p (l c)", p=P))\
                        .then_inc(wff_in, 16)
                if not last:
                    sp.wait_ge(wqkv_in, 16 * (l + 1))
                    sp.sem_inc(sp_gate, 1)
                    load_wqkv(l + 1, (l + 1) & 1)
                with sp.Fori(0, TILES) as p:
                    u = sp.snap(l * TILES + p)
                    for b in range(NB):
                        j, n = a_use(u, b, XT)
                        sp.wait_ge(a_drained[j], n)
                        load_xs(u + 1, b)
                    sp.wait_ge(rot_ready, u + 2)
                    load_trig(u + 1)
                    for b in range(NB):
                        if b == 1:
                            sp.wait_ge(x1_kept, nth(1, 2 * u + 1))
                            load_band(u + 1)
                        sp.wait_ge(o_drained[0], nth(5, 2 * u + b, WO_USE))
                        load_x(u + 1, b)
                        sp.wait_ge(o_drained[1], nth(5, 2 * u + b, 4))
                        sp.dma_start(h_rows[bass.ds(row(u + TILES, b, 1), P), :], out_tile[b][:, :]).then_inc(h_stored[b], 16)
                        sp.wait_ge(h_stored[b], 16 * (u + 2))
                        sp.sem_inc(sp_gate, 1)

            with sp.Fori(0, LAYERS - 1) as l:
                layer(l, False)
            layer(LAYERS - 1, True)
            for b in range(NB):
                sp.wait_ge(xs_in[b], 32 * (ITERS + 1))
                sp.wait_ge(x_in[b], 16 * (ITERS + 1))
            sp.wait_ge(trig_in, 16 * (ITERS + 1))
            sp.wait_ge(band_in, 16 * (ITERS + 1))

        @block.tensor
        def _(pe):
            def mm(out, lhsT, rhs, start, stop):
                return nc.tensor.matmul(out, lhsT, rhs, start=start, stop=stop)

            def open_a(u, b, pos):
                j, n = a_use(u, b, pos)
                pe.wait_ge(a_drained[j], n - 1)
                return a_bank[j], a_full[j]

            def input_T(u, b):
                bank, full = open_a(u, b, XT)
                pe.wait_ge(xs_in[b], 32 * (u + 1))
                for c in range(KC):
                    last = nc.tensor.transpose(bank[:, c * P:(c + 1) * P], xs[b][:, c * P:(c + 1) * P], ident[:, :])
                last.then_inc(full, 1)

            def project(u, b, g, chunks=range(KC)):
                j, n = a_use(u, b, PROJ[g])
                if 0 in chunks:
                    open_a(u, b, PROJ[g])
                if g == 0:
                    jx, nx = a_use(u, b, XT)
                    pe.wait_ge(a_drained[jx], nx)
                    pe.wait_ge(wqkv_in, 16 * ((u >> TILE_BITS) + 1))
                for c in chunks:
                    at = ((u >> TILE_BITS) & 1) * (KC * QKV) + c * QKV + g * 512
                    last = mm(a_bank[j][:, :], xsT[b][:, c, :], wqkv[:, bass.ds(at, 512)], c == 0, c == KC - 1)
                if KC - 1 in chunks:
                    last.then_inc(a_full[j], 1)

            def turn_T(u, b, g):
                bank, full = open_a(u, b, TR[g])
                if g % 2 == 0:
                    pe.wait_ge(turned, nth(2, 2 * u + b, g // 2))
                for i in range(4):
                    pair = 4 * (g % 2) + i
                    last = nc.tensor.transpose(bank[:, i * P:(i + 1) * P],
                                               turn_c[:, g // 2, 2 * pair:2 * pair + 2, :].rearrange("p a d -> p (a d)"),
                                               ident[:, :])
                last.then_inc(full, 1)

            def scores(u, b, hp):
                k = 2 * u + b
                if hp == 0:
                    j, n = a_use(u, b, TR[3])
                    pe.wait_ge(a_drained[j], n)
                    j, n = a_use(u, b, TR[2])
                    pe.wait_ge(a_drained[j], n)
                pe.wait_ge(s_drained[hp % 2], nth(4, k, hp // 2) - 1)
                mm(s_bank[hp % 2][:, 0:2 * KEYS], qT[b][:, hp, :], kT[b][:, hp, :],
                   True, True).then_inc(s_full[hp % 2], 1)

            def probs_T(u, b, g):
                k = 2 * u + b
                pe.wait_ge(probs_ready, nth(PAIRS, k, 2 * g + 1))
                pe.wait_ge(p_drained[0], nth(7, k, PROBS_USE[0][g]) - 1)
                for i in range(4):
                    last = nc.tensor.transpose(p_bank[0][:, i * P:(i + 1) * P],
                                               sm[:, (2 * g + i // 2) % 4, OWN[i % 2]:OWN[i % 2] + P], ident[:, :])
                last.then_inc(p_full[0], 1)
                pe.wait_ge(p_drained[1], nth(7, k, g) - 1)
                for i in range(2):
                    last = nc.tensor.transpose(p_bank[1][:, i * P:(i + 1) * P], sm[:, (2 * g + i) % 4, BEFORE:BEFORE + P],
                                               ident[:, :])
                last.then_inc(p_full[1], 1)

            def weigh(u, b, g):
                k = 2 * u + b
                pe.wait_ge(p_drained[0], nth(7, k, PROBS_USE[0][g]))
                pe.wait_ge(p_drained[1], nth(7, k, g))
                if g == 0:
                    for pos in PROJ[4:6]:
                        j, n = a_use(u, b, pos)
                        pe.wait_ge(a_drained[j], n)
                pe.wait_ge(o_drained[g % 2], nth(5, k, g // 2) - 1)
                for i in range(2):
                    hp = 2 * g + i
                    out = o_bank[g % 2][:, i * 2 * (HD + 1):(i + 1) * 2 * (HD + 1)]
                    mm(out, pT_prev[:, i, :], v_prev[b][:, 2 * hp:2 * hp + 2, :].rearrange("p a d -> p (a d)"),
                       True, False)
                    for e in range(2):
                        last = mm(out[:, e * (HD + 1):(e + 1) * (HD + 1)], pT[:, 2 * i + e, :],
                                  v[b][:, 2 * hp + e, :], False, e == 1)
                last.then_inc(o_full[g % 2], 1)

            def out_T(u, b, j):
                k = 2 * u + b
                pe.wait_ge(o_drained[0], nth(5, k, j))
                pe.wait_ge(o_drained[1], nth(5, k, j))
                pe.wait_ge(p_drained[j], nth(7, k, OT_USE[j]) - 1)
                for i in range(4):
                    c = 4 * j + i
                    last = nc.tensor.transpose(p_bank[j][:, i * P:(i + 1) * P],
                                               o[:, 2 * c:2 * c + 2, :].rearrange("p a d -> p (a d)"), ident[:, :])
                last.then_inc(p_full[j], 1)

            def out_project(u, b, j):
                k = 2 * u + b
                if j == 0:
                    pe.wait_ge(wo_in, 16 * ((u >> TILE_BITS) + 1))
                    pe.wait_ge(o_drained[0], nth(5, k, WO_USE) - 1)
                pe.wait_ge(p_drained[j], nth(7, k, OT_USE[j]))
                for c in range(4 * j, 4 * j + 4):
                    last = mm(o_bank[0][:, 0:D], oT[:, c, :], wo[:, c, :], c == 0, c == OC - 1)
                if j == 1:
                    last.then_inc(o_full[0], 1)

            def shift_x1(u, b):
                k = 2 * u + b
                pe.wait_ge(o_drained[0], nth(5, k, WO_USE))
                pe.wait_ge(x1_kept, nth(1, k - 2))
                pe.wait_ge(p_drained[0], nth(7, k, SHIFT_USE) - 1)
                mm(p_bank[0][:, 0:P], shift[:, 0, :], x1[b][:, P:D], True, False)
                mm(p_bank[0][:, 0:P], shift[:, 1, :], x1_prev[b][:, :], False, True).then_inc(p_full[0], 1)

            def norm_T(u, b):
                k = 2 * u + b
                pe.wait_ge(p_drained[0], nth(7, k, SHIFT_USE))
                pe.wait_ge(p_drained[1], nth(7, k, 5) - 1)
                for c in range(KC):
                    last = nc.tensor.transpose(p_bank[1][:, c * P:(c + 1) * P], yn[:, c * P:(c + 1) * P], ident[:, :])
                last.then_inc(p_full[1], 1)

            def expand(u, b, g):
                k = 2 * u + b
                if g == 0:
                    pe.wait_ge(p_drained[1], nth(7, k, 5))
                    pe.wait_ge(wff_in, 16 * 7 * ((u >> TILE_BITS) + 1))
                j = 1 - g % 2
                pos = (2, 3, 3, 4)[g]
                pe.wait_ge(o_drained[j], nth(5, k, pos) - 1)
                first = (F, F + HALF, 0, HALF)[g]
                for c in range(KC):
                    last = mm(o_bank[j][:, 0:HALF], yT[:, c, :], w1[:, c, first:first + HALF], c == 0, c == KC - 1)
                last.then_inc(o_full[j], 1)

            def ff_T(u, b):
                k = 2 * u + b
                pe.wait_ge(ff_ready, nth(2, k, 1))
                for j in range(2):
                    n = 4 if j == 0 else FC - 4
                    pe.wait_ge(p_drained[j], nth(7, k, HT_USE) - 1)
                    for i in range(n):
                        c = 4 * j + i
                        last = nc.tensor.transpose(p_bank[j][:, i * P:(i + 1) * P], ff[:, c * P:(c + 1) * P], ident[:, :])
                    last.then_inc(p_full[j], 1)

            def contract(u, b):
                k = 2 * u + b
                pe.wait_ge(o_drained[1], nth(5, k, 4) - 1)
                for c in range(FC):
                    if c % 4 == 0:
                        pe.wait_ge(p_drained[c // 4], nth(7, k, HT_USE))
                    last = mm(o_bank[1][:, 0:D], fT[:, c, :], w2[:, c, :], c == 0, c == FC - 1)
                last.then_inc(o_full[1], 1)

            def unit(u, b, nxt):
                def A(f, *a):
                    if nxt is not None:
                        f(*nxt, *a)
                A(input_T)
                scores(u, b, 2)
                scores(u, b, 3)
                A(project, 0)
                probs_T(u, b, 0)
                scores(u, b, 4)
                scores(u, b, 5)
                A(project, 1)
                weigh(u, b, 0)
                probs_T(u, b, 1)
                scores(u, b, 6)
                scores(u, b, 7)
                A(project, 2)
                weigh(u, b, 1)
                probs_T(u, b, 2)
                A(project, 3)
                out_T(u, b, 0)
                weigh(u, b, 2)
                probs_T(u, b, 3)
                A(project, 4)
                weigh(u, b, 3)
                out_project(u, b, 0)
                out_T(u, b, 1)
                A(turn_T, 0)
                A(turn_T, 1)
                out_project(u, b, 1)
                A(project, 5, range(0, 1))
                shift_x1(u, b)
                A(project, 5, range(1, KC))
                A(turn_T, 2)
                A(turn_T, 3)
                norm_T(u, b)
                for g in range(4):
                    expand(u, b, g)
                A(scores, 0)
                ff_T(u, b)
                A(scores, 1)
                contract(u, b)

            def first():
                input_T(0, 0)
                for g in range(5):
                    project(0, 0, g)
                turn_T(0, 0, 0)
                turn_T(0, 0, 1)
                project(0, 0, 5)
                turn_T(0, 0, 2)
                turn_T(0, 0, 3)
                scores(0, 0, 0)
                scores(0, 0, 1)

            pe.wait_ge(const_in, 48)
            pe.wait_ge(consts_set, 1)
            first()
            with pe.Fori(0, ITERS - 1) as u:
                unit(u, 0, (u, 1))
                unit(u, 1, (u + 1, 0))
            unit(ITERS - 1, 0, (ITERS - 1, 1))
            unit(ITERS - 1, 1, None)


        @block.scalar
        def _(act):
            def full_a(u, b, pos):
                j, n = a_use(u, b, pos)
                act.wait_ge(a_full[j], n)
                return a_bank[j], a_drained[j]

            def input_T(u, b):
                bank, drained = full_a(u, b, XT)
                nc.scalar.activation(xsT[b][:, :, :].rearrange("p c t -> p (c t)"), bank[:, 0:D], ACT.Copy)\
                    .then_inc(drained, 1)

            def keep_qk(u, b, g):
                k = 2 * u + b
                half, heads = g // 2, slice(8 * (g % 2), 8 * (g % 2) + 8)
                bank, drained = full_a(u, b, PROJ[g])
                act.wait_ge(turned, nth(2, k - 1, half))
                nc.scalar.activation(raw[b][:, half, heads, :].rearrange("p h d -> p (h d)"), bank[:, :], ACT.Copy)
                nc.scalar.activation(turn_s[:, half, heads, :].rearrange("p h d -> p (h d)"), bank[:, :], ACT.Square)\
                    .then_inc(drained, 1)

            def keep_v(u, b, g):
                k = 2 * u + b
                if g == 4:
                    act.wait_ge(o_full[1], nth(5, k - 2, 1))
                    act.sem_inc(act_gate, 1)
                    for e in range(2):
                        last = nc.scalar.activation(v_prev[b][WIN * e:WIN * e + WIN, e::2, :], v[b][WIN:P, e::2, :],
                                                    ACT.Copy)
                    last.then_inc(v_moved, 1)
                    act.wait_ge(v_moved, nth(1, k))
                bank, drained = full_a(u, b, PROJ[g])
                nc.scalar.activation(v[b][:, 8 * (g - 4):8 * (g - 4) + 8, 0:HD],
                                     bank[:, :].rearrange("p (h d) -> p h d", d=HD), ACT.Copy).then_inc(drained, 1)

            def keep_turned(u, b, g):
                bank, drained = full_a(u, b, TR[g])
                pairs = slice(4 * (g % 2), 4 * (g % 2) + 4)
                src = bank[:, :].rearrange("p (i t) -> p i t", t=P)
                if g < 2:
                    nc.scalar.activation(qT[b][:, pairs, :], src, ACT.Copy).then_inc(drained, 1)
                    return
                act.wait_ge(k_moved, nth(1, 2 * u + b))
                for e in range(2):
                    last = nc.scalar.activation(kT[b][HD * e:HD * e + HD, pairs, OWN[e]:OWN[e] + P],
                                                src[HD * e:HD * e + HD, :, :], ACT.Copy)
                last.then_inc(drained, 1)

            def exp(u, b, hp):
                act.wait_ge(mx_ready, nth(PAIRS, 2 * u + b, hp))
                for e in range(2):
                    tile = sm[:, hp % 4, e * KEYS:(e + 1) * KEYS]
                    last = nc.scalar.activation(tile, tile, ACT.Exp, bias=minus_max[:, hp % 4, e:e + 1])
                last.then_inc(probs_ready, 1)

            def keep_probs(u, b, g):
                act.wait_ge(p_full[0], nth(7, 2 * u + b, PROBS_USE[0][g]))
                nc.scalar.activation(pT[:, :, :].rearrange("p i t -> p (i t)"), p_bank[0][:, :], ACT.Copy)\
                    .then_inc(p_drained[0], 1)

            def keep_oT(u, b, j):
                act.wait_ge(p_full[j], nth(7, 2 * u + b, OT_USE[j]))
                nc.scalar.activation(oT[:, 4 * j:4 * j + 4, :].rearrange("p i t -> p (i t)"), p_bank[j][:, :],
                                     ACT.Copy).then_inc(p_drained[j], 1)

            def keep_yT(u, b):
                act.wait_ge(wff_in, 16 * 7 * ((u >> TILE_BITS) + 1))
                act.wait_ge(p_full[1], nth(7, 2 * u + b, 5))
                for c in range(KC):
                    last = nc.scalar.activation(yT[:, c, :], p_bank[1][:, c * P:(c + 1) * P], ACT.Identity,
                                                bias=lnb[:, c:c + 1], scale=lng[:, c:c + 1])
                last.then_inc(p_drained[1], 1)

            def gelu(u, b, j):
                act.wait_ge(o_drained[1 - j], nth(5, 2 * u + b, 2 + j))
                part = gate[:, j * HALF:(j + 1) * HALF]
                nc.scalar.activation(part, part, ACT.Gelu).then_inc(gelu_ready, 1)

            def keep_fT(u, b):
                for j in range(2):
                    n = 4 if j == 0 else FC - 4
                    act.wait_ge(p_full[j], nth(7, 2 * u + b, HT_USE))
                    nc.scalar.activation(fT[:, 4 * j:4 * j + n, :].rearrange("p i t -> p (i t)"),
                                         p_bank[j][:, 0:n * P], ACT.Copy).then_inc(p_drained[j], 1)

            def unit(u, b, nxt):
                def A(f, *a):
                    if nxt is not None:
                        f(*nxt, *a)
                A(input_T)
                exp(u, b, 2)
                exp(u, b, 3)
                keep_probs(u, b, 0)
                A(keep_qk, 0)
                exp(u, b, 4)
                exp(u, b, 5)
                A(keep_qk, 1)
                keep_probs(u, b, 1)
                exp(u, b, 6)
                A(keep_qk, 2)
                exp(u, b, 7)
                keep_probs(u, b, 2)
                A(keep_qk, 3)
                keep_oT(u, b, 0)
                keep_probs(u, b, 3)
                A(keep_v, 4)
                keep_oT(u, b, 1)
                A(keep_turned, 0)
                A(keep_turned, 1)
                A(keep_v, 5)
                keep_yT(u, b)
                A(keep_turned, 2)
                gelu(u, b, 0)
                A(keep_turned, 3)
                gelu(u, b, 1)
                keep_fT(u, b)
                A(exp, 0)
                A(exp, 1)

            act.wait_ge(consts_set, 1)
            input_T(0, 0)
            for g in range(4):
                keep_qk(0, 0, g)
            keep_v(0, 0, 4)
            keep_turned(0, 0, 0)
            keep_turned(0, 0, 1)
            keep_v(0, 0, 5)
            keep_turned(0, 0, 2)
            keep_turned(0, 0, 3)
            exp(0, 0, 0)
            exp(0, 0, 1)
            with act.Fori(0, ITERS - 1) as u:
                unit(u, 0, (u, 1))
                unit(u, 1, (u + 1, 0))
            unit(ITERS - 1, 0, (ITERS - 1, 1))
            unit(ITERS - 1, 1, None)

        @block.vector
        def _(dve):
            def bounded_scores(u, b, hp):
                k = 2 * u + b
                tile = sm[:, hp % 4, :]
                if hp == 0:
                    dve.wait_ge(band_in, 16 * (u + 1))
                dve.wait_ge(p_full[1], nth(7, k, (hp - 4) // 2) if hp >= 4 else nth(7, k - 1, (hp + 4) // 2))
                dve.wait_ge(s_full[hp % 2], nth(4, k, hp // 2))
                nc.vector.tensor_tensor(tile, s_bank[hp % 2][:, 0:2 * KEYS], band[:, 0:2 * KEYS], ALU.add)\
                    .then_inc(s_drained[hp % 2], 1)
                dve.wait_ge(s_drained[hp % 2], nth(4, k, hp // 2))
                nc.vector.reduce_max(minus_max[:, hp % 4, :], tile.rearrange("p (a n) -> p a n", a=2), AX, negate=True)\
                    .then_inc(mx_ready, 1)

            def start_turn(u, b, half):
                k = 2 * u + b
                for g in (2 * half, 2 * half + 1):
                    j, n = a_use(u, b, PROJ[g])
                    dve.wait_ge(a_drained[j], n)
                dve.wait_ge(rn_ready, nth(2, k - 1, half))
                nc.vector.reduce_sum(ss[:, half, :], turn_s[:, half, :, :], AX).then_inc(squares_summed, 1)
                dve.wait_ge(squares_summed, nth(2, k, half))
                nc.vector.tensor_scalar(ss[:, half, :], ss[:, half, :], 1e-24, None, ALU.max).then_inc(ss_ready, 1)
                dve.wait_ge(rot_ready, u + 2)
                for g in TR[2 * half:2 * half + 2]:
                    j, n = a_use(u - 1 + b, 1 - b, g)
                    dve.wait_ge(a_full[j], n)
                nc.vector.tensor_tensor(turn_c[:, half, :, :], raw[b][:, half, :, :],
                                        rot_c[:, half, :].unsqueeze(1).to_broadcast([P, HEADS, HD]), ALU.mult)\
                    .then_inc(c_turned, 1)

            def end_turn(u, b, half):
                k = 2 * u + b
                both = turn_c[:, half, :, :]
                dve.wait_ge(c_turned, nth(2, k, half))
                dve.wait_ge(turn_s_ready, nth(2, k, half))
                nc.vector.tensor_tensor(both, both, turn_s[:, half, :, :], ALU.add).then_inc(added, 1)
                dve.wait_ge(added, nth(2, k, half))
                dve.wait_ge(rn_ready, nth(2, k, half))
                nc.vector.tensor_tensor(both, both, rn[:, half, :].unsqueeze(2).to_broadcast([P, HEADS, HD]), ALU.mult)\
                    .then_inc(turned, 1)

            def keep_probs(u, b, g):
                dve.wait_ge(p_full[1], nth(7, 2 * u + b, g))
                nc.vector.tensor_copy(pT_prev[:, :, :].rearrange("p i t -> p (i t)"), p_bank[1][:, 0:2 * P])\
                    .then_inc(p_drained[1], 1)

            def keep_o(u, b, g):
                k = 2 * u + b
                weighed = o_bank[g % 2][:, 0:4 * (HD + 1)].rearrange("p (h d) -> p h d", d=HD + 1)
                dve.wait_ge(o_full[g % 2], nth(5, k, g // 2))
                nc.vector.reciprocal(rec[:, :].unsqueeze(2), weighed[:, :, HD:HD + 1]).then_inc(rec_ready, 1)
                if g == 0:
                    dve.wait_ge(p_full[1], nth(7, k - 1, 4))
                dve.wait_ge(rec_ready, nth(4, k, g))
                nc.vector.tensor_tensor(o[:, 4 * g:4 * g + 4, :], weighed[:, :, 0:HD],
                                        rec[:, :].unsqueeze(2).to_broadcast([P, 4, HD]), ALU.mult)\
                    .then_inc(o_drained[g % 2], 1)

            def add_residual(u, b):
                k = 2 * u + b
                dve.wait_ge(x_in[b], 16 * (u + 1))
                dve.wait_ge(x1_kept, nth(1, k - 1))
                dve.wait_ge(o_full[0], nth(5, k, WO_USE))
                nc.vector.tensor_tensor(x1[b][:, :], o_bank[0][:, 0:D], x[b][:, :], ALU.add).then_inc(o_drained[0], 1)

            def norm(u, b):
                k = 2 * u + b
                dve.wait_ge(o_drained[0], nth(5, k, WO_USE))
                nc.vector.bn_stats(stats[:, 0, :], x1[b][:, 0:P]).then_inc(stats_ready, 1)
                dve.wait_ge(p_full[0], nth(7, k, SHIFT_USE))
                nc.vector.bn_stats(stats[:, 1, :], p_bank[0][:, 0:P]).then_inc(stats_ready, 1)
                dve.wait_ge(stats_ready, nth(2, k, 1))
                dve.sem_inc(dve_gate, 1)
                nc.vector.bn_aggr(mv[:, :], stats[:, :, :].rearrange("p a s -> p (a s)")).then_inc(mv_ready, 1)
                dve.wait_ge(mv_ready, nth(1, k))
                nc.vector.tensor_scalar(ve[:, :], mv[:, 1:2], 1e-5, None, ALU.add).then_inc(ve_ready, 1)
                dve.wait_ge(p_full[1], nth(7, k - 1, 5))
                dve.wait_ge(rstd_ready, nth(1, k))
                nc.vector.tensor_scalar(yn[:, 0:P], x1[b][:, 0:P], mv[:, 0:1], rstd[:, :], ALU.subtract, ALU.mult)
                nc.vector.tensor_scalar(yn[:, P:D], p_bank[0][:, 0:P], mv[:, 0:1], rstd[:, :], ALU.subtract, ALU.mult)\
                    .then_inc(p_drained[0], 1)

            def keep_gate(u, b, j):
                k = 2 * u + b
                if j == 0:
                    dve.wait_ge(wff_in, 16 * 7 * ((u >> TILE_BITS) + 1))
                dve.wait_ge(o_full[1 - j], nth(5, k, 2 + j))
                nc.vector.tensor_tensor(gate[:, j * HALF:(j + 1) * HALF], o_bank[1 - j][:, 0:HALF],
                                        b1[:, F + j * HALF:F + (j + 1) * HALF], ALU.add).then_inc(o_drained[1 - j], 1)

            def keep_up(u, b, j):
                k = 2 * u + b
                if j == 0:
                    dve.wait_ge(p_full[1], nth(7, k - 1, HT_USE))
                dve.wait_ge(o_full[1 - j], nth(5, k, 3 + j))
                nc.vector.tensor_tensor(ff[:, j * HALF:(j + 1) * HALF], o_bank[1 - j][:, 0:HALF],
                                        b1[:, j * HALF:(j + 1) * HALF], ALU.add).then_inc(o_drained[1 - j], 1)

            def gated(u, b, j):
                k = 2 * u + b
                cols = slice(j * HALF, (j + 1) * HALF)
                dve.wait_ge(o_drained[1 - j], nth(5, k, 3 + j))
                dve.wait_ge(gelu_ready, nth(2, k, j))
                nc.vector.tensor_tensor(ff[:, cols], ff[:, cols], gate[:, cols], ALU.mult).then_inc(ff_ready, 1)

            def output(u, b):
                k = 2 * u + b
                dve.wait_ge(x1_kept, nth(1, k))
                dve.wait_ge(o_full[1], nth(5, k, 4))
                nc.vector.tensor_tensor(out_tile[b][:, :], o_bank[1][:, 0:D], out_tile[b][:, :], ALU.add)\
                    .then_inc(o_drained[1], 1)

            def unit(u, b, nxt):
                def A(f, *a):
                    if nxt is not None:
                        f(*nxt, *a)
                bounded_scores(u, b, 2)
                bounded_scores(u, b, 3)
                keep_probs(u, b, 0)
                bounded_scores(u, b, 4)
                bounded_scores(u, b, 5)
                keep_o(u, b, 0)
                keep_probs(u, b, 1)
                A(start_turn, 0)
                bounded_scores(u, b, 6)
                bounded_scores(u, b, 7)
                keep_o(u, b, 1)
                keep_probs(u, b, 2)
                A(start_turn, 1)
                keep_o(u, b, 2)
                keep_probs(u, b, 3)
                A(end_turn, 0)
                keep_o(u, b, 3)
                A(end_turn, 1)
                add_residual(u, b)
                norm(u, b)
                keep_gate(u, b, 0)
                keep_gate(u, b, 1)
                keep_up(u, b, 0)
                gated(u, b, 0)
                keep_up(u, b, 1)
                gated(u, b, 1)
                A(bounded_scores, 0)
                A(bounded_scores, 1)
                output(u, b)

            for b in range(NB):
                nc.vector.memset(v[b][:, :, :], 1.0)
                nc.vector.memset(v_prev[b][:, :, :], 0.0)
                nc.vector.memset(kT[b][:, :, :], 0.0)
                nc.vector.memset(x1_prev[b][:, :], 0.0)
            nc.vector.memset(minus_half[:, :], -0.5)
            nc.vector.memset(ff[:, :], 0.0)
            nc.vector.memset(w2[:, FC - 1, :], 0.0).then_inc(consts_set, 1)
            for half in range(2):
                start_turn(0, 0, half)
                end_turn(0, 0, half)
            bounded_scores(0, 0, 0)
            bounded_scores(0, 0, 1)
            with dve.Fori(0, ITERS - 1) as u:
                unit(u, 0, (u, 1))
                unit(u, 1, (u + 1, 0))
            unit(ITERS - 1, 0, (ITERS - 1, 1))
            unit(ITERS - 1, 1, None)

        @block.gpsimd
        def _(pool):
            def rotary(u, k_before):
                pool.wait_ge(trig_in, 16 * (u + 1))
                pool.wait_ge(turned, nth(2, k_before, 1))
                pool.sem_inc(pool_gate, 1)
                sc = scales[:, bass.ds(within(u >> TILE_BITS, LAYERS - 1), 1), :, :].rearrange("p l a d -> p (l a) d")
                pool_scales = sc
                nc.gpsimd.tensor_tensor(rot_c[:, :, :], trig[:, :, 0, :], pool_scales, ALU.mult)
                nc.gpsimd.tensor_tensor(rot_s[:, :, 0:HD // 2], trig[:, :, 1, 0:HD // 2], pool_scales[:, :, HD // 2:HD],
                                        ALU.mult)
                nc.gpsimd.tensor_tensor(rot_s[:, :, HD // 2:HD], trig[:, :, 1, HD // 2:HD], pool_scales[:, :, 0:HD // 2],
                                        ALU.mult).then_inc(rot_ready, 1)

            def move_window(u, b):
                pool.wait_ge(s_full[1], nth(4, 2 * u + b - 2, 3))
                pool.sem_inc(pool_gate, 1)
                chunks = kT[b][:, :, :].rearrange("p i (c w) -> p i c w", w=WIN)
                nc.gpsimd.tensor_copy(chunks[:, :, 2:4, :], chunks[:, :, 1:6:4, :]).then_inc(k_moved, 1)

            def turn(u, b, half):
                k = 2 * u + b
                H2 = HD // 2
                pool.wait_ge(ss_ready, nth(2, k, half))
                pool.wait_ge(turned, nth(2, k - 1, half))
                nc.gpsimd.tensor_tensor(rn[:, half, :], ss[:, half, :], minus_half[:, :], ALU.pow).then_inc(rn_ready, 1)
                pool.wait_ge(rot_ready, u + 2)
                for first, other in ((0, H2), (H2, 0)):
                    last = nc.gpsimd.tensor_tensor(
                        turn_s[:, half, :, first:first + H2], raw[b][:, half, :, other:other + H2],
                        rot_s[:, half, first:first + H2].unsqueeze(1).to_broadcast([P, HEADS, H2]), ALU.mult)
                last.then_inc(turn_s_ready, 1)

            def keep_x1(u, b):
                k = 2 * u + b
                pool.wait_ge(p_full[0], nth(7, k, SHIFT_USE))
                pool.sem_inc(pool_gate, 1)
                nc.gpsimd.tensor_scalar(x1_prev[b][:, :], x1[b][:, P:D], band[:, 2 * KEYS:2 * KEYS + 1], None, ALU.mult)
                pool.wait_ge(wff_in, 16 * 7 * ((u >> TILE_BITS) + 1))
                pool.wait_ge(h_stored[b], 16 * (u + 1))
                nc.gpsimd.tensor_tensor(out_tile[b][:, :], x1[b][:, :], b2[:, :], ALU.add).then_inc(x1_kept, 1)

            def reciprocal_root(u, b):
                pool.wait_ge(ve_ready, nth(1, 2 * u + b))
                nc.gpsimd.tensor_tensor(rstd[:, :], ve[:, :], minus_half[:, 0:1], ALU.pow).then_inc(rstd_ready, 1)

            def unit(u, b, nxt):
                def A(f, *a):
                    if nxt is not None:
                        f(*nxt, *a)
                A(move_window)
                A(turn, 0)
                A(turn, 1)
                reciprocal_root(u, b)
                keep_x1(u, b)
                if b == 0 and nxt is not None and not (isinstance(u, int) and u == ITERS - 1):
                    rotary(u + 1, 2 * u + 1)

            pool.wait_ge(const_in, 48)
            pool.wait_ge(consts_set, 1)
            rotary(0, -1)
            move_window(0, 0)
            turn(0, 0, 0)
            turn(0, 0, 1)
            with pool.Fori(0, ITERS - 1) as u:
                unit(u, 0, (u, 1))
                unit(u, 1, (u + 1, 0))
            unit(ITERS - 1, 0, (ITERS - 1, 1))
            unit(ITERS - 1, 1, None)


def gla_stage(nc, ident_dram, spans_dram, after_dram, pairs_dram, wqk_dram, wk_dram, wv_dram, wg_dram, gk1_dram,
              gk2_dram, gkb_dram, norm_dram, wo_dram, h1_dram, tower_out, h3_dram):
    NB, T, D = h1_dram.shape
    KC = D // P
    TILES = T // P
    HEADS = 4
    DV = wv_dram.shape[1] // HEADS
    DK = wk_dram.shape[1] // HEADS
    V = HEADS * DV
    HALVES = HEADS * DK // P
    LEVELS = 7
    DIAG, CARRY = LEVELS, LEVELS
    RANK = gk1_dram.shape[1]
    OC = V // P
    INV_NORM = 1.0 / 16.0
    Q_SCALE = DK ** -0.5

    USES = {0: ["x0", "x1", "oT0", "oT1"],
            1: ["z1_0", "z1_1", "z0", "z1", "after0", "after1"],
            2: ["k0", "k1", "decay0", "decay1", "o0", "wo0"],
            3: ["v0", "v1", "decay0", "decay1", "kv0"],
            4: ["g0", "g1", "decay0", "decay1", "o1", "wo1"],
            5: ["qk0", "qk1", "decay0", "decay1", "kv1"],
            6: [f"pair{b}_{l}" for b in range(NB) for l in range(0, LEVELS + 1, 2)],
            7: [f"pair{b}_{l}" for b in range(NB) for l in range(1, LEVELS + 1, 2)]}

    with ExitStack() as ctx:
        ctx.enter_context(nc.cleanup_on_exit())
        def sb(name, shape, dt=F32):
            return ctx.enter_context(nc.sbuf_tensor("ga_" + name, shape, dt))

        def sem(name):
            return nc.alloc_semaphore("ga_" + name)

        def each(name, shape):
            return [sb(f"{name}{b}", shape) for b in range(NB)]

        ident = sb("ident", [P, P])
        spans = sb("spans", [P, LEVELS + 1, P])
        after = sb("after", [P, P])
        pairs = sb("pairs", [P, LEVELS + 1, P], mybir.dt.int32)
        wqk = sb("wqk", [P, KC, 2 * HALVES * P])
        wk = sb("wk", [P, KC, HALVES * P])
        wv = sb("wv", [P, KC, V])
        wg = sb("wg", [P, KC, V])
        gk1 = sb("gk1", [P, KC, RANK])
        gk2 = sb("gk2", [RANK, HEADS * DK])
        gkb = sb("gkb", [P, HEADS * DK])
        norm_w = sb("norm_w", [P, DV])
        wo = sb("wo", [P, OC, D])
        minus_half = sb("minus_half", [P, HEADS])
        h1, tower, h2, h3 = each("h1", [P, D]), each("tower", [P, D]), each("h2", [P, D]), each("h3", [P, D])
        stats, mv, ve, rstd = each("stats", [P, 6]), each("mv", [P, 2]), each("ve", [P, 1]), each("rstd", [P, 1])
        xn, xT = each("xn", [P, D]), each("xT", [P, KC, P])
        z1T, z = each("z1T", [RANK, P]), each("z", [P, HEADS * DK])
        small, soft, gates = each("small", [P, HEADS * DK]), each("soft", [P, HEADS * DK]), each("gates", [P, HEADS * DK])
        k_rows, k_left, decay_left = each("k_rows", [P, 256]), each("k_left", [P, 256]), each("decay_left", [P, 256])
        v, silu, out_gate = each("v", [P, V]), each("silu", [P, V]), each("out_gate", [P, V])
        q = [[sb(f"q{b}{j}", [P, LEVELS + 1, P]) for j in range(HALVES)] for b in range(NB)]
        q_carry = [[sb(f"q_carry{b}{j}", [P, P]) for j in range(HALVES)] for b in range(NB)]
        k = [[sb(f"k{b}{h}", [P, LEVELS + 1, P]) for h in range(HEADS)] for b in range(NB)]
        decay = [[sb(f"decay{b}{j}", [P, LEVELS + 1, P]) for j in range(HALVES)] for b in range(NB)]
        weights = each("weights", [P, HEADS, P])
        state = [[sb(f"state{b}{j}", [P, 2 * DV]) for j in range(HALVES)] for b in range(NB)]
        squares, ssum = each("squares", [P, HEADS, DV]), each("ssum", [P, HEADS])
        meansq, rms = each("meansq", [P, HEADS]), each("rms", [P, HEADS])
        gated, gT = each("gated", [P, V]), each("gT", [P, OC, P])
        bank = [ctx.enter_context(nc.psum_tensor(f"ga_bank{j}", [P, 512], F32)) for j in range(8)]

        full, drained = [sem(f"full{j}") for j in range(8)], [sem(f"drained{j}") for j in range(8)]
        const_in, filled = sem("const_in"), sem("filled")
        NAMES = ["h2_ready", "stats_ready", "mv_ready", "ve_ready", "rstd_ready", "xn_ready", "z_ready",
                 "small_ready", "exp_ready", "soft_ready", "gates_ready", "k_kept", "q_ready", "k_ready",
                 "k_left_ready", "state_ready", "squared", "meansq_ready", "rms_ready", "out_gate_ready",
                 "gated_ready", "h3_ready"]
        s = [{n: sem(f"{n}{b}") for n in NAMES} for b in range(NB)]
        h1_in, tower_in, h3_stored = [[sem(f"{n}{b}") for b in range(NB)] for n in ("h1_in", "tower_in", "h3_stored")]
        act_gate, dve_gate, pool_gate, sp_gate, pe_gate = (sem("act_gate"), sem("dve_gate"), sem("pool_gate"),
                                                           sem("sp_gate"), sem("pe_gate"))

        def now(i):
            return i + 2

        def use(i, j, name):
            return len(USES[j]) * (i + 1) + USES[j].index(name) + 1

        def head_rows(h):
            return slice(DK * (h % 2), DK * (h % 2) + DK)

        block = ctx.enter_context(nc.Block())

        @block.sync
        def _(sp):
            for j in range(8):
                sp.sem_inc(full[j], len(USES[j]))
                sp.sem_inc(drained[j], len(USES[j]))
            for b in range(NB):
                for n in NAMES:
                    sp.sem_inc(s[b][n], HEADS if n == "k_ready" else 1)
                sp.sem_inc(h3_stored[b], 16)

            def load(i, b):
                sp.dma_start(h1[b][:, :], h1_dram[b, bass.ds(i * P, P), :]).then_inc(h1_in[b], 16)
                sp.dma_start(tower[b][:, :], tower_out[b, bass.ds(i * P, P), :]).then_inc(tower_in[b], 16)

            def store(i, b):
                sp.wait_ge(h3_stored[b], 16 * (i + 1))
                sp.sem_inc(sp_gate, 1)
                sp.wait_ge(s[b]["h3_ready"], now(i))
                sp.sem_inc(sp_gate, 1)
                sp.dma_start(h3_dram[b, bass.ds(i * P, P), :], h3[b][:, :]).then_inc(h3_stored[b], 16)

            for b in range(NB):
                load(0, b)
            for dst, src in ((ident[:, :], ident_dram), (gk1[:, :, :], gk1_dram.rearrange("(c p) n -> p c n", p=P)),
                             (gk2[:, :], gk2_dram), (gkb[:, :], gkb_dram.partition_broadcast(P)),
                             (wk[:, :, :], wk_dram.rearrange("(c p) n -> p c n", p=P)),
                             (wv[:, :, :], wv_dram.rearrange("(c p) n -> p c n", p=P)),
                             (wg[:, :, :], wg_dram.rearrange("(c p) n -> p c n", p=P)),
                             (wqk[:, :, :], wqk_dram.rearrange("(c p) n -> p c n", p=P)),
                             (spans[:, :, :], spans_dram), (after[:, :], after_dram), (pairs[:, :, :], pairs_dram),
                             (norm_w[:, :], norm_dram.partition_broadcast(P)),
                             (wo[:, :, :], wo_dram.rearrange("(c p) n -> p c n", p=P))):
                sp.dma_start(dst, src).then_inc(const_in, 16)
            with sp.Fori(0, TILES - 1) as i:
                for b in range(NB):
                    sp.wait_ge(s[b]["h2_ready"], now(i))
                    sp.sem_inc(sp_gate, 1)
                    load(i + 1, b)
                for b in range(NB):
                    store(i, b)
            for b in range(NB):
                store(TILES - 1, b)
            for b in range(NB):
                sp.wait_ge(h3_stored[b], 16 * (TILES + 1))

        CONSTS = 16 * 13

        @block.tensor
        def _(pe):
            def mm(out, lhsT, rhs, start, stop):
                return nc.tensor.matmul(out, lhsT, rhs, start=start, stop=stop)

            def free(i, j, name):
                pe.wait_ge(drained[j], use(i, j, name) - 1)

            def project(i, b, j, name, w):
                free(i, j, f"{name}{b}")
                for c in range(KC):
                    last = mm(bank[j][:, 0:w.shape[2]], xT[b][:, c, :], w[:, c, :], c == 0, c == KC - 1)
                last.then_inc(full[j], 1)

            def project_turned(i, b):
                free(i, 5, f"qk{b}")
                for n in range(2 * HALVES):
                    for c in range(KC):
                        last = mm(bank[5][:, n * P:(n + 1) * P], wqk[:, c, n * P:(n + 1) * P], xT[b][:, c, :], c == 0,
                                  c == KC - 1)
                last.then_inc(full[5], 1)

            def gate_sums(i, b):
                pe.wait_ge(s[b]["gates_ready"], now(i))
                for j in range(HALVES):
                    for half in range(2):
                        at = 2 + 2 * j + half
                        free(i, at, f"decay{b}")
                        mm(bank[at][:, :], gates[b][:, j * P:(j + 1) * P],
                           spans[:, 4 * half:4 * half + 4, :].rearrange("p l t -> p (l t)"), True, True)\
                            .then_inc(full[at], 1)
                free(i, 1, f"after{b}")
                mm(bank[1][:, 0:HEADS * DK], after[:, :], gates[b][:, :], True, True).then_inc(full[1], 1)

            def pair_products(i, b):
                pe.wait_ge(s[b]["q_ready"], now(i))
                pe.wait_ge(s[b]["k_ready"], HEADS * (i + 2))
                for l in range(LEVELS + 1):
                    j = 6 + l % 2
                    free(i, j, f"pair{b}_{l}")
                    for h in range(HEADS):
                        last = mm(bank[j][:, h * P:(h + 1) * P], k[b][h][:, l, :], q[b][h // 2][:, l, :], True, True)
                    last.then_inc(full[j], 1)

            def outputs(i, b):
                free(i, 2 + 2 * b, f"o{b}")
                pe.wait_ge(s[b]["state_ready"], now(i - 1))
                pe.wait_ge(drained[7], use(i, 7, f"pair{b}_{LEVELS}"))
                pe.wait_ge(drained[3], use(i, 3, f"v{b}"))
                for j in range(HALVES):
                    mm(bank[2 + 2 * b][:, j * 2 * DV:(j + 1) * 2 * DV], q_carry[b][j][:, :], state[b][j][:, :], True, False)
                    for h in (2 * j, 2 * j + 1):
                        last = mm(bank[2 + 2 * b][:, h * DV:(h + 1) * DV], weights[b][:, h, :], v[b][:, h * DV:(h + 1) * DV],
                                  False, h % 2 == 1)
                last.then_inc(full[2 + 2 * b], 1)
                free(i, 3 + 2 * b, f"kv{b}")
                pe.wait_ge(s[b]["k_left_ready"], now(i))
                for j in range(HALVES):
                    last = mm(bank[3 + 2 * b][:, j * 2 * DV:(j + 1) * 2 * DV], k_left[b][:, j * P:(j + 1) * P],
                              v[b][:, j * 2 * DV:(j + 1) * 2 * DV], True, True)
                last.then_inc(full[3 + 2 * b], 1)

            pe.wait_ge(const_in, CONSTS)
            with pe.Fori(0, TILES) as i:
                for b in range(NB):
                    pe.wait_ge(s[b]["xn_ready"], now(i))
                    free(i, 0, f"x{b}")
                    for c in range(KC):
                        last = nc.tensor.transpose(bank[0][:, c * P:(c + 1) * P], xn[b][:, c * P:(c + 1) * P],
                                                   ident[:, :])
                    last.then_inc(full[0], 1)
                for b in range(NB):
                    pe.wait_ge(drained[0], use(i, 0, f"x{b}"))
                    free(i, 1, f"z1_{b}")
                    for c in range(KC):
                        last = mm(bank[1][0:RANK, 0:P], gk1[:, c, :], xT[b][:, c, :], c == 0, c == KC - 1)
                    last.then_inc(full[1], 1)
                project(i, 0, 2, "k", wk)
                for b in range(NB):
                    pe.wait_ge(drained[1], use(i, 1, f"z1_{b}"))
                    free(i, 1, f"z{b}")
                    mm(bank[1][:, 0:HEADS * DK], z1T[b][:, :], gk2[:, :], True, True).then_inc(full[1], 1)
                project(i, 0, 3, "v", wv)
                project_turned(i, 0)
                project(i, 0, 4, "g", wg)
                project(i, 1, 2, "k", wk)
                project(i, 1, 3, "v", wv)
                project_turned(i, 1)
                project(i, 1, 4, "g", wg)
                gate_sums(i, 0)
                gate_sums(i, 1)
                pair_products(i, 0)
                pair_products(i, 1)
                for b in range(NB):
                    outputs(i, b)
                for b in range(NB):
                    pe.wait_ge(s[b]["gated_ready"], now(i))
                    free(i, 0, f"oT{b}")
                    for c in range(OC):
                        last = nc.tensor.transpose(bank[0][:, c * P:(c + 1) * P], gated[b][:, c * P:(c + 1) * P],
                                                   ident[:, :])
                    last.then_inc(full[0], 1)
                for b in range(NB):
                    pe.wait_ge(drained[0], use(i, 0, f"oT{b}"))
                    free(i, 2 + 2 * b, f"wo{b}")
                    for c in range(OC):
                        last = mm(bank[2 + 2 * b][:, 0:D], gT[b][:, c, :], wo[:, c, :], c == 0, c == OC - 1)
                    last.then_inc(full[2 + 2 * b], 1)

        @block.scalar
        def _(act):
            act.wait_ge(filled, 1)
            act.wait_ge(const_in, CONSTS)
            with act.Fori(0, TILES) as i:
                for b in range(NB):
                    act.wait_ge(full[0], use(i, 0, f"x{b}"))
                    nc.scalar.copy(xT[b][:, :, :].rearrange("p c t -> p (c t)"), bank[0][:, 0:D])\
                        .then_inc(drained[0], 1)
                for b in range(NB):
                    act.wait_ge(full[1], use(i, 1, f"z1_{b}"))
                    nc.scalar.copy(z1T[b][:, :], bank[1][0:RANK, 0:P]).then_inc(drained[1], 1)
                for b in range(NB):
                    act.wait_ge(full[3], use(i, 3, f"v{b}"))
                    nc.scalar.copy(v[b][:, :], bank[3][:, :]).then_inc(drained[3], 1)
                    act.wait_ge(full[5], use(i, 5, f"qk{b}"))
                    for j in range(HALVES):
                        nc.scalar.mul(q[b][j][:, DIAG, :], bank[5][:, j * P:(j + 1) * P], Q_SCALE)
                    for h in range(HEADS):
                        rows, n = head_rows(h), HALVES + h // 2
                        last = nc.scalar.copy(k[b][h][rows, DIAG, :], bank[5][rows, n * P:(n + 1) * P])
                    last.then_inc(drained[5], 1)
                    act.wait_ge(s[b]["small_ready"], now(i))
                    nc.scalar.activation(soft[b][:, :], small[b][:, :], ACT.Exp).then_inc(s[b]["exp_ready"], 1)
                    act.wait_ge(s[b]["exp_ready"], now(i))
                    nc.scalar.activation(soft[b][:, :], soft[b][:, :], ACT.Ln, bias=1.0)\
                        .then_inc(s[b]["soft_ready"], 1)
                    act.wait_ge(s[b]["out_gate_ready"], now(i - 1))
                    act.wait_ge(full[4], use(i, 4, f"g{b}"))
                    nc.scalar.activation(silu[b][:, :], bank[4][:, :], ACT.Silu).then_inc(drained[4], 1)
                for b in range(NB):
                    act.wait_ge(s[b]["state_ready"], now(i - 1))
                    for at in range(2, 6):
                        j, half = (at - 2) // 2, at % 2
                        act.wait_ge(full[at], use(i, at, f"decay{b}"))
                        nc.scalar.activation(decay[b][j][:, 4 * half:4 * half + 4, :].rearrange("p l t -> p (l t)"),
                                             bank[at][:, :], ACT.Exp, scale=INV_NORM).then_inc(drained[at], 1)
                    act.wait_ge(full[1], use(i, 1, f"after{b}"))
                    nc.scalar.activation(decay_left[b][:, :], bank[1][:, 0:HEADS * DK], ACT.Exp, scale=INV_NORM)\
                        .then_inc(drained[1], 1)
                for b in range(NB):
                    act.wait_ge(full[2 + 2 * b], use(i, 2 + 2 * b, f"o{b}"))
                    for h in range(HEADS):
                        last = nc.scalar.activation(squares[b][:, h, :], bank[2 + 2 * b][:, h * DV:(h + 1) * DV], ACT.Square,
                                                    accum_out=ssum[b][:, h:h + 1])
                    last.then_inc(s[b]["squared"], 1)
                for b in range(NB):
                    act.wait_ge(full[0], use(i, 0, f"oT{b}"))
                    nc.scalar.copy(gT[b][:, :, :].rearrange("p c t -> p (c t)"), bank[0][:, :])\
                        .then_inc(drained[0], 1)

        @block.gpsimd
        def _(pool):
            pool.wait_ge(filled, 1)
            pool.wait_ge(const_in, CONSTS)
            with pool.Fori(0, TILES) as i:
                for b in range(NB):
                    pool.wait_ge(s[b]["ve_ready"], now(i))
                    nc.gpsimd.tensor_tensor(rstd[b][:, :], ve[b][:, :], minus_half[:, 0:1], ALU.pow)\
                        .then_inc(s[b]["rstd_ready"], 1)
                for b in range(NB):
                    pool.wait_ge(drained[5], use(i, 5, f"qk{b}"))
                    pool.wait_ge(drained[3], use(i, 3, f"decay{b}"))
                    pool.wait_ge(drained[5], use(i, 5, f"decay{b}"))
                    for h in range(HEADS):
                        rows = head_rows(h)
                        nc.gpsimd.tensor_tensor(
                            k[b][h][rows, 0:LEVELS, :], decay[b][h // 2][rows, 0:LEVELS, :],
                            k[b][h][rows, DIAG:DIAG + 1, :].to_broadcast([DK, LEVELS, P]), ALU.mult)\
                            .then_inc(s[b]["k_ready"], 1)
                        pool.wait_ge(s[b]["k_ready"], HEADS * (i + 1) + h + 1)
                for b in range(NB):
                    pool.wait_ge(drained[4], use(i, 4, f"g{b}"))
                    pool.wait_ge(s[b]["gated_ready"], now(i - 1))
                    nc.gpsimd.tensor_tensor(out_gate[b][:, :].rearrange("p (h d) -> p h d", d=DV),
                                            silu[b][:, :].rearrange("p (h d) -> p h d", d=DV),
                                            norm_w[:, :].unsqueeze(1).to_broadcast([P, HEADS, DV]), ALU.mult)\
                        .then_inc(s[b]["out_gate_ready"], 1)
                for b in range(NB):
                    pool.wait_ge(s[b]["squared"], now(i))
                    pool.sem_inc(pool_gate, 1)
                    nc.gpsimd.tensor_scalar(meansq[b][:, :], ssum[b][:, :], 1.0 / DV, 1e-5, ALU.mult, ALU.add)\
                        .then_inc(s[b]["meansq_ready"], 1)
                    pool.wait_ge(s[b]["meansq_ready"], now(i))
                    nc.gpsimd.tensor_tensor(rms[b][:, :], meansq[b][:, :], minus_half[:, :], ALU.pow)\
                        .then_inc(s[b]["rms_ready"], 1)

        @block.vector
        def _(dve):
            for b in range(NB):
                for h in range(HEADS):
                    nc.vector.memset(k[b][h][:, :, :], 0.0)
                for j in range(HALVES):
                    nc.vector.memset(state[b][j][:, :], 0.0)
                nc.vector.memset(weights[b][:, :, :], 0.0)
            nc.vector.memset(minus_half[:, :], -0.5).then_inc(filled, 1)
            dve.wait_ge(const_in, CONSTS)
            dve.wait_ge(filled, 1)
            with dve.Fori(0, TILES) as i:
                for b in range(NB):
                    dve.wait_ge(h1_in[b], 16 * (i + 1))
                    dve.wait_ge(tower_in[b], 16 * (i + 1))
                    dve.wait_ge(s[b]["h3_ready"], now(i - 1))
                    nc.vector.tensor_tensor(h2[b][:, :], h1[b][:, :], tower[b][:, :], ALU.add)\
                        .then_inc(s[b]["h2_ready"], 1)
                for b in range(NB):
                    dve.wait_ge(s[b]["h2_ready"], now(i))
                    dve.sem_inc(dve_gate, 1)
                    nc.vector.bn_stats(stats[b][:, :], h2[b][:, :]).then_inc(s[b]["stats_ready"], 1)
                for b in range(NB):
                    dve.wait_ge(s[b]["stats_ready"], now(i))
                    dve.sem_inc(dve_gate, 1)
                    nc.vector.bn_aggr(mv[b][:, :], stats[b][:, :]).then_inc(s[b]["mv_ready"], 1)
                for b in range(NB):
                    dve.wait_ge(s[b]["mv_ready"], now(i))
                    nc.vector.tensor_scalar(ve[b][:, :], mv[b][:, 1:2], 1e-5, None, ALU.add)\
                        .then_inc(s[b]["ve_ready"], 1)
                for b in range(NB):
                    dve.wait_ge(s[b]["rstd_ready"], now(i))
                    nc.vector.tensor_scalar(xn[b][:, :], h2[b][:, :], mv[b][:, 0:1], rstd[b][:, :], ALU.subtract,
                                            ALU.mult).then_inc(s[b]["xn_ready"], 1)
                for b in range(NB):
                    dve.wait_ge(s[b]["gates_ready"], now(i - 1))
                    dve.wait_ge(full[1], use(i, 1, f"z{b}"))
                    nc.vector.tensor_tensor(z[b][:, :], bank[1][:, 0:HEADS * DK], gkb[:, :], ALU.add)\
                        .then_inc(drained[1], 1)
                    dve.wait_ge(drained[1], use(i, 1, f"z{b}"))
                    nc.vector.scalar_tensor_tensor(small[b][:, :], z[b][:, :], -1.0, z[b][:, :], ALU.mult, ALU.min)\
                        .then_inc(s[b]["small_ready"], 1)
                for b in range(NB):
                    dve.wait_ge(s[b]["k_left_ready"], now(i - 1))
                    dve.wait_ge(full[2], use(i, 2, f"k{b}"))
                    nc.vector.tensor_copy(k_rows[b][:, :], bank[2][:, 0:HEADS * DK]).then_inc(drained[2], 1)
                    dve.wait_ge(s[b]["soft_ready"], now(i))
                    dve.wait_ge(full[1], use(i - 1, 1, f"after{b}"))
                    nc.vector.scalar_tensor_tensor(gates[b][:, :], z[b][:, :], 0.0, soft[b][:, :], ALU.min,
                                                   ALU.subtract).then_inc(s[b]["gates_ready"], 1)
                for b in range(NB):
                    dve.wait_ge(drained[5], use(i, 5, f"qk{b}"))
                    for j in range(HALVES):
                        dve.wait_ge(drained[3 + 2 * j], use(i, 3 + 2 * j, f"decay{b}"))
                        nc.vector.tensor_tensor(q[b][j][:, 0:LEVELS, :], decay[b][j][:, 0:LEVELS, :],
                                                q[b][j][:, DIAG:DIAG + 1, :].to_broadcast([P, LEVELS, P]), ALU.mult)
                        last = nc.vector.tensor_tensor(q_carry[b][j][:, :], decay[b][j][:, CARRY, :],
                                                       q[b][j][:, DIAG, :], ALU.mult)
                    last.then_inc(s[b]["q_ready"], 1)
                    dve.wait_ge(drained[2], use(i, 2, f"k{b}"))
                    dve.wait_ge(drained[1], use(i, 1, f"after{b}"))
                    nc.vector.tensor_tensor(k_left[b][:, :], decay_left[b][:, :], k_rows[b][:, :], ALU.mult)\
                        .then_inc(s[b]["k_left_ready"], 1)
                for b in range(NB):
                    for l in range(LEVELS + 1):
                        j = 6 + l % 2
                        if l:
                            dve.wait_ge(drained[6 + (l - 1) % 2], use(i, 6 + (l - 1) % 2, f"pair{b}_{l - 1}"))
                        dve.wait_ge(full[j], use(i, j, f"pair{b}_{l}"))
                        dve.sem_inc(dve_gate, 1)
                        nc.vector.copy_predicated(weights[b][:, :, :],
                                                  pairs[:, l:l + 1, :].to_broadcast([P, HEADS, P]),
                                                  bank[j][:, :].rearrange("p (h t) -> p h t", t=P))\
                            .then_inc(drained[j], 1)
                for b in range(NB):
                    dve.wait_ge(s[b]["state_ready"], now(i - 1))
                    dve.wait_ge(full[3 + 2 * b], use(i, 3 + 2 * b, f"kv{b}"))
                    for h in range(HEADS):
                        j, rows, cols = h // 2, head_rows(h), slice((h % 2) * DV, (h % 2 + 1) * DV)
                        last = nc.vector.scalar_tensor_tensor(
                            state[b][j][rows, cols], state[b][j][rows, cols], decay[b][j][rows, CARRY, P - 1:P],
                            bank[3 + 2 * b][rows, h * DV:(h + 1) * DV], ALU.mult, ALU.add)
                    last.then_inc(drained[3 + 2 * b], 1)
                    dve.wait_ge(drained[3 + 2 * b], use(i, 3 + 2 * b, f"kv{b}"))
                    dve.sem_inc(s[b]["state_ready"], 1)
                    dve.wait_ge(s[b]["out_gate_ready"], now(i))
                    dve.wait_ge(s[b]["rms_ready"], now(i))
                    for h in range(HEADS):
                        cols = slice(h * DV, (h + 1) * DV)
                        last = nc.vector.scalar_tensor_tensor(gated[b][:, cols], bank[2 + 2 * b][:, cols], rms[b][:, h:h + 1],
                                                              out_gate[b][:, cols], ALU.mult, ALU.mult)
                    last.then_inc(drained[2 + 2 * b], 1)
                    dve.wait_ge(drained[2 + 2 * b], use(i, 2 + 2 * b, f"o{b}"))
                    dve.sem_inc(s[b]["gated_ready"], 1)
                for b in range(NB):
                    dve.wait_ge(h3_stored[b], 16 * (i + 1))
                    dve.wait_ge(full[2 + 2 * b], use(i, 2 + 2 * b, f"wo{b}"))
                    nc.vector.tensor_tensor(h3[b][:, :], bank[2 + 2 * b][:, 0:D], h2[b][:, :], ALU.add)\
                        .then_inc(drained[2 + 2 * b], 1)
                    dve.wait_ge(drained[2 + 2 * b], use(i, 2 + 2 * b, f"wo{b}"))
                    dve.sem_inc(s[b]["h3_ready"], 1)


def gla_consts():
    import numpy as np
    N, LEVELS = 128, 7
    u = np.arange(N)[:, None]
    t = np.arange(N)[None, :]
    spans = np.zeros((N, LEVELS + 1, N), np.float32)
    pairs = np.zeros((N, LEVELS + 1, N), np.int32)
    for l in range(LEVELS):
        m = N >> (l + 1)
        middle = t // (2 * m) * (2 * m) + m
        right = t >= middle
        spans[:, l, :] = np.where(right, (u >= middle) & (u <= t), (u > t) & (u < middle))
        s = u
        pairs[:, l, :] = right & (s // (2 * m) == t // (2 * m)) & (s < middle)
    spans[:, LEVELS, :] = u <= t
    pairs[:, LEVELS, :] = u == t
    after = (u > t).astype(np.float32)
    return spans, after, pairs


def moe_route(nc, ident_dram, h3_dram, gate_w_dram, gate_b_dram, h3_all, xT_all, comb_all):
    NB, T, D = h3_dram.shape
    KC = D // P
    TILES = T // P
    EXPERTS = gate_w_dram.shape[1]
    TOP, WIDE = 4, 8
    SLOTS = EXPERTS + WIDE
    LOWEST, TAKEN = -3.0e38, 3.0e38
    ROUTE_SCALE = 2.5

    with ExitStack() as ctx:
        ctx.enter_context(nc.cleanup_on_exit())
        def sb(name, shape, dt=F32):
            return ctx.enter_context(nc.sbuf_tensor("mr_" + name, shape, dt))

        def sem(name):
            return nc.alloc_semaphore("mr_" + name)

        def each(name, shape):
            return [sb(f"{name}{b}", shape) for b in range(NB)]

        ident = sb("ident", [P, P])
        gate_w = sb("gate_w", [P, KC, EXPERTS])
        gate_b = sb("gate_b", [P, EXPERTS])
        minus_half = sb("minus_half", [P, 1])
        stats, mv, ve, rstd = each("stats", [P, 6]), each("mv", [P, 2]), each("ve", [P, 1]), each("rstd", [P, 1])
        xn, xT = each("xn", [P, D]), each("xT", [P, KC, P])
        scores, biased = each("scores", [P, EXPERTS]), each("biased", [P, SLOTS])
        best, chosen = each("best", [P, WIDE]), each("chosen", [P, WIDE])
        marked, taken, total = each("marked", [P, SLOTS]), each("taken", [P, EXPERTS]), each("total", [P, 1])
        t_bank = [ctx.enter_context(nc.psum_tensor(f"mr_t{b}", [P, 512], F32)) for b in range(NB)]
        g_bank = [ctx.enter_context(nc.psum_tensor(f"mr_g{b}", [P, 512], F32)) for b in range(NB)]
        const_in, h3_in, filled = sem("const_in"), sem("h3_in"), sem("filled")
        NAMES = ["stats_ready", "mv_ready", "ve_ready", "rstd_ready", "xn_ready", "t_full", "xT_ready", "xT_kept",
                 "g_full", "scores_ready", "biased_ready", "best_ready", "chosen_ready", "marked_ready", "taken_ready",
                 "weights_ready", "total_ready", "inverse_ready", "comb_ready"]
        s = [{n: sem(f"{n}{b}") for n in NAMES} for b in range(NB)]
        act_gate, dve_gate, pool_gate = sem("act_gate"), sem("dve_gate"), sem("pool_gate")

        def now(i):
            return i + 2

        def rows(b, i):
            return bass.ds(b * TILES + i, 1)

        block = ctx.enter_context(nc.Block())

        @block.sync
        def _(sp):
            for b in range(NB):
                for n in NAMES:
                    sp.sem_inc(s[b][n], 1)
            sp.dma_start(h3_all[:, :, :], h3_dram.rearrange("b (i p) d -> p (b i) d", p=P)).then_inc(h3_in, 16)
            for dst, src in ((ident[:, :], ident_dram), (gate_w[:, :, :], gate_w_dram.rearrange("(c p) n -> p c n", p=P)),
                             (gate_b[:, :], gate_b_dram.partition_broadcast(P))):
                sp.dma_start(dst, src).then_inc(const_in, 16)

        @block.vector
        def _(dve):
            nc.vector.memset(minus_half[:, :], -0.5)
            nc.vector.memset(comb_all[:, :, :], 1.0)
            for b in range(NB):
                nc.vector.memset(biased[b][:, :], LOWEST)
                nc.vector.memset(chosen[b][:, :], LOWEST)
            nc.vector.memset(xn[0][:, :], 0.0).then_inc(filled, 1)
            dve.wait_ge(const_in, 48)
            dve.wait_ge(h3_in, 16)
            dve.wait_ge(filled, 1)
            with dve.Fori(0, TILES) as i:
                for b in range(NB):
                    nc.vector.bn_stats(stats[b][:, :], h3_all[:, rows(b, i), :].rearrange("p a d -> p (a d)"))\
                        .then_inc(s[b]["stats_ready"], 1)
                for b in range(NB):
                    dve.wait_ge(s[b]["stats_ready"], now(i))
                    dve.sem_inc(dve_gate, 1)
                    nc.vector.bn_aggr(mv[b][:, :], stats[b][:, :]).then_inc(s[b]["mv_ready"], 1)
                for b in range(NB):
                    dve.wait_ge(s[b]["mv_ready"], now(i))
                    nc.vector.tensor_scalar(ve[b][:, :], mv[b][:, 1:2], 1e-5, None, ALU.add)\
                        .then_inc(s[b]["ve_ready"], 1)
                for b in range(NB):
                    dve.wait_ge(s[b]["rstd_ready"], now(i))
                    dve.wait_ge(s[b]["t_full"], now(i - 1))
                    dve.sem_inc(dve_gate, 1)
                    nc.vector.tensor_scalar(xn[b][:, :], h3_all[:, rows(b, i), :].rearrange("p a d -> p (a d)"),
                                            mv[b][:, 0:1], rstd[b][:, :], ALU.subtract, ALU.mult)\
                        .then_inc(s[b]["xn_ready"], 1)
                for b in range(NB):
                    dve.wait_ge(s[b]["scores_ready"], now(i))
                    dve.wait_ge(s[b]["taken_ready"], now(i - 1))
                    nc.vector.tensor_tensor(biased[b][:, 0:EXPERTS], scores[b][:, :], gate_b[:, :], ALU.add)\
                        .then_inc(s[b]["biased_ready"], 1)
                for b in range(NB):
                    dve.wait_ge(s[b]["biased_ready"], now(i))
                    dve.wait_ge(s[b]["chosen_ready"], now(i - 1))
                    dve.sem_inc(dve_gate, 1)
                    nc.vector.max(best[b][:, :], biased[b][:, :]).then_inc(s[b]["best_ready"], 1)
                for b in range(NB):
                    dve.wait_ge(s[b]["best_ready"], now(i))
                    dve.wait_ge(s[b]["marked_ready"], now(i - 1))
                    nc.vector.tensor_copy(chosen[b][:, 0:TOP], best[b][:, 0:TOP]).then_inc(s[b]["chosen_ready"], 1)
                for b in range(NB):
                    dve.wait_ge(s[b]["chosen_ready"], now(i))
                    dve.sem_inc(dve_gate, 1)
                    nc.vector.match_replace(marked[b][:, :], chosen[b][:, :], biased[b][:, :], TAKEN)\
                        .then_inc(s[b]["marked_ready"], 1)
                for b in range(NB):
                    dve.wait_ge(s[b]["marked_ready"], now(i))
                    nc.vector.tensor_tensor(taken[b][:, :], marked[b][:, 0:EXPERTS], biased[b][:, 0:EXPERTS],
                                            ALU.not_equal).then_inc(s[b]["taken_ready"], 1)
                for b in range(NB):
                    dve.wait_ge(s[b]["taken_ready"], now(i))
                    nc.vector.tensor_tensor(taken[b][:, :], taken[b][:, :], scores[b][:, :], ALU.mult)\
                        .then_inc(s[b]["weights_ready"], 1)
                for b in range(NB):
                    dve.wait_ge(s[b]["weights_ready"], now(i))
                    nc.vector.tensor_reduce(total[b][:, :], taken[b][:, :], AX, ALU.add)\
                        .then_inc(s[b]["total_ready"], 1)
                for b in range(NB):
                    dve.wait_ge(s[b]["total_ready"], now(i))
                    nc.vector.reciprocal(total[b][:, :], total[b][:, :]).then_inc(s[b]["inverse_ready"], 1)
                for b in range(NB):
                    dve.wait_ge(s[b]["inverse_ready"], now(i))
                    dve.sem_inc(dve_gate, 1)
                    nc.vector.tensor_scalar(comb_all[:, rows(b, i), 0:EXPERTS].rearrange("p a d -> p (a d)"),
                                            taken[b][:, :], total[b][:, :], ROUTE_SCALE, ALU.mult, ALU.mult)\
                        .then_inc(s[b]["comb_ready"], 1)
                for b in range(NB):
                    dve.wait_ge(s[b]["comb_ready"], now(i))

        @block.gpsimd
        def _(pool):
            pool.wait_ge(filled, 1)
            with pool.Fori(0, TILES) as i:
                for b in range(NB):
                    pool.wait_ge(s[b]["ve_ready"], now(i))
                    nc.gpsimd.tensor_tensor(rstd[b][:, :], ve[b][:, :], minus_half[:, :], ALU.pow)\
                        .then_inc(s[b]["rstd_ready"], 1)
                for b in range(NB):
                    pool.wait_ge(s[b]["xT_ready"], now(i))
                    pool.sem_inc(pool_gate, 1)
                    nc.gpsimd.tensor_copy(xT_all[:, rows(b, i), :, :].rearrange("p a c t -> p (a c t)"),
                                          xT[b][:, :, :].rearrange("p c t -> p (c t)")).then_inc(s[b]["xT_kept"], 1)

        @block.tensor
        def _(pe):
            pe.wait_ge(const_in, 48)
            with pe.Fori(0, TILES) as i:
                for b in range(NB):
                    pe.wait_ge(s[b]["xn_ready"], now(i))
                    for c in range(KC):
                        last = nc.tensor.transpose(t_bank[b][:, c * P:(c + 1) * P], xn[b][:, c * P:(c + 1) * P],
                                                   ident[:, :])
                    last.then_inc(s[b]["t_full"], 1)
                for b in range(NB):
                    pe.wait_ge(s[b]["scores_ready"], now(i - 1))
                    pe.wait_ge(s[b]["xT_ready"], now(i))
                    for c in range(KC):
                        last = nc.tensor.matmul(g_bank[b][:, 0:EXPERTS], xT[b][:, c, :], gate_w[:, c, :], start=c == 0,
                                                stop=c == KC - 1)
                    last.then_inc(s[b]["g_full"], 1)

        @block.scalar
        def _(act):
            with act.Fori(0, TILES) as i:
                for b in range(NB):
                    act.wait_ge(s[b]["xT_kept"], now(i - 1))
                    act.wait_ge(s[b]["t_full"], now(i))
                    nc.scalar.copy(xT[b][:, :, :].rearrange("p c t -> p (c t)"), t_bank[b][:, 0:D])\
                        .then_inc(s[b]["xT_ready"], 1)
                for b in range(NB):
                    act.wait_ge(s[b]["g_full"], now(i))
                    act.wait_ge(s[b]["comb_ready"], now(i - 1))
                    nc.scalar.activation(scores[b][:, :], g_bank[b][:, 0:EXPERTS], ACT.Sigmoid)\
                        .then_inc(s[b]["scores_ready"], 1)


def moe_experts(nc, ident_dram, w13_dram, w2_dram, h3_all, xT_all, comb_all, out_dram):
    D, EXPERTS, GU = w13_dram.shape
    INTER = GU // 2
    KC = D // P
    NB, T, _ = out_dram.shape
    TILES = T // P
    PAIRS = (EXPERTS + 1) // 2
    STEPS = [(b, p) for b in range(NB) for p in range(PAIRS)]
    G_RING = 3
    G_USES = len(STEPS) // G_RING
    assert len(STEPS) % G_RING == 0 and len(STEPS) % 2 == 0 and INTER == P

    def experts(p):
        return range(2 * p, min(2 * p + 2, EXPERTS))

    with ExitStack() as ctx:
        ctx.enter_context(nc.cleanup_on_exit())
        def sb(name, shape, dt=F32):
            return ctx.enter_context(nc.sbuf_tensor("me_" + name, shape, dt))

        def sem(name):
            return nc.alloc_semaphore("me_" + name)

        def pb(name):
            return ctx.enter_context(nc.psum_tensor("me_bank_" + name, [P, 512], F32))

        ident = sb("ident", [P, P])
        w13 = sb("w13", [P, KC, EXPERTS, GU])
        w2 = sb("w2", [P, EXPERTS, D])
        xT = [sb(f"xT{b}", [P, KC, P]) for b in range(NB)]
        comb = [sb(f"comb{b}", [P, EXPERTS]) for b in range(NB)]
        silu = [sb(f"silu{r}", [P, 2, P]) for r in range(2)]
        hidden = [sb(f"hidden{r}", [P, 2, P]) for r in range(2)]
        hT = [sb(f"hT{r}", [P, 2, P]) for r in range(2)]
        y = [sb(f"y{b}", [P, D]) for b in range(NB)]
        g_bank = [pb(f"g{r}") for r in range(G_RING)]
        t_bank = [pb(f"t{r}") for r in range(2)]
        y_bank = [pb(f"y{b}") for b in range(NB)]
        const_in = sem("const_in")
        g_full, g_drained = [sem(f"g_full{r}") for r in range(G_RING)], [sem(f"g_drained{r}") for r in range(G_RING)]
        t_full, t_drained = [sem(f"t_full{r}") for r in range(2)], [sem(f"t_drained{r}") for r in range(2)]
        silu_ready = [sem(f"silu_ready{r}") for r in range(2)]
        y_full, y_ready = [sem(f"y_full{b}") for b in range(NB)], [sem(f"y_ready{b}") for b in range(NB)]
        xT_copied, comb_copied = [sem(f"xT_copied{b}") for b in range(NB)], [sem(f"comb_copied{b}") for b in range(NB)]
        y_stored = [sem(f"y_stored{b}") for b in range(NB)]
        act_gate, dve_gate, pool_gate, sp_gate = (sem("act_gate"), sem("dve_gate"), sem("pool_gate"), sem("sp_gate"))
        T_USES = len(STEPS) // 2

        def count(per, i, pos):
            return per * (i + 1) + pos + 1

        block = ctx.enter_context(nc.Block())

        @block.sync
        def _(sp):
            for r in range(G_RING):
                sp.sem_inc(g_full[r], G_USES)
                sp.sem_inc(g_drained[r], G_USES)
            for r in range(2):
                for x in (t_full[r], t_drained[r], silu_ready[r]):
                    sp.sem_inc(x, T_USES)
            for b in range(NB):
                for x in (y_full[b], y_ready[b], xT_copied[b], comb_copied[b]):
                    sp.sem_inc(x, 1)
                sp.sem_inc(y_stored[b], 16)
            sp.dma_start(ident[:, :], ident_dram).then_inc(const_in, 16)
            for c in range(KC):
                sp.dma_start(w13[:, c, :, :], w13_dram[c * P:(c + 1) * P, :, :]).then_inc(const_in, 16)
            sp.dma_start(w2[:, :, :], w2_dram).then_inc(const_in, 16)
            with sp.Fori(0, TILES) as i:
                for b in range(NB):
                    sp.wait_ge(y_stored[b], 16 * (i + 1))
                    sp.sem_inc(sp_gate, 1)
                    sp.wait_ge(y_ready[b], count(1, i, 0))
                    sp.sem_inc(sp_gate, 1)
                    sp.dma_start(out_dram[b, bass.ds(i * P, P), :], y[b][:, :]).then_inc(y_stored[b], 16)
            for b in range(NB):
                sp.wait_ge(y_stored[b], 16 * (TILES + 1))

        @block.gpsimd
        def _(pool):
            with pool.Fori(0, TILES) as i:
                for b in range(NB):
                    pool.wait_ge(y_full[b], count(1, i - 1, 0))
                    pool.sem_inc(pool_gate, 1)
                    nc.gpsimd.tensor_copy(xT[b][:, :, :].rearrange("p c t -> p (c t)"),
                                          xT_all[:, bass.ds(b * TILES + i, 1), :, :].rearrange("p a c t -> p (a c t)"))\
                        .then_inc(xT_copied[b], 1)
                    nc.gpsimd.tensor_copy(comb[b][:, :], comb_all[:, bass.ds(b * TILES + i, 1), :]
                                          .rearrange("p a e -> p (a e)")).then_inc(comb_copied[b], 1)

        @block.tensor
        def _(pe):
            def gate_up(i, n):
                b, p = STEPS[n]
                r, pos = n % G_RING, n // G_RING
                if p == 0:
                    pe.wait_ge(xT_copied[b], count(1, i, 0))
                pe.wait_ge(g_drained[r], count(G_USES, i, pos) - 1)
                cols = len(experts(p)) * GU
                for c in range(KC):
                    last = nc.tensor.matmul(g_bank[r][:, 0:cols], xT[b][:, c, :],
                                            w13[:, c, experts(p).start:experts(p).stop, :].rearrange("p e n -> p (e n)"),
                                            start=c == 0, stop=c == KC - 1)
                last.then_inc(g_full[r], 1)

            def turn(i, n):
                b, p = STEPS[n]
                pe.wait_ge(g_drained[n % G_RING], count(G_USES, i, n // G_RING))
                pe.wait_ge(t_drained[n % 2], count(T_USES, i, n // 2) - 1)
                for j in range(len(experts(p))):
                    last = nc.tensor.transpose(t_bank[n % 2][:, j * P:(j + 1) * P], hidden[n % 2][:, j, :], ident[:, :])
                last.then_inc(t_full[n % 2], 1)

            def down(i, n):
                b, p = STEPS[n]
                if p == 0:
                    pe.wait_ge(y_ready[b], count(1, i - 1, 0))
                pe.wait_ge(t_drained[n % 2], count(T_USES, i, n // 2))
                for j, e in enumerate(experts(p)):
                    last = nc.tensor.matmul(y_bank[b][:, 0:D], hT[n % 2][:, j, :], w2[:, e, :], start=e == 0,
                                            stop=e == EXPERTS - 1)
                if p == PAIRS - 1:
                    last.then_inc(y_full[b], 1)

            pe.wait_ge(const_in, 64)
            with pe.Fori(0, TILES) as i:
                for n in range(len(STEPS) + 3):
                    if n < len(STEPS):
                        gate_up(i, n)
                    if 0 <= n - 2 < len(STEPS):
                        turn(i, n - 2)
                    if 0 <= n - 3:
                        down(i, n - 3)

        @block.scalar
        def _(act):
            def gates(i, n):
                b, p = STEPS[n]
                m = len(experts(p))
                before = (i, n - 2) if n >= 2 else (i - 1, n - 2 + len(STEPS))
                act.wait_ge(g_drained[before[1] % G_RING], count(G_USES, before[0], before[1] // G_RING))
                act.wait_ge(g_full[n % G_RING], count(G_USES, i, n // G_RING))
                nc.scalar.activation(silu[n % 2][:, 0:m, :],
                                     g_bank[n % G_RING][:, 0:m * GU].rearrange("p (e g d) -> p e g d", e=m, g=2)[:, :, 0, :],
                                     ACT.Silu).then_inc(silu_ready[n % 2], 1)

            def keep(i, n):
                m = len(experts(STEPS[n][1]))
                act.wait_ge(t_full[n % 2], count(T_USES, i, n // 2))
                nc.scalar.copy(hT[n % 2][:, 0:m, :].rearrange("p e t -> p (e t)"), t_bank[n % 2][:, 0:m * P])\
                    .then_inc(t_drained[n % 2], 1)

            with act.Fori(0, TILES) as i:
                for n in range(len(STEPS) + 2):
                    if n < len(STEPS):
                        gates(i, n)
                    if 0 <= n - 2:
                        keep(i, n - 2)

        @block.vector
        def _(dve):
            def weigh(i, n):
                b, p = STEPS[n]
                if p == 0:
                    dve.wait_ge(comb_copied[b], count(1, i, 0))
                before = (i, n - 2) if n >= 2 else (i - 1, n - 2 + len(STEPS))
                dve.wait_ge(t_full[n % 2], count(T_USES, before[0], before[1] // 2))
                dve.wait_ge(silu_ready[n % 2], count(T_USES, i, n // 2))
                for j, e in enumerate(experts(p)):
                    last = nc.vector.scalar_tensor_tensor(
                        hidden[n % 2][:, j, :], g_bank[n % G_RING][:, j * GU + INTER:(j + 1) * GU], comb[b][:, e:e + 1],
                        silu[n % 2][:, j, :], ALU.mult, ALU.mult)
                last.then_inc(g_drained[n % G_RING], 1)

            def residual(i, b):
                dve.wait_ge(y_stored[b], 16 * (i + 1))
                dve.wait_ge(y_full[b], count(1, i, 0))
                nc.vector.tensor_tensor(y[b][:, :], y_bank[b][:, 0:D],
                                        h3_all[:, bass.ds(b * TILES + i, 1), :].rearrange("p a d -> p (a d)"), ALU.add)\
                    .then_inc(y_ready[b], 1)

            with dve.Fori(0, TILES) as i:
                for n in range(len(STEPS)):
                    weigh(i, n)
                    if n == PAIRS + 4:
                        residual(i, 0)
                residual(i, 1)


def moe_stage(nc, ident, gate_w, gate_b, w13, w2, h3_dram, out_dram):
    TILES = h3_dram.shape[0] * h3_dram.shape[1] // P
    with ExitStack() as ctx:
        h3_all = ctx.enter_context(nc.sbuf_tensor("h3_all", [P, TILES, 256], F32))
        xT_all = ctx.enter_context(nc.sbuf_tensor("xT_all", [P, TILES, 2, P], F32))
        comb_all = ctx.enter_context(nc.sbuf_tensor("comb_all", [P, TILES, 17], F32))
        moe_route(nc, ident, h3_dram, gate_w, gate_b, h3_all, xT_all, comb_all)
        moe_experts(nc, ident, w13, w2, h3_all, xT_all, comb_all, out_dram)


def zero_rows(nc, h_versions):
    LAYERS, NB, _, D = h_versions.shape
    with ExitStack() as ctx:
        ctx.enter_context(nc.cleanup_on_exit())
        zeros = ctx.enter_context(nc.sbuf_tensor("zero_row", [1, LAYERS * NB * D], F32))
        filled = nc.alloc_semaphore("zero_filled")
        stored = nc.alloc_semaphore("zero_stored")
        block = ctx.enter_context(nc.Block())

        @block.vector
        def _(dve):
            nc.vector.memset(zeros[:, :], 0.0).then_inc(filled, 1)

        @block.sync
        def _(sp):
            sp.wait_ge(filled, 1)
            sp.dma_start(h_versions[:, :, 0:1, :].rearrange("l b t d -> t (l b) d"),
                         zeros[:, :].rearrange("p (a d) -> p a d", d=D)).then_inc(stored, 16)
            sp.wait_ge(stored, 16)


def program(nc, a, out):
    NB, T, D = out.shape
    LAYERS = a["ffn_wqkv"].shape[0]
    h1 = nc.dram_tensor("h1_rows", (NB, T, D), F32).ap()
    h3 = nc.dram_tensor("h3_rows", (NB, T, D), F32).ap()
    h_versions = nc.dram_tensor("tower_rows", (LAYERS + 1, NB, T + 1, D), F32).ap()
    zero_rows(nc, h_versions)
    mla_stage(nc, a["ids"], a["embedding"], a["ident"], a["rope"], a["causal"], a["mla_w_x"], a["mla_g_kv"],
              a["mla_w_kvdec"], a["mla_w_q"], a["mla_w_o"], h1, h_versions[0, :, 1:T + 1, :])
    local_tower(nc, a["ident"], a["trig"], a["band"], a["shift"], h_versions, a["qk_scale"], a["ffn_wqkv"],
                a["ffn_wo"], a["ffn_ln_g"], a["ffn_ln_b"], a["ffn_w1"], a["ffn_b1"], a["ffn_w2"], a["ffn_b2"])
    gla_stage(nc, a["ident"], a["spans"], a["after"], a["pairs"], a["gla_wqk"], a["gla_wk"], a["gla_wv"],
              a["gla_wg"], a["gla_gk1"], a["gla_gk2"], a["gla_gkb"], a["gla_norm"], a["gla_wo"], h1,
              h_versions[LAYERS, :, 1:T + 1, :], h3)
    moe_stage(nc, a["ident"], a["gate_w"], a["gate_b"], a["w13"], a["w2"], h3, out)


def kernel(x, L0_tok_embedding, L0_attn_W_kv, L0_attn_g_kv, L0_attn_W_kdec, L0_attn_W_vdec, L0_attn_W_q,
           L0_attn_W_qdec, L0_attn_W_krope, L0_attn_W_qrope, L0_attn_W_o, L0_ffn_Wqkv, L0_ffn_q_scale, L0_ffn_k_scale,
           L0_ffn_Wo, L0_ffn_ln_g, L0_ffn_ln_b, L0_ffn_W1, L0_ffn_b1, L0_ffn_W2, L0_ffn_b2, L1_attn_Wq, L1_attn_Wk,
           L1_attn_Wv, L1_attn_Wg, L1_attn_gk_w1, L1_attn_gk_w2, L1_attn_gk_b2, L1_attn_g_norm_w, L1_attn_Wo,
           L1_ffn_input_ids, L1_ffn_gate_w, L1_ffn_gate_b, L1_ffn_w13, L1_ffn_w2, L1_ffn_w13_s, L1_ffn_w2_s):
    import concourse.bacc as bacc
    import numpy as np
    from concourse.bass_utils import run_bass_kernel_spmd

    host = np.asarray
    NB, T = x.shape
    D = L0_tok_embedding.shape[1]
    ident, trig, band, shift = tower_consts(T // P)
    rope, causal = mla_consts(T)
    spans, after, pairs = gla_consts()
    a = dict(
        ident=ident, trig=trig, band=band, shift=shift, rope=rope, causal=causal, spans=spans, after=after,
        pairs=pairs,
        ids=host(x).reshape(NB * T // P, P).T,
        embedding=host(L0_tok_embedding),
        mla_w_x=np.concatenate([host(L0_attn_W_krope), host(L0_attn_W_kv), host(L0_attn_W_q)], 1),
        mla_g_kv=host(L0_attn_g_kv),
        mla_w_kvdec=np.concatenate([host(L0_attn_W_kdec), host(L0_attn_W_vdec)], 1),
        mla_w_q=np.concatenate([host(L0_attn_W_qrope), host(L0_attn_W_qdec)], 1),
        mla_w_o=host(L0_attn_W_o),
        qk_scale=np.stack([host(L0_ffn_q_scale), host(L0_ffn_k_scale)], 1),
        ffn_wqkv=host(L0_ffn_Wqkv), ffn_wo=host(L0_ffn_Wo), ffn_ln_g=host(L0_ffn_ln_g), ffn_ln_b=host(L0_ffn_ln_b),
        ffn_w1=host(L0_ffn_W1), ffn_b1=host(L0_ffn_b1), ffn_w2=host(L0_ffn_W2), ffn_b2=host(L0_ffn_b2),
        gla_wqk=np.concatenate([host(L1_attn_Wq), host(L1_attn_Wk)], 1),
        gla_wk=host(L1_attn_Wk), gla_wv=host(L1_attn_Wv), gla_wg=host(L1_attn_Wg), gla_gk1=host(L1_attn_gk_w1),
        gla_gk2=host(L1_attn_gk_w2), gla_gkb=host(L1_attn_gk_b2), gla_norm=host(L1_attn_g_norm_w),
        gla_wo=host(L1_attn_Wo),
        gate_w=host(L1_ffn_gate_w).T, gate_b=host(L1_ffn_gate_b),
        w13=np.concatenate([host(L1_ffn_w13), host(L1_ffn_w13_s)[None]]).transpose(2, 0, 1),
        w2=np.concatenate([host(L1_ffn_w2), host(L1_ffn_w2_s)[None]]).transpose(2, 0, 1),
    )
    a = {n: np.ascontiguousarray(v) for n, v in a.items()}

    nc = bacc.Bacc("TRN2", target_bir_lowering=False, num_devices=1)
    aps = {n: nc.dram_tensor("in_" + n, v.shape, mybir.dt.int32 if n in ("ids", "pairs") else F32,
                             kind="ExternalInput").ap() for n, v in a.items()}
    out = nc.dram_tensor("out_0", (NB, T, D), F32, kind="ExternalOutput").ap()
    program(nc, aps, out)
    result = run_bass_kernel_spmd(nc, [{"in_" + n: v for n, v in a.items()}], core_ids=[0])
    return result.results[0]["out_0"]
```

```python
from contextlib import ExitStack

import concourse.bass as bass
from concourse import mybir

F32 = mybir.dt.float32
ALU = mybir.AluOpType
ACT = mybir.ActivationFunctionType
AX = mybir.AxisListType.X
P = 128


def tower_consts(TILES):
    import numpy as np
    P, HD, WIN = 128, 64, 64
    T = TILES * P
    f32 = np.float32
    half = np.arange(0, HD, 2, dtype=f32)
    inv_freq = (f32(1.0) / np.power(f32(10000.0), half / f32(HD))).astype(f32)
    t = np.arange(T, dtype=f32)
    freqs = t[:, None] * inv_freq[None, :]
    freqs = np.concatenate([freqs, freqs], -1)
    base = (half + f32(0.4 * HD)) / f32(1.4 * HD)
    power = (t - T // 2) / f32(WIN // 2)
    scale = np.power(base[None, :], power[:, None]).astype(f32)
    scale = np.concatenate([scale, scale], -1)
    inv = (f32(1.0) / scale).astype(f32)
    sign = np.where(np.arange(HD) < HD // 2, -1.0, 1.0).astype(f32)
    cos, sin = np.cos(freqs), np.sin(freqs) * sign
    QK_SCALE = 8.0
    trig = np.stack([np.stack([cos * scale * QK_SCALE, sin * scale * QK_SCALE], 1), np.stack([cos * inv, sin * inv], 1)], 1)
    trig = trig.reshape(TILES, P, 4 * HD).astype(f32)
    i = np.arange(P)[:, None]
    c = np.arange(WIN + P)[None, :]
    ok = (i <= c) & (c <= i + WIN)
    mask = np.repeat(np.where(ok, 0.0, -1e30)[None], TILES, 0)
    mask[0, :, :WIN] = -1e30
    before, own = mask[:, :, :WIN], mask[:, :, WIN:]
    keep = np.ones((TILES, P, 1))
    keep[TILES - 1] = 0.0
    band = np.concatenate([own, before, before, own, keep], -1).astype(f32)
    ident = np.eye(P, dtype=f32)
    shift = np.zeros((2, P, P), f32)
    shift[0, np.arange(P - 1), np.arange(1, P)] = 1.0
    shift[1, P - 1, 0] = 1.0
    return ident, trig, band, shift


def mla_consts(T):
    import numpy as np
    f32 = np.float32
    dim = 32
    inv_freq = 1.0 / 10000.0 ** (np.arange(0, dim, 2, dtype=f32) / dim)
    freqs = np.outer(np.arange(T, dtype=f32), inv_freq)
    emb = np.concatenate([freqs, freqs], -1)
    sign = np.where(np.arange(dim) < dim // 2, -1.0, 1.0).astype(f32)
    rope = np.stack([np.cos(emb), np.sin(emb) * sign], 1).astype(f32)
    causal = np.where(np.arange(128)[None, :] <= np.arange(128)[:, None], 0.0, -1e30).astype(f32)
    return rope, causal


def mla_project(nc, ids_dram, emb_dram, ident_dram, rope_dram, w_x_dram, g_kv_dram, w_kvdec_dram, w_q_dram,
                emb, qT_all, kT_all, v_all):
    VOCAB, D = emb_dram.shape
    KC = D // P
    RANK = w_kvdec_dram.shape[0]
    QRANK = w_q_dram.shape[0]
    HEADS, CONT, ROPE, SLOT = 16, 16, 32, 64
    RH = ROPE // 2
    PAIRS = HEADS // 2
    KR = HEADS * ROPE
    HC = HEADS * CONT
    NB = 2
    TILES = ids_dram.shape[1] // NB
    VD = CONT + 1

    with ExitStack() as ctx:
        ctx.enter_context(nc.cleanup_on_exit())
        def sb(name, shape, dt=F32):
            return ctx.enter_context(nc.sbuf_tensor("mp_" + name, shape, dt))

        def sem(name):
            return nc.alloc_semaphore("mp_" + name)

        bank = [ctx.enter_context(nc.psum_tensor(f"mp_bank{j}", [P, 512], F32)) for j in range(8)]
        ident = sb("ident", [P, P])
        rope = sb("rope", [P, TILES, 2, ROPE])
        w_x = sb("w_x", [P, KC, KR + RANK + QRANK])
        w_kvdec = sb("w_kvdec", [RANK, 2 * HC])
        w_q = sb("w_q", [P, KR + HC])
        g_kv = sb("g_kv", [P, RANK])
        minus_half = sb("minus_half", [P, 1])
        ids = sb("ids", [P, NB * TILES], mybir.dt.int32)
        idsf = sb("idsf", [P, NB * TILES])
        below = sb("below", [P, NB * TILES])
        rows = sb("rows", [P, NB * TILES], mybir.dt.int32)
        stats = [sb(f"stats{b}", [P, 6]) for b in range(NB)]
        mv = [sb(f"mv{b}", [P, 2]) for b in range(NB)]
        ve = [sb(f"ve{b}", [P, 1]) for b in range(NB)]
        rstd = [sb(f"rstd{b}", [P, 1]) for b in range(NB)]
        xn = [sb(f"xn{b}", [P, D]) for b in range(NB)]
        xT = [sb(f"xT{b}", [P, KC, P]) for b in range(NB)]
        sq = [sb(f"sq{b}", [P, RANK]) for b in range(NB)]
        ssum = [sb(f"ssum{b}", [P, 1]) for b in range(NB)]
        ms = [sb(f"ms{b}", [P, 1]) for b in range(NB)]
        rms = [sb(f"rms{b}", [P, 1]) for b in range(NB)]
        comp = [sb(f"comp{b}", [P, RANK + QRANK]) for b in range(NB)]
        compT = [sb(f"compT{b}", [P, 2, P]) for b in range(NB)]
        packed = [sb(f"packed{b}", [P, 2, HEADS, SLOT]) for b in range(NB)]
        cross = sb("cross", [P, 2, HEADS, ROPE])

        USES = [2, 1, 1, 1, 1, 1, 2, 2]
        full = [sem(f"full{j}") for j in range(8)]
        drained = [sem(f"drained{j}") for j in range(8)]
        const_in, ready, ids_in, rows_ready, gathered = (sem("const_in"), sem("ready"), sem("ids_in"),
                                                         sem("rows_ready"), sem("gathered"))
        ONES = ["stats_ready", "mv_ready", "ve_ready", "rstd_ready", "xn_ready", "squared", "ms_ready", "rms_ready",
                "comp_ready"]
        s = {n: sem(n) for n in ONES}
        TWOS = ["crossed", "straight", "packed_ready"]
        s.update({n: sem(n) for n in TWOS})
        id_step, act_gate, dve_gate = sem("id_step"), sem("act_gate"), sem("dve_gate")

        def nth(per, k, pos=0):
            return per * (k + 2) + pos + 1

        def in0(i, use):
            return 4 * (i + 1) + use + 1

        block = ctx.enter_context(nc.Block())

        @block.sync
        def _(sp):
            for j in range(8):
                sp.sem_inc(full[j], 2 * USES[j])
                sp.sem_inc(drained[j], 2 * USES[j])
            for n in ONES:
                sp.sem_inc(s[n], 2)
            for n in TWOS:
                sp.sem_inc(s[n], 4)
            sp.dma_start(ids[:, :], ids_dram).then_inc(ids_in, 16)
            for dst, src in ((ident[:, :], ident_dram),
                             (rope[:, :, :, :], rope_dram.rearrange("(i p) a d -> p i a d", p=P)),
                             (w_x[:, :, :], w_x_dram.rearrange("(c p) n -> p c n", p=P)),
                             (w_kvdec[:, :], w_kvdec_dram), (w_q[:, :], w_q_dram),
                             (g_kv[:, :], g_kv_dram.partition_broadcast(P))):
                sp.dma_start(dst, src).then_inc(const_in, 16)

        @block.vector
        def _(dve):
            nc.vector.memset(minus_half[:, :], -0.5)
            nc.vector.memset(v_all[:, :, :, :], 1.0)
            for b in range(NB):
                nc.vector.memset(packed[b][:, :, :, :], 0.0)
            nc.vector.memset(emb[:, :, :], 0.0).then_inc(ready, 1)
            dve.wait_ge(ids_in, 16)
            nc.vector.tensor_copy(idsf[:, :], ids[:, :]).then_inc(id_step, 1)
            dve.wait_ge(id_step, 1)
            nc.vector.tensor_scalar(idsf[:, :], idsf[:, :], float(VOCAB), -1.0, ALU.min, ALU.max).then_inc(id_step, 1)
            dve.wait_ge(id_step, 2)
            nc.vector.tensor_scalar(below[:, :], idsf[:, :], 0.0, float(VOCAB + 1), ALU.is_lt, ALU.mult)\
                .then_inc(id_step, 1)
            dve.wait_ge(id_step, 3)
            nc.vector.tensor_tensor(rows[:, :], idsf[:, :], below[:, :], ALU.add).then_inc(rows_ready, 1)
            dve.wait_ge(const_in, 96)
            dve.wait_ge(gathered, 16 * NB * TILES)

            def norms(i):
                src = [emb[:, bass.ds(b * TILES + i, 1), :].rearrange("p a d -> p (a d)") for b in range(NB)]
                for b in range(NB):
                    nc.vector.bn_stats(stats[b][:, :], src[b]).then_inc(s["stats_ready"], 1)
                for b in range(NB):
                    dve.wait_ge(s["stats_ready"], nth(1, 2 * i + b))
                    dve.sem_inc(dve_gate, 1)
                    nc.vector.bn_aggr(mv[b][:, :], stats[b][:, :]).then_inc(s["mv_ready"], 1)
                for b in range(NB):
                    dve.wait_ge(s["mv_ready"], nth(1, 2 * i + b))
                    nc.vector.tensor_scalar(ve[b][:, :], mv[b][:, 1:2], 1e-5, None, ALU.add).then_inc(s["ve_ready"], 1)
                for b in range(NB):
                    dve.wait_ge(s["rstd_ready"], nth(1, 2 * i + b))
                    dve.wait_ge(full[0], in0(i - 1, b))
                    dve.sem_inc(dve_gate, 1)
                    nc.vector.tensor_scalar(xn[b][:, :], src[b], mv[b][:, 0:1], rstd[b][:, :], ALU.subtract, ALU.mult)\
                        .then_inc(s["xn_ready"], 1)

            def compress(i, b):
                k = 2 * i + b
                dve.wait_ge(s["squared"], nth(1, k))
                nc.vector.tensor_scalar(ms[b][:, :], ssum[b][:, :], 1.0 / RANK, 1e-6, ALU.mult, ALU.add)\
                    .then_inc(s["ms_ready"], 1)
                dve.wait_ge(s["rms_ready"], nth(1, k))
                dve.wait_ge(full[0], in0(i - 1, 2 + b))
                nc.vector.scalar_tensor_tensor(comp[b][:, 0:RANK], bank[2][:, 0:RANK], rms[b][:, :], g_kv[:, :],
                                               ALU.mult, ALU.mult)
                nc.vector.tensor_copy(comp[b][:, RANK:RANK + QRANK], bank[2][:, RANK:RANK + QRANK])\
                    .then_inc(drained[2], 1)

            def rotate(i, b, h):
                k = 2 * i + b
                j = (4, 1)[h]
                src = bank[j][:, :].rearrange("p (n d) -> p n d", d=ROPE)
                dve.wait_ge(full[6 + h], nth(2, k - 2, 1))
                dve.wait_ge(s["packed_ready"], nth(2, k, 0 if h == 1 else 1) - 1)
                dve.wait_ge(full[j], nth(1, k))
                dve.sem_inc(dve_gate, 1)
                cos = rope[:, bass.ds(i, 1), 0, :].to_broadcast([P, HEADS, ROPE])
                nc.vector.tensor_tensor(packed[b][:, h, :, CONT:CONT + ROPE], src, cos, ALU.mult)\
                    .then_inc(s["straight"], 1)
                for first, other in ((0, RH), (RH, 0)):
                    sin = rope[:, bass.ds(i, 1), 1, first:first + RH].to_broadcast([P, HEADS, RH])
                    last = nc.vector.tensor_tensor(cross[:, h, :, first:first + RH], src[:, :, other:other + RH], sin,
                                                   ALU.mult)
                last.then_inc(drained[j], 1)
                dve.wait_ge(drained[j], nth(1, k))
                nc.vector.tensor_tensor(packed[b][:, h, :, CONT:CONT + ROPE], packed[b][:, h, :, CONT:CONT + ROPE],
                                        cross[:, h, :, :], ALU.add).then_inc(s["packed_ready"], 1)

            def keep_kT(i, b):
                for g in range(2):
                    dve.wait_ge(full[7], nth(2, 2 * i + b, g))
                    dve.sem_inc(dve_gate, 1)
                    nc.vector.tensor_copy(kT_all[:, b * PAIRS + 4 * g:b * PAIRS + 4 * g + 4, bass.ds(i * P, P)],
                                          bank[7][:, :].rearrange("p (n t) -> p n t", t=P)).then_inc(drained[7], 1)

            def tiles(i, following):
                compress(i, 0)
                rotate(i, 0, 1)
                compress(i, 1)
                rotate(i, 0, 0)
                keep_kT(i, 0)
                rotate(i, 1, 1)
                if following is not None:
                    norms(following)
                rotate(i, 1, 0)
                keep_kT(i, 1)

            norms(0)
            with dve.Fori(0, TILES - 1) as i:
                tiles(i, i + 1)
            tiles(TILES - 1, None)

        @block.gpsimd
        def _(pool):
            pool.wait_ge(ready, 1)
            pool.wait_ge(rows_ready, 1)
            for g in range(NB * TILES):
                pool.indirect_dma_start(
                    out=emb[:, g, :], out_offset=None, in_=emb_dram,
                    in_offset=bass.IndirectOffsetOnAxis(ap=rows[:, g:g + 1].bitcast(mybir.dt.uint32), axis=0),
                    bounds_check=VOCAB - 1, oob_is_err=False).then_inc(gathered, 16)
            def root(i, b, ready, x, done, y):
                pool.wait_ge(ready, nth(1, 2 * i + b))
                nc.gpsimd.tensor_tensor(y[b][:, :], x[b][:, :], minus_half[:, :], ALU.pow).then_inc(done, 1)

            def tiles(i, following):
                for b in range(NB):
                    root(i, b, s["ms_ready"], ms, s["rms_ready"], rms)
                if following is not None:
                    for b in range(NB):
                        root(following, b, s["ve_ready"], ve, s["rstd_ready"], rstd)

            for b in range(NB):
                root(0, b, s["ve_ready"], ve, s["rstd_ready"], rstd)
            with pool.Fori(0, TILES - 1) as i:
                tiles(i, i + 1)
            tiles(TILES - 1, None)

        @block.tensor
        def _(pe):
            def mm(out, lhsT, rhs, start, stop):
                return nc.tensor.matmul(out, lhsT, rhs, start=start, stop=stop)

            pe.wait_ge(const_in, 96)
            def turn_input(i, b):
                pe.wait_ge(s["xn_ready"], nth(1, 2 * i + b))
                pe.wait_ge(drained[0], in0(i, b) - 1)
                for c in range(KC):
                    last = nc.tensor.transpose(bank[0][:, c * P:(c + 1) * P], xn[b][:, c * P:(c + 1) * P], ident[:, :])
                last.then_inc(full[0], 1)

            def project(i, b, j, cols):
                k = 2 * i + b
                pe.wait_ge(drained[0], in0(i, b))
                pe.wait_ge(drained[j], nth(1, k - 1))
                for c in range(KC):
                    last = mm(bank[j][:, 0:cols.stop - cols.start], xT[b][:, c, :], w_x[:, c, cols], c == 0,
                              c == KC - 1)
                last.then_inc(full[j], 1)

            def turn_compressed(i, b):
                pe.wait_ge(drained[2], nth(1, 2 * i + b))
                pe.wait_ge(drained[0], in0(i, 2 + b) - 1)
                nc.tensor.transpose(bank[0][:, P:2 * P], comp[b][:, RANK:RANK + QRANK], ident[:, :])
                nc.tensor.transpose(bank[0][0:RANK, 0:P], comp[b][:, 0:RANK], ident[:, :]).then_inc(full[0], 1)

            def decompress(i, b):
                k = 2 * i + b
                pe.wait_ge(drained[0], in0(i, 2 + b))
                for j, x, w in ((3, compT[b][0:RANK, 0, :], w_kvdec[:, :]), (4, compT[b][:, 1, :], w_q[:, 0:KR]),
                                (5, compT[b][:, 1, :], w_q[:, KR:KR + HC])):
                    pe.wait_ge(drained[j], nth(1, k - 1))
                    mm(bank[j][:, 0:w.shape[1]], x, w, True, True).then_inc(full[j], 1)

            def turn_packed(i, b, h, content, pos):
                k = 2 * i + b
                pe.wait_ge(s["packed_ready"], nth(2, k, pos))
                pe.wait_ge(drained[content], nth(1, k))
                for g in range(2):
                    pe.wait_ge(drained[6 + h], nth(2, k, g) - 1)
                    for n in range(4):
                        a = 2 * (4 * g + n)
                        last = nc.tensor.transpose(bank[6 + h][:, n * P:(n + 1) * P],
                                                   packed[b][:, h, a:a + 2, :].rearrange("p n d -> p (n d)"),
                                                   ident[:, :])
                    last.then_inc(full[6 + h], 1)

            compressed, rotary = slice(KR, KR + RANK + QRANK), slice(0, KR)
            with pe.Fori(0, TILES) as i:
                turn_input(i, 0)
                turn_input(i, 1)
                project(i, 0, 2, compressed)
                project(i, 0, 1, rotary)
                project(i, 1, 2, compressed)
                turn_compressed(i, 0)
                decompress(i, 0)
                turn_compressed(i, 1)
                project(i, 1, 1, rotary)
                turn_packed(i, 0, 1, 3, 0)
                decompress(i, 1)
                turn_packed(i, 0, 0, 5, 1)
                turn_packed(i, 1, 1, 3, 0)
                turn_packed(i, 1, 0, 5, 1)

        @block.scalar
        def _(act):
            act.wait_ge(ready, 1)
            with act.Fori(0, TILES) as i:
                for b in range(NB):
                    act.wait_ge(full[0], in0(i, b))
                    nc.scalar.copy(xT[b][:, :, :].rearrange("p c t -> p (c t)"), bank[0][:, 0:KC * P])\
                        .then_inc(drained[0], 1)
                for b in range(NB):
                    act.wait_ge(full[2], nth(1, 2 * i + b))
                    nc.scalar.activation(sq[b][:, :], bank[2][:, 0:RANK], ACT.Square, accum_out=ssum[b][:, :])\
                        .then_inc(s["squared"], 1)
                for b in range(NB):
                    act.wait_ge(full[0], in0(i, 2 + b))
                    nc.scalar.copy(compT[b][0:RANK, 0, :], bank[0][0:RANK, 0:P])
                    nc.scalar.copy(compT[b][:, 1, :], bank[0][:, P:2 * P]).then_inc(drained[0], 1)
                for b in range(NB):
                    k = 2 * i + b
                    act.wait_ge(full[3], nth(1, k))
                    act.wait_ge(full[7], nth(2, k - 2, 1))
                    act.sem_inc(act_gate, 1)
                    nc.scalar.copy(packed[b][:, 1, :, 0:CONT], bank[3][:, 0:HC].rearrange("p (n d) -> p n d", d=CONT))
                    values = v_all[:, b * PAIRS:(b + 1) * PAIRS, bass.ds(i, 1), :]\
                        .rearrange("p n a (e d) -> p (n a) e d", d=VD)
                    nc.scalar.copy(values[:, :, :, 0:CONT],
                                   bank[3][:, HC:2 * HC].rearrange("p (n e d) -> p n e d", e=2, d=CONT))\
                        .then_inc(drained[3], 1)
                    act.wait_ge(full[5], nth(1, k))
                    act.wait_ge(full[6], nth(2, k - 2, 1))
                    nc.scalar.copy(packed[b][:, 0, :, 0:CONT], bank[5][:, 0:HC].rearrange("p (n d) -> p n d", d=CONT))\
                        .then_inc(drained[5], 1)
                    for g in range(2):
                        act.wait_ge(full[6], nth(2, k, g))
                        act.sem_inc(act_gate, 1)
                        nc.scalar.copy(qT_all[:, b * PAIRS + 4 * g:b * PAIRS + 4 * g + 4, bass.ds(i * P, P)],
                                       bank[6][:, :].rearrange("p (n t) -> p n t", t=P)).then_inc(drained[6], 1)


def mla_attend(nc, ident_dram, causal_dram, qT_all, kT_all, v_all, o_all):
    PAIRS, T = qT_all.shape[1] // 2, qT_all.shape[2]
    ITERS = 2 * PAIRS
    TILES = T // P
    HALF_T = T // 2
    VD = v_all.shape[3] // 2
    CONT = VD - 1
    D = o_all.shape[2]
    SCALE = 48 ** -0.5
    UNITS = 2 * TILES

    with ExitStack() as ctx:
        ctx.enter_context(nc.cleanup_on_exit())
        def sb(name, shape, dt=F32):
            return ctx.enter_context(nc.sbuf_tensor("ma_" + name, shape, dt))

        def sem(name):
            return nc.alloc_semaphore("ma_" + name)

        ident = sb("ident", [P, P])
        causal = sb("causal", [P, P])
        qz = [sb(f"qz{e}", [P, T]) for e in range(2)]
        mx = [sb(f"mx{e}", [P, 1]) for e in range(2)]
        bias = [sb(f"bias{e}", [P, 1]) for e in range(2)]
        probs = [sb(f"probs{e}", [P, T]) for e in range(2)]
        pT = [sb(f"pT{j}", [P, 4, P]) for j in range(4)]
        rec = sb("rec", [P, 2])
        s_bank = [ctx.enter_context(nc.psum_tensor(f"ma_s{e}", [P, T], F32)) for e in range(2)]
        t_bank = [ctx.enter_context(nc.psum_tensor(f"ma_t{j}", [P, 512], F32)) for j in range(2)]
        o_bank = [ctx.enter_context(nc.psum_tensor(f"ma_o{j}", [P, 512], F32)) for j in range(2)]

        const_in, zeroed = sem("const_in"), sem("zeroed")
        q_in = [sem(f"q_in{j}") for j in range(2)]
        s_full, exp_done = [sem(f"s_full{e}") for e in range(2)], [sem(f"exp_done{e}") for e in range(2)]
        masked, mx_ready, bias_ready = ([sem(f"masked{e}") for e in range(2)], [sem(f"mx_ready{e}") for e in range(2)],
                                        [sem(f"bias_ready{e}") for e in range(2)])
        t_full, t_drained = [sem(f"t_full{j}") for j in range(2)], [sem(f"t_drained{j}") for j in range(2)]
        o_full, o_drained = [sem(f"o_full{j}") for j in range(2)], [sem(f"o_drained{j}") for j in range(2)]
        o_ready, rec_ready = sem("o_ready"), sem("rec_ready")
        dve_gate, sp_gate = sem("dve_gate"), sem("sp_gate")

        ORDER = [t for n in range(TILES // 2) for t in (n, TILES - 1 - n)]
        GROUPS = []
        for unit in range(UNITS):
            tiles = ORDER[unit // 2] + 1
            for first in range(0, tiles, 4):
                GROUPS.append((unit, first, min(4, tiles - first)))
        IN_BANK = len(GROUPS) // 2
        assert len(GROUPS) % 4 == 0
        OB = TILES // 2

        def count(per, it, pos):
            return per * (it + 1) + pos + 1

        def within(it):
            if isinstance(it, int):
                return it
            return nc.s_assert_within(it, 0, ITERS - 1, skip_runtime_bounds_check_because="a pair's number")

        def ahead(it, following, unit, do):
            if unit + 2 < UNITS:
                do(it, unit + 2)
            elif following is not None:
                do(following, unit + 2 - UNITS)

        def groups_of(unit):
            return [g for g, (u, _, _) in enumerate(GROUPS) if u == unit]

        block = ctx.enter_context(nc.Block())

        @block.sync
        def _(sp):
            for e in range(2):
                for s in (s_full[e], exp_done[e], masked[e], mx_ready[e], bias_ready[e]):
                    sp.sem_inc(s, TILES)
                for s in (t_full[e], t_drained[e]):
                    sp.sem_inc(s, IN_BANK)
                for s in (o_full[e], o_drained[e]):
                    sp.sem_inc(s, OB)
            sp.sem_inc(rec_ready, TILES)
            sp.dma_start(ident[:, :], ident_dram).then_inc(const_in, 16)
            sp.dma_start(causal[:, :], causal_dram).then_inc(const_in, 16)
            sp.wait_ge(zeroed, 1)
            with sp.Fori(0, ITERS) as it:
                for j in range(2):
                    for e in range(2):
                        sp.wait_ge(s_full[e], count(TILES, it - 1, TILES - 2 + j))
                    sp.sem_inc(sp_gate, 1)
                    for e in range(2):
                        rows = slice(64 * e, 64 * e + 64)
                        sp.dma_start(qz[e][rows, j * HALF_T:(j + 1) * HALF_T],
                                     qT_all[rows, bass.ds(it, 1), j * HALF_T:(j + 1) * HALF_T]
                                     .rearrange("p a t -> p (a t)")).then_inc(q_in[j], 16)
            for j in range(2):
                sp.wait_ge(q_in[j], 32 * ITERS)

        @block.tensor
        def _(pe):
            def scores(it, unit):
                step, e = unit // 2, unit % 2
                qt = ORDER[step]
                if e == 0 and step < 2:
                    pe.wait_ge(q_in[step], 32 * (it + 1))
                pe.wait_ge(exp_done[e], count(TILES, it, step) - 1)
                for first in range(0, (qt + 1) * P, 512):
                    n = min(512, (qt + 1) * P - first)
                    last = nc.tensor.matmul(s_bank[e][:, first:first + n], qz[e][:, qt * P:(qt + 1) * P],
                                            kT_all[:, bass.ds(within(it), 1), first:first + n].rearrange("p a t -> p (a t)"),
                                            start=True, stop=True)
                last.then_inc(s_full[e], 1)

            def transpose_probs(it, unit):
                step, e = unit // 2, unit % 2
                qt = ORDER[step]
                pe.wait_ge(exp_done[e], count(TILES, it, step))
                for g in groups_of(unit):
                    _, first, n = GROUPS[g]
                    pe.wait_ge(t_drained[g % 2], count(IN_BANK, it, g // 2) - 1)
                    for a in range(n):
                        last = nc.tensor.transpose(t_bank[g % 2][:, a * P:(a + 1) * P],
                                                   probs[e][:, (first + a) * P:(first + a + 1) * P], ident[:, :])
                    last.then_inc(t_full[g % 2], 1)

            def weigh(it, unit):
                step, e = unit // 2, unit % 2
                qt = ORDER[step]
                if e == 0:
                    pe.wait_ge(o_drained[step % 2], count(OB, it, step // 2) - 1)
                for g in groups_of(unit):
                    _, first, n = GROUPS[g]
                    pe.wait_ge(t_drained[g % 2], count(IN_BANK, it, g // 2))
                    for a in range(n):
                        kt = first + a
                        last = nc.tensor.matmul(o_bank[step % 2][:, e * VD:(e + 1) * VD], pT[g % 4][:, a, :],
                                                v_all[:, bass.ds(within(it), 1), kt, e * VD:(e + 1) * VD]
                                                .rearrange("p a d -> p (a d)"), start=kt == 0, stop=kt == qt)
                if e == 1:
                    last.then_inc(o_full[step % 2], 1)

            def pair(it, following):
                for unit in range(UNITS):
                    ahead(it, following, unit, scores)
                    transpose_probs(it, unit)
                    if unit:
                        weigh(it, unit - 1)
                weigh(it, UNITS - 1)

            pe.wait_ge(const_in, 32)
            scores(0, 0)
            scores(0, 1)
            with pe.Fori(0, ITERS - 1) as it:
                pair(it, it + 1)
            pair(ITERS - 1, None)

        @block.vector
        def _(dve):
            def stats(it, unit):
                step, e = unit // 2, unit % 2
                qt = ORDER[step]
                own = s_bank[e][:, qt * P:(qt + 1) * P]
                dve.wait_ge(s_full[e], count(TILES, it, step))
                nc.vector.tensor_tensor(own, own, causal[:, :], ALU.add).then_inc(masked[e], 1)
                dve.wait_ge(masked[e], count(TILES, it, step))
                nc.vector.tensor_reduce(mx[e][:, :], s_bank[e][:, 0:(qt + 1) * P], AX, ALU.max).then_inc(mx_ready[e], 1)
                dve.wait_ge(exp_done[e], count(TILES, it, step) - 1)
                dve.wait_ge(mx_ready[e], count(TILES, it, step))
                nc.vector.tensor_scalar(bias[e][:, :], mx[e][:, :], -SCALE, None, ALU.mult).then_inc(bias_ready[e], 1)

            nc.vector.memset(qz[0][:, :], 0.0)
            nc.vector.memset(qz[1][:, :], 0.0).then_inc(zeroed, 1)
            dve.wait_ge(const_in, 32)
            def keep_o(it, step):
                qt = ORDER[step]
                got = o_bank[step % 2][:, 0:2 * VD].rearrange("p (e d) -> p e d", d=VD)
                before = (it, step - 1) if step else (it - 1, TILES - 1)
                dve.wait_ge(o_drained[before[1] % 2], count(OB, before[0], before[1] // 2))
                dve.wait_ge(o_full[step % 2], count(OB, it, step // 2))
                nc.vector.reciprocal(rec[:, :].unsqueeze(2), got[:, :, CONT:VD]).then_inc(rec_ready, 1)
                at = (it >> 3) * (TILES * D) + (it & 7) * (2 * CONT) + qt * D
                if not isinstance(it, int):
                    at = nc.s_assert_within(at, 0, 2 * TILES * D - 2 * CONT,
                                            skip_runtime_bounds_check_because="a pair's columns")
                dve.wait_ge(rec_ready, count(TILES, it, step))
                dve.sem_inc(dve_gate, 1)
                nc.vector.tensor_tensor(
                    o_all[:, :, :].rearrange("p a d -> p (a d)")[:, bass.ds(at, 2 * CONT)]
                    .rearrange("p (e d) -> p e d", d=CONT), got[:, :, 0:CONT],
                    rec[:, :].unsqueeze(2).to_broadcast([P, 2, CONT]), ALU.mult).then_inc(o_drained[step % 2], 1)

            def pair(it, following):
                for unit in range(UNITS):
                    for g in groups_of(unit):
                        if g % 2 == 0:
                            n = GROUPS[g][2]
                            dve.wait_ge(t_full[0], count(IN_BANK, it, g // 2))
                            nc.vector.tensor_copy(pT[g % 4][:, 0:n, :].rearrange("p a t -> p (a t)"),
                                                  t_bank[0][:, 0:n * P]).then_inc(t_drained[0], 1)
                    ahead(it, following, unit, stats)
                    if unit >= 2 and unit % 2 == 0:
                        keep_o(it, unit // 2 - 1)
                keep_o(it, TILES - 1)

            stats(0, 0)
            stats(0, 1)
            with dve.Fori(0, ITERS - 1) as it:
                pair(it, it + 1)
            pair(ITERS - 1, None)

        @block.scalar
        def _(act):
            def exponent(it, unit):
                step, e = unit // 2, unit % 2
                qt = ORDER[step]
                before = (it, unit - 2) if unit >= 2 else (it - 1, UNITS - 2 + unit)
                g = groups_of(before[1])[-1]
                act.wait_ge(t_full[g % 2], count(IN_BANK, before[0], g // 2))
                act.wait_ge(bias_ready[e], count(TILES, it, step))
                nc.scalar.activation(probs[e][:, 0:(qt + 1) * P], s_bank[e][:, 0:(qt + 1) * P], ACT.Exp,
                                     bias=bias[e][:, :], scale=SCALE).then_inc(exp_done[e], 1)

            def pair(it, following):
                for unit in range(UNITS):
                    for g in groups_of(unit):
                        if g % 2 == 1:
                            n = GROUPS[g][2]
                            act.wait_ge(t_full[1], count(IN_BANK, it, g // 2))
                            nc.scalar.copy(pT[g % 4][:, 0:n, :].rearrange("p a t -> p (a t)"),
                                           t_bank[1][:, 0:n * P]).then_inc(t_drained[1], 1)
                    ahead(it, following, unit, exponent)

            exponent(0, 0)
            exponent(0, 1)
            with act.Fori(0, ITERS - 1) as it:
                pair(it, it + 1)
            pair(ITERS - 1, None)


def mla_output(nc, ident_dram, o_all, emb, wo_dram, h1_dram, tower_in):
    D = wo_dram.shape[0]
    KC = D // P
    LANES = 4
    ITERS = emb.shape[1] // LANES

    with ExitStack() as ctx:
        ctx.enter_context(nc.cleanup_on_exit())
        def sb(name, shape, dt=F32):
            return ctx.enter_context(nc.sbuf_tensor("mo_" + name, shape, dt))

        def sem(name):
            return nc.alloc_semaphore("mo_" + name)

        ident = sb("ident", [P, P])
        wo = sb("wo", [P, KC, D])
        minus_half = sb("minus_half", [P, 1])
        o = [sb(f"o{b}", [P, D]) for b in range(LANES)]
        oT = [sb(f"oT{b}", [P, KC, P]) for b in range(LANES)]
        h1 = [sb(f"h1{b}", [P, D]) for b in range(LANES)]
        stats = [sb(f"stats{b}", [P, 6]) for b in range(LANES)]
        mv = [sb(f"mv{b}", [P, 2]) for b in range(LANES)]
        ve = [sb(f"ve{b}", [P, 1]) for b in range(LANES)]
        rstd = [sb(f"rstd{b}", [P, 1]) for b in range(LANES)]
        xn = [sb(f"xn{b}", [P, D]) for b in range(LANES)]
        t_bank = [ctx.enter_context(nc.psum_tensor(f"mo_t{b}", [P, 512], F32)) for b in range(LANES)]
        w_bank = [ctx.enter_context(nc.psum_tensor(f"mo_w{b}", [P, 512], F32)) for b in range(LANES)]
        const_in, root_ready = sem("const_in"), sem("root_ready")
        NAMES = ["o_copied", "t_full", "t_drained", "w_full", "h1_ready", "stats_ready", "mv_ready", "ve_ready",
                 "rstd_ready", "xn_ready"]
        s = [{n: sem(f"{n}{b}") for n in NAMES} for b in range(LANES)]
        h1_stored, xn_stored = [[sem(f"{n}{b}") for b in range(LANES)] for n in ("h1_stored", "xn_stored")]
        act_gate, dve_gate, sp_gate = sem("act_gate"), sem("dve_gate"), sem("sp_gate")

        def now(i):
            return i + 2

        block = ctx.enter_context(nc.Block())

        @block.sync
        def _(sp):
            for b in range(LANES):
                for n in NAMES:
                    sp.sem_inc(s[b][n], 1)
                sp.sem_inc(h1_stored[b], 16)
                sp.sem_inc(xn_stored[b], 16)
            sp.dma_start(ident[:, :], ident_dram).then_inc(const_in, 16)
            sp.dma_start(wo[:, :, :], wo_dram.rearrange("(c p) n -> p c n", p=P)).then_inc(const_in, 16)
            with sp.Fori(0, ITERS) as i:
                for b in range(LANES):
                    sp.wait_ge(h1_stored[b], 16 * (i + 1))
                    sp.sem_inc(sp_gate, 1)
                    sp.wait_ge(s[b]["h1_ready"], now(i))
                    sp.sem_inc(sp_gate, 1)
                    sp.dma_start(h1_dram[b // 2, bass.ds((b % 2) * ITERS * P + i * P, P), :], h1[b][:, :]).then_inc(h1_stored[b], 16)
                    sp.wait_ge(xn_stored[b], 16 * (i + 1))
                    sp.sem_inc(sp_gate, 1)
                    sp.wait_ge(s[b]["xn_ready"], now(i))
                    sp.sem_inc(sp_gate, 1)
                    sp.dma_start(tower_in[b // 2, bass.ds((b % 2) * ITERS * P + i * P, P), :], xn[b][:, :]).then_inc(xn_stored[b], 16)
            for b in range(LANES):
                sp.wait_ge(h1_stored[b], 16 * (ITERS + 1))
                sp.wait_ge(xn_stored[b], 16 * (ITERS + 1))

        @block.scalar
        def _(act):
            with act.Fori(0, ITERS) as i:
                for b in range(LANES):
                    act.wait_ge(s[b]["t_full"], now(i - 1))
                    act.sem_inc(act_gate, 1)
                    nc.scalar.copy(o[b][:, :], o_all[:, bass.ds(b * ITERS + i, 1), :].rearrange("p a d -> p (a d)"))\
                        .then_inc(s[b]["o_copied"], 1)
                for b in range(LANES):
                    act.wait_ge(s[b]["t_full"], now(i))
                    nc.scalar.copy(oT[b][:, :, :].rearrange("p c t -> p (c t)"), t_bank[b][:, 0:D])\
                        .then_inc(s[b]["t_drained"], 1)

        @block.tensor
        def _(pe):
            pe.wait_ge(const_in, 32)
            with pe.Fori(0, ITERS) as i:
                for b in range(LANES):
                    pe.wait_ge(s[b]["o_copied"], now(i))
                    for c in range(KC):
                        last = nc.tensor.transpose(t_bank[b][:, c * P:(c + 1) * P], o[b][:, c * P:(c + 1) * P],
                                                   ident[:, :])
                    last.then_inc(s[b]["t_full"], 1)
                for b in range(LANES):
                    pe.wait_ge(s[b]["t_drained"], now(i))
                    pe.wait_ge(s[b]["h1_ready"], now(i - 1))
                    for c in range(KC):
                        last = nc.tensor.matmul(w_bank[b][:, 0:D], oT[b][:, c, :], wo[:, c, :], start=c == 0,
                                                stop=c == KC - 1)
                    last.then_inc(s[b]["w_full"], 1)

        @block.vector
        def _(dve):
            nc.vector.memset(minus_half[:, :], -0.5).then_inc(root_ready, 1)
            with dve.Fori(0, ITERS) as i:
                for b in range(LANES):
                    dve.wait_ge(h1_stored[b], 16 * (i + 1))
                    dve.wait_ge(s[b]["xn_ready"], now(i - 1))
                    dve.wait_ge(s[b]["w_full"], now(i))
                    dve.sem_inc(dve_gate, 1)
                    nc.vector.tensor_tensor(h1[b][:, :], w_bank[b][:, 0:D],
                                            emb[:, bass.ds(b * ITERS + i, 1), :].rearrange("p a d -> p (a d)"),
                                            ALU.add).then_inc(s[b]["h1_ready"], 1)
                for b in range(LANES):
                    dve.wait_ge(s[b]["h1_ready"], now(i))
                    dve.sem_inc(dve_gate, 1)
                    nc.vector.bn_stats(stats[b][:, :], h1[b][:, :]).then_inc(s[b]["stats_ready"], 1)
                for b in range(LANES):
                    dve.wait_ge(s[b]["stats_ready"], now(i))
                    dve.sem_inc(dve_gate, 1)
                    nc.vector.bn_aggr(mv[b][:, :], stats[b][:, :]).then_inc(s[b]["mv_ready"], 1)
                for b in range(LANES):
                    dve.wait_ge(s[b]["mv_ready"], now(i))
                    nc.vector.tensor_scalar(ve[b][:, :], mv[b][:, 1:2], 1e-5, None, ALU.add)\
                        .then_inc(s[b]["ve_ready"], 1)
                for b in range(LANES):
                    dve.wait_ge(s[b]["rstd_ready"], now(i))
                    dve.wait_ge(xn_stored[b], 16 * (i + 1))
                    nc.vector.tensor_scalar(xn[b][:, :], h1[b][:, :], mv[b][:, 0:1], rstd[b][:, :], ALU.subtract,
                                            ALU.mult).then_inc(s[b]["xn_ready"], 1)

        @block.gpsimd
        def _(pool):
            pool.wait_ge(root_ready, 1)
            with pool.Fori(0, ITERS) as i:
                for b in range(LANES):
                    pool.wait_ge(s[b]["ve_ready"], now(i))
                    nc.gpsimd.tensor_tensor(rstd[b][:, :], ve[b][:, :], minus_half[:, :], ALU.pow)\
                        .then_inc(s[b]["rstd_ready"], 1)


def mla_stage(nc, ids, embedding, ident, rope, causal, w_x, g_kv, w_kvdec, w_q, wo, h1_dram, tower_in):
    PAIRS, T = 8, h1_dram.shape[1]
    TILES = T // P
    with ExitStack() as ctx:
        emb = ctx.enter_context(nc.sbuf_tensor("emb_rows", [P, 2 * TILES, 256], F32))
        with ExitStack() as inner:
            qT_all = inner.enter_context(nc.sbuf_tensor("qT_all", [P, 2 * PAIRS, T], F32))
            kT_all = inner.enter_context(nc.sbuf_tensor("kT_all", [P, 2 * PAIRS, T], F32))
            v_all = inner.enter_context(nc.sbuf_tensor("v_all", [P, 2 * PAIRS, TILES, 34], F32))
            mla_project(nc, ids, embedding, ident, rope, w_x, g_kv, w_kvdec, w_q, emb, qT_all, kT_all, v_all)
            o_all = inner.enter_context(nc.sbuf_tensor("o_all", [P, 2 * TILES, 256], F32))
            mla_attend(nc, ident, causal, qT_all, kT_all, v_all, o_all)
            mla_output(nc, ident, o_all, emb, wo, h1_dram, tower_in)


def local_tower(nc, ident_dram, trig_dram, band_dram, shift_dram, h_dram, scale_dram, wqkv_dram, wo_dram,
                lng_dram, lnb_dram, w1_dram, b1_dram, w2_dram, b2_dram):
    LAYERS, D, QKV = wqkv_dram.shape
    F2 = w1_dram.shape[2]
    F = F2 // 2
    HALF = F // 2
    HD, WIN = 64, 64
    INNER = QKV // 3
    HEADS = INNER // HD
    PAIRS = HEADS // 2
    KC = D // P
    NB, ROWS = h_dram.shape[1], h_dram.shape[2]
    TILES = (ROWS - 1) // P
    ITERS = LAYERS * TILES
    TILE_BITS = TILES.bit_length() - 1
    assert TILES == 1 << TILE_BITS and NB == 2
    KEYS = WIN + P
    OWN, BEFORE = (0, P + 2 * WIN), P
    FC = (F + P - 1) // P
    FTAIL = F - (FC - 1) * P
    OC = INNER // P
    h_rows = h_dram.rearrange("l b t d -> (l b t) d")

    def within(value, most):
        if isinstance(value, int):
            return value
        return nc.s_assert_within(value, 0, most,
                                  skip_runtime_bounds_check_because="layer and tile come from one count")

    with ExitStack() as ctx:
        ctx.enter_context(nc.cleanup_on_exit())
        def sb(name, shape):
            return ctx.enter_context(nc.sbuf_tensor("lt_" + name, shape, F32))

        def pb(name):
            return ctx.enter_context(nc.psum_tensor("lt_" + name, [P, 512], F32))

        def sem(name):
            return nc.alloc_semaphore("lt_" + name)

        ident = sb("ident", [P, P])
        shift = sb("shift", [P, 2, P])
        wqkv = sb("wqkv", [P, 2 * KC * QKV])
        wo = sb("wo", [P, OC, D])
        w1 = sb("w1", [P, KC, F2])
        w2 = sb("w2", [P, FC, D])
        b1 = sb("b1", [P, F2])
        b2 = sb("b2", [P, D])
        lng = sb("lng", [P, KC])
        lnb = sb("lnb", [P, KC])
        scales = sb("scales", [P, LAYERS, 2, HD])
        trig = sb("trig", [P, 2, 2, HD])
        rot_c = sb("rot_c", [P, 2, HD])
        rot_s = sb("rot_s", [P, 2, HD])
        band = sb("band", [P, 2 * KEYS + 1])
        minus_half = sb("minus_half", [P, HEADS])
        x = [sb(f"x{b}", [P, D]) for b in range(NB)]
        xs = [sb(f"xs{b}", [P, D]) for b in range(NB)]
        xsT = [sb(f"xsT{b}", [P, KC, P]) for b in range(NB)]
        raw = [sb(f"raw{b}", [P, 2, HEADS, HD]) for b in range(NB)]
        qT = [sb(f"qT{b}", [P, PAIRS, P]) for b in range(NB)]
        kT = [sb(f"kT{b}", [P, PAIRS, 2 * KEYS]) for b in range(NB)]
        v = [sb(f"v{b}", [P, HEADS, HD + 1]) for b in range(NB)]
        v_prev = [sb(f"v_prev{b}", [P, HEADS, HD + 1]) for b in range(NB)]
        x1 = [sb(f"x1{b}", [P, D]) for b in range(NB)]
        x1_prev = [sb(f"x1_prev{b}", [P, P]) for b in range(NB)]
        out_tile = [sb(f"out_tile{b}", [P, D]) for b in range(NB)]
        turn_c = sb("turn_c", [P, 2, HEADS, HD])
        turn_s = sb("turn_s", [P, 2, HEADS, HD])
        ss = sb("ss", [P, 2, HEADS])
        rn = sb("rn", [P, 2, HEADS])
        sm = sb("sm", [P, 4, 2 * KEYS])
        minus_max = sb("minus_max", [P, 4, 2])
        pT = sb("pT", [P, 4, P])
        pT_prev = sb("pT_prev", [P, 2, P])
        rec = sb("rec", [P, 4])
        o = sb("o", [P, HEADS, HD])
        oT = sb("oT", [P, OC, P])
        stats = sb("stats", [P, 2, 6])
        mv = sb("mv", [P, 2])
        ve = sb("ve", [P, 1])
        rstd = sb("rstd", [P, 1])
        yn = sb("yn", [P, D])
        yT = sb("yT", [P, KC, P])
        gate = sb("gate", [P, F])
        ff = sb("ff", [P, FC * P])
        fT = sb("fT", [P, FC, P])

        a_bank = [pb("a0"), pb("a1")]
        s_bank = [pb("s0"), pb("s1")]
        p_bank = [pb("p0"), pb("p1")]
        o_bank = [pb("o0"), pb("o1")]

        a_full, a_drained = [sem("a0_full"), sem("a1_full")], [sem("a0_drained"), sem("a1_drained")]
        s_full, s_drained = [sem("s0_full"), sem("s1_full")], [sem("s0_drained"), sem("s1_drained")]
        p_full, p_drained = [sem("p0_full"), sem("p1_full")], [sem("p0_drained"), sem("p1_drained")]
        o_full, o_drained = [sem("o0_full"), sem("o1_full")], [sem("o0_drained"), sem("o1_drained")]
        const_in, consts_set = sem("const_in"), sem("consts_set")
        wqkv_in, wo_in, wff_in = sem("wqkv_in"), sem("wo_in"), sem("wff_in")
        xs_in = [sem(f"xs_in{b}") for b in range(NB)]
        x_in = [sem(f"x_in{b}") for b in range(NB)]
        trig_in, band_in = sem("trig_in"), sem("band_in")
        h_stored = [sem(f"h_stored{b}") for b in range(NB)]
        rot_ready = sem("rot_ready")
        ss_ready, rn_ready, turn_s_ready, turned = sem("ss_ready"), sem("rn_ready"), sem("turn_s_ready"), sem("turned")
        mx_ready, probs_ready = sem("mx_ready"), sem("probs_ready")
        ve_ready, rstd_ready = sem("ve_ready"), sem("rstd_ready")
        x1_kept, gelu_ready, ff_ready = sem("x1_kept"), sem("gelu_ready"), sem("ff_ready")
        squares_summed, c_turned, added = sem("squares_summed"), sem("c_turned"), sem("added")
        v_moved, k_moved, yT_begun = sem("v_moved"), sem("k_moved"), sem("yT_begun")
        rec_ready, stats_ready, mv_ready = sem("rec_ready"), sem("stats_ready"), sem("mv_ready")
        act_gate, dve_gate, pool_gate, sp_gate = sem("act_gate"), sem("dve_gate"), sem("pool_gate"), sem("sp_gate")

        COUNTS = [(s_full, 4), (s_drained, 4), (p_full, 7), (p_drained, 7), (o_full, 5), (o_drained, 5)]
        ONES = [(ss_ready, 2), (rn_ready, 2), (turn_s_ready, 2), (turned, 2), (mx_ready, PAIRS),
                (probs_ready, PAIRS), (ve_ready, 1), (rstd_ready, 1), (x1_kept, 1), (gelu_ready, 2),
                (ff_ready, 2), (squares_summed, 2), (c_turned, 2), (added, 2), (rec_ready, 4), (yT_begun, 1), (stats_ready, 2),
                (mv_ready, 1), (v_moved, 1), (k_moved, 1)]
        A_USES = 11
        XT, PROJ, TR = 0, (1, 2, 3, 4, 5, 8), (6, 7, 9, 10)
        PROBS_USE, OT_USE, SHIFT_USE, HT_USE = ((0, 1, 2, 4), (0, 1, 2, 3)), (3, 4), 5, 6
        WO_USE = 2

        def nth(per, k, pos=0):
            return per * (k + 2) + pos + 1

        def a_use(u, b, pos):
            n = A_USES * b + pos
            return n % 2, A_USES * (u + 1) + n // 2 + 1

        block = ctx.enter_context(nc.Block())

        @block.sync
        def _(sp):
            for banks, n in COUNTS:
                for s in banks:
                    sp.sem_inc(s, 2 * n)
            for s in a_full + a_drained:
                sp.sem_inc(s, A_USES)
            for s, n in ONES:
                sp.sem_inc(s, 2 * n)
            sp.sem_inc(rot_ready, 1)
            for s in h_stored:
                sp.sem_inc(s, 16)
            sp.dma_start(ident[:, :], ident_dram).then_inc(const_in, 16)
            sp.dma_start(shift[:, :, :], shift_dram.rearrange("a p q -> p a q")).then_inc(const_in, 16)
            sp.dma_start(scales[:, :, :, :].rearrange("p l a d -> p (l a d)"),
                         scale_dram.rearrange("l a d -> (l a d)").partition_broadcast(P)).then_inc(const_in, 16)

            def load_wqkv(l, parity):
                sp.dma_start(wqkv[:, bass.ds(parity * (KC * QKV), KC * QKV)].rearrange("p (c n) -> p c n", c=KC),
                             wqkv_dram[bass.ds(l, 1), :, :].rearrange("l (c p) n -> p (l c) n", p=P)).then_inc(wqkv_in, 16)

            def row(u, b, first):
                at = ((u >> TILE_BITS) * NB + b) * ROWS + (u & (TILES - 1)) * P + first
                return within(at, (LAYERS + 1) * NB * ROWS - P)

            def load_xs(u, b):
                sp.dma_start(xs[b][:, 0:P], h_rows[bass.ds(row(u, b, 1), P), 0:P]).then_inc(xs_in[b], 16)
                sp.dma_start(xs[b][:, P:D], h_rows[bass.ds(row(u, b, 0), P), P:D]).then_inc(xs_in[b], 16)

            def load_x(u, b):
                sp.dma_start(x[b][:, :], h_rows[bass.ds(row(u, b, 1), P), :]).then_inc(x_in[b], 16)

            def load_trig(u):
                sp.dma_start(trig[:, :, :, :].rearrange("p a c d -> p (a c d)"),
                             trig_dram[bass.ds(u & (TILES - 1), 1), :, :].rearrange("t p n -> p (t n)")).then_inc(trig_in, 16)

            def load_band(u):
                sp.dma_start(band[:, :], band_dram[bass.ds(u & (TILES - 1), 1), :, :].rearrange("t p n -> p (t n)"))\
                    .then_inc(band_in, 16)

            load_wqkv(0, 0)
            for b in range(NB):
                load_xs(0, b)
            load_trig(0)
            load_band(0)
            for b in range(NB):
                load_x(0, b)

            def layer(l, last):
                sp.dma_start(wo[:, :, :], wo_dram[bass.ds(l, 1), :, :].rearrange("l (c p) n -> p (l c) n", p=P))\
                    .then_inc(wo_in, 16)
                sp.dma_start(w1[:, :, :], w1_dram[bass.ds(l, 1), :, :].rearrange("l (c p) n -> p (l c) n", p=P))\
                    .then_inc(wff_in, 16)
                w2_l = w2_dram[bass.ds(l, 1), :, :]
                sp.wait_ge(consts_set, 1)
                sp.dma_start(w2[:, 0:FC - 1, :], w2_l[:, 0:(FC - 1) * P, :].rearrange("l (c p) n -> p (l c) n", p=P))\
                    .then_inc(wff_in, 16)
                sp.dma_start(w2[0:FTAIL, FC - 1, :], w2_l[:, (FC - 1) * P:F, :].rearrange("l p n -> p (l n)"))\
                    .then_inc(wff_in, 16)
                sp.dma_start(b1[:, :], b1_dram[bass.ds(l, 1), :].rearrange("l n -> (l n)").partition_broadcast(P))\
                    .then_inc(wff_in, 16)
                sp.dma_start(b2[:, :], b2_dram[bass.ds(l, 1), :].rearrange("l n -> (l n)").partition_broadcast(P))\
                    .then_inc(wff_in, 16)
                with nc.allow_non_contiguous_dma(reason="256 gains and biases, one to a partition"):
                    sp.dma_start(lng[:, :], lng_dram[bass.ds(l, 1), :].rearrange("l (c p) -> p (l c)", p=P))\
                        .then_inc(wff_in, 16)
                    sp.dma_start(lnb[:, :], lnb_dram[bass.ds(l, 1), :].rearrange("l (c p) -> p (l c)", p=P))\
                        .then_inc(wff_in, 16)
                if not last:
                    sp.wait_ge(wqkv_in, 16 * (l + 1))
                    sp.sem_inc(sp_gate, 1)
                    load_wqkv(l + 1, (l + 1) & 1)
                with sp.Fori(0, TILES) as p:
                    u = sp.snap(l * TILES + p)
                    for b in range(NB):
                        j, n = a_use(u, b, XT)
                        sp.wait_ge(a_drained[j], n)
                        load_xs(u + 1, b)
                    sp.wait_ge(rot_ready, u + 2)
                    load_trig(u + 1)
                    for b in range(NB):
                        if b == 1:
                            sp.wait_ge(x1_kept, nth(1, 2 * u + 1))
                            load_band(u + 1)
                        sp.wait_ge(o_drained[0], nth(5, 2 * u + b, WO_USE))
                        load_x(u + 1, b)
                        sp.wait_ge(o_drained[1], nth(5, 2 * u + b, 4))
                        sp.dma_start(h_rows[bass.ds(row(u + TILES, b, 1), P), :], out_tile[b][:, :]).then_inc(h_stored[b], 16)
                        sp.wait_ge(h_stored[b], 16 * (u + 2))
                        sp.sem_inc(sp_gate, 1)

            with sp.Fori(0, LAYERS - 1) as l:
                layer(l, False)
            layer(LAYERS - 1, True)
            for b in range(NB):
                sp.wait_ge(xs_in[b], 32 * (ITERS + 1))
                sp.wait_ge(x_in[b], 16 * (ITERS + 1))
            sp.wait_ge(trig_in, 16 * (ITERS + 1))
            sp.wait_ge(band_in, 16 * (ITERS + 1))

        @block.tensor
        def _(pe):
            def mm(out, lhsT, rhs, start, stop):
                return nc.tensor.matmul(out, lhsT, rhs, start=start, stop=stop)

            def open_a(u, b, pos):
                j, n = a_use(u, b, pos)
                pe.wait_ge(a_drained[j], n - 1)
                return a_bank[j], a_full[j]

            def input_T(u, b):
                bank, full = open_a(u, b, XT)
                pe.wait_ge(xs_in[b], 32 * (u + 1))
                for c in range(KC):
                    last = nc.tensor.transpose(bank[:, c * P:(c + 1) * P], xs[b][:, c * P:(c + 1) * P], ident[:, :])
                last.then_inc(full, 1)

            def project(u, b, g, chunks=range(KC)):
                j, n = a_use(u, b, PROJ[g])
                if 0 in chunks:
                    open_a(u, b, PROJ[g])
                if g == 0:
                    jx, nx = a_use(u, b, XT)
                    pe.wait_ge(a_drained[jx], nx)
                    pe.wait_ge(wqkv_in, 16 * ((u >> TILE_BITS) + 1))
                for c in chunks:
                    at = ((u >> TILE_BITS) & 1) * (KC * QKV) + c * QKV + g * 512
                    last = mm(a_bank[j][:, :], xsT[b][:, c, :], wqkv[:, bass.ds(at, 512)], c == 0, c == KC - 1)
                if KC - 1 in chunks:
                    last.then_inc(a_full[j], 1)

            def turn_T(u, b, g):
                bank, full = open_a(u, b, TR[g])
                if g % 2 == 0:
                    pe.wait_ge(turned, nth(2, 2 * u + b, g // 2))
                for i in range(4):
                    pair = 4 * (g % 2) + i
                    last = nc.tensor.transpose(bank[:, i * P:(i + 1) * P],
                                               turn_c[:, g // 2, 2 * pair:2 * pair + 2, :].rearrange("p a d -> p (a d)"),
                                               ident[:, :])
                last.then_inc(full, 1)

            def scores(u, b, hp):
                k = 2 * u + b
                if hp == 0:
                    j, n = a_use(u, b, TR[3])
                    pe.wait_ge(a_drained[j], n)
                    j, n = a_use(u, b, TR[2])
                    pe.wait_ge(a_drained[j], n)
                pe.wait_ge(s_drained[hp % 2], nth(4, k, hp // 2) - 1)
                mm(s_bank[hp % 2][:, 0:2 * KEYS], qT[b][:, hp, :], kT[b][:, hp, :],
                   True, True).then_inc(s_full[hp % 2], 1)

            def probs_T(u, b, g):
                k = 2 * u + b
                pe.wait_ge(probs_ready, nth(PAIRS, k, 2 * g + 1))
                pe.wait_ge(p_drained[0], nth(7, k, PROBS_USE[0][g]) - 1)
                for i in range(4):
                    last = nc.tensor.transpose(p_bank[0][:, i * P:(i + 1) * P],
                                               sm[:, (2 * g + i // 2) % 4, OWN[i % 2]:OWN[i % 2] + P], ident[:, :])
                last.then_inc(p_full[0], 1)
                pe.wait_ge(p_drained[1], nth(7, k, g) - 1)
                for i in range(2):
                    last = nc.tensor.transpose(p_bank[1][:, i * P:(i + 1) * P], sm[:, (2 * g + i) % 4, BEFORE:BEFORE + P],
                                               ident[:, :])
                last.then_inc(p_full[1], 1)

            def weigh(u, b, g):
                k = 2 * u + b
                pe.wait_ge(p_drained[0], nth(7, k, PROBS_USE[0][g]))
                pe.wait_ge(p_drained[1], nth(7, k, g))
                if g == 0:
                    for pos in PROJ[4:6]:
                        j, n = a_use(u, b, pos)
                        pe.wait_ge(a_drained[j], n)
                pe.wait_ge(o_drained[g % 2], nth(5, k, g // 2) - 1)
                for i in range(2):
                    hp = 2 * g + i
                    out = o_bank[g % 2][:, i * 2 * (HD + 1):(i + 1) * 2 * (HD + 1)]
                    mm(out, pT_prev[:, i, :], v_prev[b][:, 2 * hp:2 * hp + 2, :].rearrange("p a d -> p (a d)"),
                       True, False)
                    for e in range(2):
                        last = mm(out[:, e * (HD + 1):(e + 1) * (HD + 1)], pT[:, 2 * i + e, :],
                                  v[b][:, 2 * hp + e, :], False, e == 1)
                last.then_inc(o_full[g % 2], 1)

            def out_T(u, b, j):
                k = 2 * u + b
                pe.wait_ge(o_drained[0], nth(5, k, j))
                pe.wait_ge(o_drained[1], nth(5, k, j))
                pe.wait_ge(p_drained[j], nth(7, k, OT_USE[j]) - 1)
                for i in range(4):
                    c = 4 * j + i
                    last = nc.tensor.transpose(p_bank[j][:, i * P:(i + 1) * P],
                                               o[:, 2 * c:2 * c + 2, :].rearrange("p a d -> p (a d)"), ident[:, :])
                last.then_inc(p_full[j], 1)

            def out_project(u, b, j):
                k = 2 * u + b
                if j == 0:
                    pe.wait_ge(wo_in, 16 * ((u >> TILE_BITS) + 1))
                    pe.wait_ge(o_drained[0], nth(5, k, WO_USE) - 1)
                pe.wait_ge(p_drained[j], nth(7, k, OT_USE[j]))
                for c in range(4 * j, 4 * j + 4):
                    last = mm(o_bank[0][:, 0:D], oT[:, c, :], wo[:, c, :], c == 0, c == OC - 1)
                if j == 1:
                    last.then_inc(o_full[0], 1)

            def shift_x1(u, b):
                k = 2 * u + b
                pe.wait_ge(o_drained[0], nth(5, k, WO_USE))
                pe.wait_ge(x1_kept, nth(1, k - 2))
                pe.wait_ge(p_drained[0], nth(7, k, SHIFT_USE) - 1)
                mm(p_bank[0][:, 0:P], shift[:, 0, :], x1[b][:, P:D], True, False)
                mm(p_bank[0][:, 0:P], shift[:, 1, :], x1_prev[b][:, :], False, True).then_inc(p_full[0], 1)

            def norm_T(u, b):
                k = 2 * u + b
                pe.wait_ge(p_drained[0], nth(7, k, SHIFT_USE))
                pe.wait_ge(p_drained[1], nth(7, k, 5) - 1)
                for c in range(KC):
                    last = nc.tensor.transpose(p_bank[1][:, c * P:(c + 1) * P], yn[:, c * P:(c + 1) * P], ident[:, :])
                last.then_inc(p_full[1], 1)

            def expand(u, b, g):
                k = 2 * u + b
                if g == 0:
                    pe.wait_ge(yT_begun, nth(1, k))
                    pe.wait_ge(wff_in, 16 * 7 * ((u >> TILE_BITS) + 1))
                j = 1 - g % 2
                pos = (2, 3, 3, 4)[g]
                pe.wait_ge(o_drained[j], nth(5, k, pos) - 1)
                first = (F, F + HALF, 0, HALF)[g]
                for c in range(KC):
                    if g == 0 and c == 1:
                        pe.wait_ge(p_drained[1], nth(7, k, 5))
                    last = mm(o_bank[j][:, 0:HALF], yT[:, c, :], w1[:, c, first:first + HALF], c == 0, c == KC - 1)
                last.then_inc(o_full[j], 1)

            def ff_T(u, b):
                k = 2 * u + b
                pe.wait_ge(ff_ready, nth(2, k, 1))
                for j in range(2):
                    n = 4 if j == 0 else FC - 4
                    pe.wait_ge(p_drained[j], nth(7, k, HT_USE) - 1)
                    for i in range(n):
                        c = 4 * j + i
                        last = nc.tensor.transpose(p_bank[j][:, i * P:(i + 1) * P], ff[:, c * P:(c + 1) * P], ident[:, :])
                    last.then_inc(p_full[j], 1)

            def contract(u, b):
                k = 2 * u + b
                pe.wait_ge(o_drained[1], nth(5, k, 4) - 1)
                for c in range(FC):
                    if c % 4 == 0:
                        pe.wait_ge(p_drained[c // 4], nth(7, k, HT_USE))
                    last = mm(o_bank[1][:, 0:D], fT[:, c, :], w2[:, c, :], c == 0, c == FC - 1)
                last.then_inc(o_full[1], 1)

            def unit(u, b, nxt):
                def A(f, *a):
                    if nxt is not None:
                        f(*nxt, *a)
                A(input_T)
                scores(u, b, 2)
                scores(u, b, 3)
                A(project, 0)
                probs_T(u, b, 0)
                scores(u, b, 4)
                scores(u, b, 5)
                A(project, 1)
                weigh(u, b, 0)
                probs_T(u, b, 1)
                scores(u, b, 6)
                scores(u, b, 7)
                A(project, 2)
                weigh(u, b, 1)
                probs_T(u, b, 2)
                A(project, 3)
                out_T(u, b, 0)
                weigh(u, b, 2)
                probs_T(u, b, 3)
                A(project, 4)
                weigh(u, b, 3)
                out_project(u, b, 0)
                out_T(u, b, 1)
                A(turn_T, 0)
                A(turn_T, 1)
                out_project(u, b, 1)
                A(project, 5, range(0, 1))
                shift_x1(u, b)
                A(project, 5, range(1, KC))
                A(turn_T, 2)
                A(turn_T, 3)
                norm_T(u, b)
                for g in range(4):
                    expand(u, b, g)
                A(scores, 0)
                ff_T(u, b)
                A(scores, 1)
                contract(u, b)

            def first():
                input_T(0, 0)
                for g in range(5):
                    project(0, 0, g)
                turn_T(0, 0, 0)
                turn_T(0, 0, 1)
                project(0, 0, 5)
                turn_T(0, 0, 2)
                turn_T(0, 0, 3)
                scores(0, 0, 0)
                scores(0, 0, 1)

            pe.wait_ge(const_in, 48)
            pe.wait_ge(consts_set, 1)
            first()
            with pe.Fori(0, ITERS - 1) as u:
                unit(u, 0, (u, 1))
                unit(u, 1, (u + 1, 0))
            unit(ITERS - 1, 0, (ITERS - 1, 1))
            unit(ITERS - 1, 1, None)


        @block.scalar
        def _(act):
            def full_a(u, b, pos):
                j, n = a_use(u, b, pos)
                act.wait_ge(a_full[j], n)
                return a_bank[j], a_drained[j]

            def input_T(u, b):
                bank, drained = full_a(u, b, XT)
                nc.scalar.activation(xsT[b][:, :, :].rearrange("p c t -> p (c t)"), bank[:, 0:D], ACT.Copy)\
                    .then_inc(drained, 1)

            def keep_qk(u, b, g):
                k = 2 * u + b
                half, heads = g // 2, slice(8 * (g % 2), 8 * (g % 2) + 8)
                bank, drained = full_a(u, b, PROJ[g])
                act.wait_ge(turned, nth(2, k - 1, half))
                nc.scalar.activation(raw[b][:, half, heads, :].rearrange("p h d -> p (h d)"), bank[:, :], ACT.Copy)
                nc.scalar.activation(turn_s[:, half, heads, :].rearrange("p h d -> p (h d)"), bank[:, :], ACT.Square)\
                    .then_inc(drained, 1)

            def keep_v(u, b, g):
                k = 2 * u + b
                if g == 4:
                    act.wait_ge(o_full[1], nth(5, k - 2, 1))
                    act.sem_inc(act_gate, 1)
                    for e in range(2):
                        last = nc.scalar.activation(v_prev[b][WIN * e:WIN * e + WIN, e::2, :], v[b][WIN:P, e::2, :],
                                                    ACT.Copy)
                    last.then_inc(v_moved, 1)
                    act.wait_ge(v_moved, nth(1, k))
                bank, drained = full_a(u, b, PROJ[g])
                nc.scalar.activation(v[b][:, 8 * (g - 4):8 * (g - 4) + 8, 0:HD],
                                     bank[:, :].rearrange("p (h d) -> p h d", d=HD), ACT.Copy).then_inc(drained, 1)

            def keep_turned(u, b, g):
                bank, drained = full_a(u, b, TR[g])
                pairs = slice(4 * (g % 2), 4 * (g % 2) + 4)
                src = bank[:, :].rearrange("p (i t) -> p i t", t=P)
                if g < 2:
                    nc.scalar.activation(qT[b][:, pairs, :], src, ACT.Copy).then_inc(drained, 1)
                    return
                act.wait_ge(k_moved, nth(1, 2 * u + b))
                for e in range(2):
                    last = nc.scalar.activation(kT[b][HD * e:HD * e + HD, pairs, OWN[e]:OWN[e] + P],
                                                src[HD * e:HD * e + HD, :, :], ACT.Copy)
                last.then_inc(drained, 1)

            def exp(u, b, hp):
                act.wait_ge(mx_ready, nth(PAIRS, 2 * u + b, hp))
                for e in range(2):
                    tile = sm[:, hp % 4, e * KEYS:(e + 1) * KEYS]
                    last = nc.scalar.activation(tile, tile, ACT.Exp, bias=minus_max[:, hp % 4, e:e + 1])
                last.then_inc(probs_ready, 1)

            def keep_probs(u, b, g):
                act.wait_ge(p_full[0], nth(7, 2 * u + b, PROBS_USE[0][g]))
                nc.scalar.activation(pT[:, :, :].rearrange("p i t -> p (i t)"), p_bank[0][:, :], ACT.Copy)\
                    .then_inc(p_drained[0], 1)

            def keep_oT(u, b, j):
                act.wait_ge(p_full[j], nth(7, 2 * u + b, OT_USE[j]))
                nc.scalar.activation(oT[:, 4 * j:4 * j + 4, :].rearrange("p i t -> p (i t)"), p_bank[j][:, :],
                                     ACT.Copy).then_inc(p_drained[j], 1)

            def keep_yT(u, b):
                act.wait_ge(wff_in, 16 * 7 * ((u >> TILE_BITS) + 1))
                act.wait_ge(p_full[1], nth(7, 2 * u + b, 5))
                for c, done in ((0, yT_begun), (1, p_drained[1])):
                    nc.scalar.activation(yT[:, c, :], p_bank[1][:, c * P:(c + 1) * P], ACT.Identity,
                                         bias=lnb[:, c:c + 1], scale=lng[:, c:c + 1]).then_inc(done, 1)

            def gelu(u, b, j):
                act.wait_ge(o_drained[1 - j], nth(5, 2 * u + b, 2 + j))
                part = gate[:, j * HALF:(j + 1) * HALF]
                nc.scalar.activation(part, part, ACT.Gelu).then_inc(gelu_ready, 1)

            def keep_fT(u, b):
                for j in range(2):
                    n = 4 if j == 0 else FC - 4
                    act.wait_ge(p_full[j], nth(7, 2 * u + b, HT_USE))
                    nc.scalar.activation(fT[:, 4 * j:4 * j + n, :].rearrange("p i t -> p (i t)"),
                                         p_bank[j][:, 0:n * P], ACT.Copy).then_inc(p_drained[j], 1)

            def unit(u, b, nxt):
                def A(f, *a):
                    if nxt is not None:
                        f(*nxt, *a)
                A(input_T)
                exp(u, b, 2)
                exp(u, b, 3)
                keep_probs(u, b, 0)
                A(keep_qk, 0)
                exp(u, b, 4)
                exp(u, b, 5)
                A(keep_qk, 1)
                keep_probs(u, b, 1)
                A(keep_qk, 2)
                exp(u, b, 6)
                keep_probs(u, b, 2)
                exp(u, b, 7)
                A(keep_qk, 3)
                keep_oT(u, b, 0)
                keep_probs(u, b, 3)
                A(keep_v, 4)
                keep_oT(u, b, 1)
                A(keep_turned, 0)
                A(keep_turned, 1)
                A(keep_v, 5)
                keep_yT(u, b)
                A(keep_turned, 2)
                gelu(u, b, 0)
                A(keep_turned, 3)
                gelu(u, b, 1)
                keep_fT(u, b)
                A(exp, 0)
                A(exp, 1)

            act.wait_ge(consts_set, 1)
            input_T(0, 0)
            for g in range(4):
                keep_qk(0, 0, g)
            keep_v(0, 0, 4)
            keep_turned(0, 0, 0)
            keep_turned(0, 0, 1)
            keep_v(0, 0, 5)
            keep_turned(0, 0, 2)
            keep_turned(0, 0, 3)
            exp(0, 0, 0)
            exp(0, 0, 1)
            with act.Fori(0, ITERS - 1) as u:
                unit(u, 0, (u, 1))
                unit(u, 1, (u + 1, 0))
            unit(ITERS - 1, 0, (ITERS - 1, 1))
            unit(ITERS - 1, 1, None)

        @block.vector
        def _(dve):
            def bounded_scores(u, b, hp):
                k = 2 * u + b
                tile = sm[:, hp % 4, :]
                if hp == 0:
                    dve.wait_ge(band_in, 16 * (u + 1))
                dve.wait_ge(p_full[1], nth(7, k, (hp - 4) // 2) if hp >= 4 else nth(7, k - 1, (hp + 4) // 2))
                dve.wait_ge(s_full[hp % 2], nth(4, k, hp // 2))
                nc.vector.tensor_tensor(tile, s_bank[hp % 2][:, 0:2 * KEYS], band[:, 0:2 * KEYS], ALU.add)\
                    .then_inc(s_drained[hp % 2], 1)
                dve.wait_ge(s_drained[hp % 2], nth(4, k, hp // 2))
                nc.vector.reduce_max(minus_max[:, hp % 4, :], tile.rearrange("p (a n) -> p a n", a=2), AX, negate=True)\
                    .then_inc(mx_ready, 1)

            def sum_squares(u, b, half):
                k = 2 * u + b
                for g in (2 * half, 2 * half + 1):
                    j, n = a_use(u, b, PROJ[g])
                    dve.wait_ge(a_drained[j], n)
                dve.wait_ge(rn_ready, nth(2, k - 1, half))
                nc.vector.reduce_sum(ss[:, half, :], turn_s[:, half, :, :], AX).then_inc(squares_summed, 1)
                dve.wait_ge(squares_summed, nth(2, k, half))
                nc.vector.tensor_scalar(ss[:, half, :], ss[:, half, :], 1e-24, None, ALU.max).then_inc(ss_ready, 1)

            def turn_cosine(u, b, half):
                dve.wait_ge(rot_ready, u + 2)
                for g in TR[2 * half:2 * half + 2]:
                    j, n = a_use(u - 1 + b, 1 - b, g)
                    dve.wait_ge(a_full[j], n)
                nc.vector.tensor_tensor(turn_c[:, half, :, :], raw[b][:, half, :, :],
                                        rot_c[:, half, :].unsqueeze(1).to_broadcast([P, HEADS, HD]), ALU.mult)\
                    .then_inc(c_turned, 1)

            def add_sine(u, b, half):
                k = 2 * u + b
                dve.wait_ge(c_turned, nth(2, k, half))
                dve.wait_ge(turn_s_ready, nth(2, k, half))
                nc.vector.tensor_tensor(turn_c[:, half, :, :], turn_c[:, half, :, :], turn_s[:, half, :, :], ALU.add)\
                    .then_inc(added, 1)

            def normalize(u, b, half):
                k = 2 * u + b
                both = turn_c[:, half, :, :]
                dve.wait_ge(added, nth(2, k, half))
                dve.wait_ge(rn_ready, nth(2, k, half))
                nc.vector.tensor_tensor(both, both, rn[:, half, :].unsqueeze(2).to_broadcast([P, HEADS, HD]), ALU.mult)\
                    .then_inc(turned, 1)

            def keep_probs(u, b, g):
                dve.wait_ge(p_full[1], nth(7, 2 * u + b, g))
                nc.vector.tensor_copy(pT_prev[:, :, :].rearrange("p i t -> p (i t)"), p_bank[1][:, 0:2 * P])\
                    .then_inc(p_drained[1], 1)

            def keep_o(u, b, g):
                k = 2 * u + b
                weighed = o_bank[g % 2][:, 0:4 * (HD + 1)].rearrange("p (h d) -> p h d", d=HD + 1)
                dve.wait_ge(o_full[g % 2], nth(5, k, g // 2))
                nc.vector.reciprocal(rec[:, :].unsqueeze(2), weighed[:, :, HD:HD + 1]).then_inc(rec_ready, 1)
                if g == 0:
                    dve.wait_ge(p_full[1], nth(7, k - 1, 4))
                dve.wait_ge(rec_ready, nth(4, k, g))
                nc.vector.tensor_tensor(o[:, 4 * g:4 * g + 4, :], weighed[:, :, 0:HD],
                                        rec[:, :].unsqueeze(2).to_broadcast([P, 4, HD]), ALU.mult)\
                    .then_inc(o_drained[g % 2], 1)

            def add_residual(u, b):
                k = 2 * u + b
                dve.wait_ge(x_in[b], 16 * (u + 1))
                dve.wait_ge(x1_kept, nth(1, k - 1))
                dve.wait_ge(o_full[0], nth(5, k, WO_USE))
                nc.vector.tensor_tensor(x1[b][:, :], o_bank[0][:, 0:D], x[b][:, :], ALU.add).then_inc(o_drained[0], 1)

            def norm(u, b):
                k = 2 * u + b
                dve.wait_ge(o_drained[0], nth(5, k, WO_USE))
                nc.vector.bn_stats(stats[:, 0, :], x1[b][:, 0:P]).then_inc(stats_ready, 1)
                dve.wait_ge(p_full[0], nth(7, k, SHIFT_USE))
                nc.vector.bn_stats(stats[:, 1, :], p_bank[0][:, 0:P]).then_inc(stats_ready, 1)
                dve.wait_ge(stats_ready, nth(2, k, 1))
                dve.sem_inc(dve_gate, 1)
                nc.vector.bn_aggr(mv[:, :], stats[:, :, :].rearrange("p a s -> p (a s)")).then_inc(mv_ready, 1)
                dve.wait_ge(mv_ready, nth(1, k))
                nc.vector.tensor_scalar(ve[:, :], mv[:, 1:2], 1e-5, None, ALU.add).then_inc(ve_ready, 1)
                dve.wait_ge(p_full[1], nth(7, k - 1, 5))
                dve.wait_ge(rstd_ready, nth(1, k))
                nc.vector.tensor_scalar(yn[:, 0:P], x1[b][:, 0:P], mv[:, 0:1], rstd[:, :], ALU.subtract, ALU.mult)
                nc.vector.tensor_scalar(yn[:, P:D], p_bank[0][:, 0:P], mv[:, 0:1], rstd[:, :], ALU.subtract, ALU.mult)\
                    .then_inc(p_drained[0], 1)

            def keep_gate(u, b, j):
                k = 2 * u + b
                if j == 0:
                    dve.wait_ge(wff_in, 16 * 7 * ((u >> TILE_BITS) + 1))
                dve.wait_ge(o_full[1 - j], nth(5, k, 2 + j))
                nc.vector.tensor_tensor(gate[:, j * HALF:(j + 1) * HALF], o_bank[1 - j][:, 0:HALF],
                                        b1[:, F + j * HALF:F + (j + 1) * HALF], ALU.add).then_inc(o_drained[1 - j], 1)

            def keep_up(u, b, j):
                k = 2 * u + b
                if j == 0:
                    dve.wait_ge(p_full[1], nth(7, k - 1, HT_USE))
                dve.wait_ge(o_full[1 - j], nth(5, k, 3 + j))
                nc.vector.tensor_tensor(ff[:, j * HALF:(j + 1) * HALF], o_bank[1 - j][:, 0:HALF],
                                        b1[:, j * HALF:(j + 1) * HALF], ALU.add).then_inc(o_drained[1 - j], 1)

            def gated(u, b, j):
                k = 2 * u + b
                cols = slice(j * HALF, (j + 1) * HALF)
                dve.wait_ge(o_drained[1 - j], nth(5, k, 3 + j))
                dve.wait_ge(gelu_ready, nth(2, k, j))
                nc.vector.tensor_tensor(ff[:, cols], ff[:, cols], gate[:, cols], ALU.mult).then_inc(ff_ready, 1)

            def output(u, b):
                k = 2 * u + b
                dve.wait_ge(x1_kept, nth(1, k))
                dve.wait_ge(o_full[1], nth(5, k, 4))
                nc.vector.tensor_tensor(out_tile[b][:, :], o_bank[1][:, 0:D], out_tile[b][:, :], ALU.add)\
                    .then_inc(o_drained[1], 1)

            def unit(u, b, nxt):
                def A(f, *a):
                    if nxt is not None:
                        f(*nxt, *a)
                bounded_scores(u, b, 2)
                bounded_scores(u, b, 3)
                keep_probs(u, b, 0)
                bounded_scores(u, b, 4)
                bounded_scores(u, b, 5)
                keep_o(u, b, 0)
                keep_probs(u, b, 1)
                A(sum_squares, 0)
                A(turn_cosine, 0)
                bounded_scores(u, b, 6)
                bounded_scores(u, b, 7)
                keep_o(u, b, 1)
                keep_probs(u, b, 2)
                A(sum_squares, 1)
                keep_o(u, b, 2)
                keep_probs(u, b, 3)
                A(turn_cosine, 1)
                A(add_sine, 0)
                keep_o(u, b, 3)
                A(normalize, 0)
                A(add_sine, 1)
                A(normalize, 1)
                add_residual(u, b)
                norm(u, b)
                keep_gate(u, b, 0)
                keep_gate(u, b, 1)
                keep_up(u, b, 0)
                gated(u, b, 0)
                keep_up(u, b, 1)
                gated(u, b, 1)
                A(bounded_scores, 0)
                A(bounded_scores, 1)
                output(u, b)

            for b in range(NB):
                nc.vector.memset(v[b][:, :, :], 1.0)
                nc.vector.memset(v_prev[b][:, :, :], 0.0)
                nc.vector.memset(kT[b][:, :, :], 0.0)
                nc.vector.memset(x1_prev[b][:, :], 0.0)
            nc.vector.memset(minus_half[:, :], -0.5)
            nc.vector.memset(ff[:, :], 0.0)
            nc.vector.memset(w2[:, FC - 1, :], 0.0).then_inc(consts_set, 1)
            for half in range(2):
                sum_squares(0, 0, half)
                turn_cosine(0, 0, half)
                add_sine(0, 0, half)
                normalize(0, 0, half)
            bounded_scores(0, 0, 0)
            bounded_scores(0, 0, 1)
            with dve.Fori(0, ITERS - 1) as u:
                unit(u, 0, (u, 1))
                unit(u, 1, (u + 1, 0))
            unit(ITERS - 1, 0, (ITERS - 1, 1))
            unit(ITERS - 1, 1, None)

        @block.gpsimd
        def _(pool):
            def rotary(u, k_before):
                pool.wait_ge(trig_in, 16 * (u + 1))
                pool.wait_ge(turned, nth(2, k_before, 1))
                pool.sem_inc(pool_gate, 1)
                sc = scales[:, bass.ds(within(u >> TILE_BITS, LAYERS - 1), 1), :, :].rearrange("p l a d -> p (l a) d")
                pool_scales = sc
                nc.gpsimd.tensor_tensor(rot_c[:, :, :], trig[:, :, 0, :], pool_scales, ALU.mult)
                nc.gpsimd.tensor_tensor(rot_s[:, :, 0:HD // 2], trig[:, :, 1, 0:HD // 2], pool_scales[:, :, HD // 2:HD],
                                        ALU.mult)
                nc.gpsimd.tensor_tensor(rot_s[:, :, HD // 2:HD], trig[:, :, 1, HD // 2:HD], pool_scales[:, :, 0:HD // 2],
                                        ALU.mult).then_inc(rot_ready, 1)

            def move_window(u, b):
                pool.wait_ge(s_full[1], nth(4, 2 * u + b - 2, 3))
                pool.sem_inc(pool_gate, 1)
                chunks = kT[b][:, :, :].rearrange("p i (c w) -> p i c w", w=WIN)
                nc.gpsimd.tensor_copy(chunks[:, :, 2:4, :], chunks[:, :, 1:6:4, :]).then_inc(k_moved, 1)

            def turn(u, b, half):
                k = 2 * u + b
                H2 = HD // 2
                pool.wait_ge(ss_ready, nth(2, k, half))
                pool.wait_ge(turned, nth(2, k - 1, half))
                nc.gpsimd.tensor_tensor(rn[:, half, :], ss[:, half, :], minus_half[:, :], ALU.pow).then_inc(rn_ready, 1)
                pool.wait_ge(rot_ready, u + 2)
                for first, other in ((0, H2), (H2, 0)):
                    last = nc.gpsimd.tensor_tensor(
                        turn_s[:, half, :, first:first + H2], raw[b][:, half, :, other:other + H2],
                        rot_s[:, half, first:first + H2].unsqueeze(1).to_broadcast([P, HEADS, H2]), ALU.mult)
                last.then_inc(turn_s_ready, 1)

            def keep_x1(u, b):
                k = 2 * u + b
                pool.wait_ge(p_full[0], nth(7, k, SHIFT_USE))
                pool.sem_inc(pool_gate, 1)
                nc.gpsimd.tensor_scalar(x1_prev[b][:, :], x1[b][:, P:D], band[:, 2 * KEYS:2 * KEYS + 1], None, ALU.mult)
                pool.wait_ge(wff_in, 16 * 7 * ((u >> TILE_BITS) + 1))
                pool.wait_ge(h_stored[b], 16 * (u + 1))
                nc.gpsimd.tensor_tensor(out_tile[b][:, :], x1[b][:, :], b2[:, :], ALU.add).then_inc(x1_kept, 1)

            def reciprocal_root(u, b):
                pool.wait_ge(ve_ready, nth(1, 2 * u + b))
                nc.gpsimd.tensor_tensor(rstd[:, :], ve[:, :], minus_half[:, 0:1], ALU.pow).then_inc(rstd_ready, 1)

            def unit(u, b, nxt):
                def A(f, *a):
                    if nxt is not None:
                        f(*nxt, *a)
                A(move_window)
                A(turn, 0)
                A(turn, 1)
                reciprocal_root(u, b)
                keep_x1(u, b)
                if b == 0 and nxt is not None and not (isinstance(u, int) and u == ITERS - 1):
                    rotary(u + 1, 2 * u + 1)

            pool.wait_ge(const_in, 48)
            pool.wait_ge(consts_set, 1)
            rotary(0, -1)
            move_window(0, 0)
            turn(0, 0, 0)
            turn(0, 0, 1)
            with pool.Fori(0, ITERS - 1) as u:
                unit(u, 0, (u, 1))
                unit(u, 1, (u + 1, 0))
            unit(ITERS - 1, 0, (ITERS - 1, 1))
            unit(ITERS - 1, 1, None)


def gla_stage(nc, ident_dram, spans_dram, after_dram, pairs_dram, wqk_dram, wk_dram, wv_dram, wg_dram, gk1_dram,
              gk2_dram, gkb_dram, norm_dram, wo_dram, h1_dram, tower_out, h3_dram, later):
    NB, T, D = h1_dram.shape
    KC = D // P
    TILES = T // P
    HEADS = 4
    DV = wv_dram.shape[1] // HEADS
    DK = wk_dram.shape[1] // HEADS
    V = HEADS * DV
    HALVES = HEADS * DK // P
    LEVELS = 7
    DIAG, CARRY = LEVELS, LEVELS
    RANK = gk1_dram.shape[1]
    OC = V // P
    INV_NORM = 1.0 / 16.0
    Q_SCALE = DK ** -0.5

    USES = {1: ["z1_0", "z1_1", "z0", "z1", "after0", "after1", "oT0", "oT1"],
            2: ["k0", "decay0", "k1", "decay1", "o0", "wo0"],
            3: ["v0", "decay0", "v1", "decay1", "kv0"],
            4: ["g0", "decay0", "g1", "decay1", "o1", "wo1"],
            5: ["qk0", "decay0", "qk1", "decay1", "kv1"],
            6: [f"pair{b}_{l}" for b in range(NB) for l in range(0, LEVELS + 1, 2)],
            7: [f"pair{b}_{l}" for b in range(NB) for l in range(1, LEVELS + 1, 2)]}

    with ExitStack() as ctx:
        ctx.enter_context(nc.cleanup_on_exit())
        def sb(name, shape, dt=F32):
            return ctx.enter_context(nc.sbuf_tensor("ga_" + name, shape, dt))

        def sem(name):
            return nc.alloc_semaphore("ga_" + name)

        def each(name, shape):
            return [sb(f"{name}{b}", shape) for b in range(NB)]

        ident = sb("ident", [P, P])
        spans = sb("spans", [P, LEVELS + 1, P])
        after = sb("after", [P, P])
        pairs = sb("pairs", [P, LEVELS + 1, P], mybir.dt.int32)
        wqk = sb("wqk", [P, KC, 2 * HALVES * P])
        wk = sb("wk", [P, KC, HALVES * P])
        wv = sb("wv", [P, KC, V])
        wg = sb("wg", [P, KC, V])
        gk1 = sb("gk1", [P, KC, RANK])
        gk2 = sb("gk2", [RANK, HEADS * DK])
        gkb = sb("gkb", [P, HEADS * DK])
        norm_w = sb("norm_w", [P, DV])
        wo = sb("wo", [P, OC, D])
        minus_half = sb("minus_half", [P, HEADS])
        h1, tower, h2, h3 = each("h1", [P, D]), each("tower", [P, D]), each("h2", [P, D]), each("h3", [P, D])
        base = each("base", [P, D])
        stats, mv, ve, rstd = each("stats", [P, 6]), each("mv", [P, 2]), each("ve", [P, 1]), each("rstd", [P, 1])
        xn, xT = each("xn", [P, D]), each("xT", [P, KC, P])
        z1T, z = each("z1T", [RANK, P]), each("z", [P, HEADS * DK])
        small, soft, gates = each("small", [P, HEADS * DK]), each("soft", [P, HEADS * DK]), each("gates", [P, HEADS * DK])
        k_rows, k_left, decay_left = each("k_rows", [P, 256]), each("k_left", [P, 256]), each("decay_left", [P, 256])
        v, silu, out_gate = each("v", [P, V]), each("silu", [P, V]), each("out_gate", [P, V])
        q = [[sb(f"q{b}{j}", [P, LEVELS + 1, P]) for j in range(HALVES)] for b in range(NB)]
        q_carry = [[sb(f"q_carry{b}{j}", [P, P]) for j in range(HALVES)] for b in range(NB)]
        k = [[sb(f"k{b}{h}", [P, LEVELS + 1, P]) for h in range(HEADS)] for b in range(NB)]
        decay = [[sb(f"decay{b}{j}", [P, LEVELS + 1, P]) for j in range(HALVES)] for b in range(NB)]
        weights = each("weights", [P, HEADS, P])
        state = [[sb(f"state{b}{j}", [P, 2 * DV]) for j in range(HALVES)] for b in range(NB)]
        ssum = each("ssum", [P, HEADS])
        meansq, rms = each("meansq", [P, HEADS]), each("rms", [P, HEADS])
        gated, gT = each("gated", [P, V]), each("gT", [P, OC, P])
        bank = [ctx.enter_context(nc.psum_tensor(f"ga_bank{j}", [P, 512], F32)) for j in range(8)]

        full, drained = [sem(f"full{j}") for j in range(8)], [sem(f"drained{j}") for j in range(8)]
        const_in, filled, later_in = sem("const_in"), sem("filled"), sem("later_in")
        NAMES = ["h2_ready", "base_ready", "x_full", "xT_ready", "stats_ready", "mv_ready", "ve_ready", "rstd_ready", "xn_ready", "z_ready",
                 "small_ready", "exp_ready", "soft_ready", "gates_ready", "k_kept", "q_ready", "k_ready",
                 "k_left_ready", "state_ready", "squared", "meansq_ready", "rms_ready", "silu_ready", "out_gate_ready",
                 "gated_ready", "h3_ready"]
        s = [{n: sem(f"{n}{b}") for n in NAMES} for b in range(NB)]
        h1_in, tower_in, h3_stored = [[sem(f"{n}{b}") for b in range(NB)] for n in ("h1_in", "tower_in", "h3_stored")]
        act_gate, dve_gate, pool_gate, sp_gate, pe_gate = (sem("act_gate"), sem("dve_gate"), sem("pool_gate"),
                                                           sem("sp_gate"), sem("pe_gate"))

        def now(i):
            return i + 2

        def use(i, j, name):
            return len(USES[j]) * (i + 1) + USES[j].index(name) + 1

        def head_rows(h):
            return slice(DK * (h % 2), DK * (h % 2) + DK)

        block = ctx.enter_context(nc.Block())

        @block.sync
        def _(sp):
            for j in USES:
                sp.sem_inc(full[j], len(USES[j]))
                sp.sem_inc(drained[j], len(USES[j]))
            for b in range(NB):
                for n in NAMES:
                    sp.sem_inc(s[b][n], 2 if n == "k_ready" else 1)
                sp.sem_inc(h3_stored[b], 16)

            def load(i, b):
                sp.dma_start(h1[b][:, :], h1_dram[b, bass.ds(i * P, P), :]).then_inc(h1_in[b], 16)
                sp.dma_start(tower[b][:, :], tower_out[b, bass.ds(i * P, P), :]).then_inc(tower_in[b], 16)

            def store(i, b):
                sp.wait_ge(h3_stored[b], 16 * (i + 1))
                sp.sem_inc(sp_gate, 1)
                sp.wait_ge(s[b]["h3_ready"], now(i))
                sp.sem_inc(sp_gate, 1)
                sp.dma_start(h3_dram[b, bass.ds(i * P, P), :], h3[b][:, :]).then_inc(h3_stored[b], 16)

            for b in range(NB):
                load(0, b)
            for dst, src in ((ident[:, :], ident_dram), (gk1[:, :, :], gk1_dram.rearrange("(c p) n -> p c n", p=P)),
                             (gk2[:, :], gk2_dram), (gkb[:, :], gkb_dram.partition_broadcast(P)),
                             (wk[:, :, :], wk_dram.rearrange("(c p) n -> p c n", p=P)),
                             (wv[:, :, :], wv_dram.rearrange("(c p) n -> p c n", p=P)),
                             (wg[:, :, :], wg_dram.rearrange("(c p) n -> p c n", p=P)),
                             (wqk[:, :, :], wqk_dram.rearrange("(c p) n -> p c n", p=P)),
                             (spans[:, :, :], spans_dram), (after[:, :], after_dram), (pairs[:, :, :], pairs_dram),
                             (norm_w[:, :], norm_dram.partition_broadcast(P)),
                             (wo[:, :, :], wo_dram.rearrange("(c p) n -> p c n", p=P))):
                sp.dma_start(dst, src).then_inc(const_in, 16)
            for dst, src in later:
                sp.dma_start(dst, src).then_inc(later_in, 16)
            with sp.Fori(0, TILES - 1) as i:
                for b in range(NB):
                    sp.wait_ge(s[b]["h2_ready"], now(i))
                    sp.sem_inc(sp_gate, 1)
                    load(i + 1, b)
                for b in range(NB):
                    store(i, b)
            for b in range(NB):
                store(TILES - 1, b)
            for b in range(NB):
                sp.wait_ge(h3_stored[b], 16 * (TILES + 1))
            sp.wait_ge(later_in, 16 * len(later))

        CONSTS = 16 * 13

        @block.tensor
        def _(pe):
            def mm(out, lhsT, rhs, start, stop):
                return nc.tensor.matmul(out, lhsT, rhs, start=start, stop=stop)

            def free(i, j, name):
                pe.wait_ge(drained[j], use(i, j, name) - 1)

            def project(i, b, j, name, w):
                free(i, j, f"{name}{b}")
                for c in range(KC):
                    last = mm(bank[j][:, 0:w.shape[2]], xT[b][:, c, :], w[:, c, :], c == 0, c == KC - 1)
                last.then_inc(full[j], 1)

            def project_turned(i, b):
                free(i, 5, f"qk{b}")
                for n in range(2 * HALVES):
                    for c in range(KC):
                        last = mm(bank[5][:, n * P:(n + 1) * P], wqk[:, c, n * P:(n + 1) * P], xT[b][:, c, :], c == 0,
                                  c == KC - 1)
                last.then_inc(full[5], 1)

            def gate_sums(i, b):
                pe.wait_ge(s[b]["gates_ready"], now(i))
                for j in range(HALVES):
                    for half in range(2):
                        at = 2 + 2 * j + half
                        free(i, at, f"decay{b}")
                        mm(bank[at][:, :], gates[b][:, j * P:(j + 1) * P],
                           spans[:, 4 * half:4 * half + 4, :].rearrange("p l t -> p (l t)"), True, True)\
                            .then_inc(full[at], 1)
                free(i, 1, f"after{b}")
                mm(bank[1][:, 0:HEADS * DK], after[:, :], gates[b][:, :], True, True).then_inc(full[1], 1)

            def pair_products(i, b):
                pe.wait_ge(s[b]["q_ready"], now(i))
                pe.wait_ge(s[b]["k_ready"], 2 * (i + 2))
                for l in range(LEVELS + 1):
                    j = 6 + l % 2
                    free(i, j, f"pair{b}_{l}")
                    for h in range(HEADS):
                        last = mm(bank[j][:, h * P:(h + 1) * P], k[b][h][:, l, :], q[b][h // 2][:, l, :], True, True)
                    last.then_inc(full[j], 1)

            def outputs(i, b):
                free(i, 2 + 2 * b, f"o{b}")
                pe.wait_ge(s[b]["state_ready"], now(i - 1))
                pe.wait_ge(drained[7], use(i, 7, f"pair{b}_{LEVELS}"))
                pe.wait_ge(drained[3], use(i, 3, f"v{b}"))
                for j in range(HALVES):
                    mm(bank[2 + 2 * b][:, j * 2 * DV:(j + 1) * 2 * DV], q_carry[b][j][:, :], state[b][j][:, :], True, False)
                    for h in (2 * j, 2 * j + 1):
                        last = mm(bank[2 + 2 * b][:, h * DV:(h + 1) * DV], weights[b][:, h, :], v[b][:, h * DV:(h + 1) * DV],
                                  False, h % 2 == 1)
                last.then_inc(full[2 + 2 * b], 1)
                free(i, 3 + 2 * b, f"kv{b}")
                pe.wait_ge(s[b]["k_left_ready"], now(i))
                for j in range(HALVES):
                    last = mm(bank[3 + 2 * b][:, j * 2 * DV:(j + 1) * 2 * DV], k_left[b][:, j * P:(j + 1) * P],
                              v[b][:, j * 2 * DV:(j + 1) * 2 * DV], True, True)
                last.then_inc(full[3 + 2 * b], 1)

            def turn_inputs(i):
                for b in range(NB):
                    pe.wait_ge(s[1 - b]["xT_ready"], now(i - 1 + b))
                    pe.wait_ge(s[b]["xn_ready"], now(i))
                    for c in range(KC):
                        last = nc.tensor.transpose(bank[0][:, b * D + c * P:b * D + (c + 1) * P],
                                                   xn[b][:, c * P:(c + 1) * P], ident[:, :])
                    last.then_inc(s[b]["x_full"], 1)

            def tile(i, following):
                for b in range(NB):
                    pe.wait_ge(s[b]["xT_ready"], now(i))
                    free(i, 1, f"z1_{b}")
                    for c in range(KC):
                        last = mm(bank[1][0:RANK, 0:P], gk1[:, c, :], xT[b][:, c, :], c == 0, c == KC - 1)
                    last.then_inc(full[1], 1)
                project(i, 0, 2, "k", wk)
                for b in range(NB):
                    pe.wait_ge(drained[1], use(i, 1, f"z1_{b}"))
                    free(i, 1, f"z{b}")
                    mm(bank[1][:, 0:HEADS * DK], z1T[b][:, :], gk2[:, :], True, True).then_inc(full[1], 1)
                project(i, 0, 3, "v", wv)
                project_turned(i, 0)
                project(i, 0, 4, "g", wg)
                gate_sums(i, 0)
                project(i, 1, 2, "k", wk)
                project(i, 1, 3, "v", wv)
                project_turned(i, 1)
                project(i, 1, 4, "g", wg)
                gate_sums(i, 1)
                pair_products(i, 0)
                pair_products(i, 1)
                for b in range(NB):
                    outputs(i, b)
                if following is not None:
                    turn_inputs(following)
                for b in range(NB):
                    pe.wait_ge(s[b]["gated_ready"], now(i))
                    free(i, 1, f"oT{b}")
                    for c in range(OC):
                        last = nc.tensor.transpose(bank[1][:, c * P:(c + 1) * P], gated[b][:, c * P:(c + 1) * P],
                                                   ident[:, :])
                    last.then_inc(full[1], 1)
                for b in range(NB):
                    pe.wait_ge(drained[1], use(i, 1, f"oT{b}"))
                    free(i, 2 + 2 * b, f"wo{b}")
                    for c in range(OC):
                        last = mm(bank[2 + 2 * b][:, 0:D], gT[b][:, c, :], wo[:, c, :], c == 0, c == OC - 1)
                    last.then_inc(full[2 + 2 * b], 1)

            pe.wait_ge(const_in, CONSTS)
            turn_inputs(0)
            with pe.Fori(0, TILES - 1) as i:
                tile(i, i + 1)
            tile(TILES - 1, None)

        @block.scalar
        def _(act):
            def keep_inputs(i):
                for b in range(NB):
                    act.wait_ge(s[b]["x_full"], now(i))
                    nc.scalar.copy(xT[b][:, :, :].rearrange("p c t -> p (c t)"), bank[0][:, b * D:(b + 1) * D])\
                        .then_inc(s[b]["xT_ready"], 1)

            def tile(i, following):
                for b in range(NB):
                    act.wait_ge(full[1], use(i, 1, f"z1_{b}"))
                    nc.scalar.copy(z1T[b][:, :], bank[1][0:RANK, 0:P]).then_inc(drained[1], 1)
                for b in range(NB):
                    act.wait_ge(s[b]["small_ready"], now(i))
                    nc.scalar.activation(soft[b][:, :], small[b][:, :], ACT.Exp).then_inc(s[b]["exp_ready"], 1)
                for b in range(NB):
                    act.wait_ge(s[b]["exp_ready"], now(i))
                    nc.scalar.activation(soft[b][:, :], soft[b][:, :], ACT.Ln, bias=1.0)\
                        .then_inc(s[b]["soft_ready"], 1)
                for b in range(NB):
                    act.wait_ge(full[2], use(i, 2, f"k{b}"))
                    nc.scalar.copy(k_rows[b][:, :], bank[2][:, 0:HEADS * DK]).then_inc(drained[2], 1)
                    act.wait_ge(full[3], use(i, 3, f"v{b}"))
                    nc.scalar.copy(v[b][:, :], bank[3][:, :]).then_inc(drained[3], 1)
                    act.wait_ge(full[5], use(i, 5, f"qk{b}"))
                    for j in range(HALVES):
                        nc.scalar.mul(q[b][j][:, DIAG, :], bank[5][:, j * P:(j + 1) * P], Q_SCALE)
                    for h in range(HEADS):
                        rows, n = head_rows(h), HALVES + h // 2
                        last = nc.scalar.copy(k[b][h][rows, DIAG, :], bank[5][rows, n * P:(n + 1) * P])
                    last.then_inc(drained[5], 1)
                    act.wait_ge(s[b]["out_gate_ready"], now(i - 1))
                    act.wait_ge(full[4], use(i, 4, f"g{b}"))
                    nc.scalar.copy(silu[b][:, :], bank[4][:, :]).then_inc(drained[4], 1)
                    act.wait_ge(s[b]["state_ready"], now(i - 1))
                    for at in range(2, 6):
                        j, half = (at - 2) // 2, at % 2
                        act.wait_ge(full[at], use(i, at, f"decay{b}"))
                        nc.scalar.activation(decay[b][j][:, 4 * half:4 * half + 4, :].rearrange("p l t -> p (l t)"),
                                             bank[at][:, :], ACT.Exp, scale=INV_NORM).then_inc(drained[at], 1)
                    act.wait_ge(full[1], use(i, 1, f"after{b}"))
                    nc.scalar.activation(decay_left[b][:, :], bank[1][:, 0:HEADS * DK], ACT.Exp, scale=INV_NORM)\
                        .then_inc(drained[1], 1)
                for b in range(NB):
                    act.wait_ge(drained[4], use(i, 4, f"g{b}"))
                    nc.scalar.activation(silu[b][:, :], silu[b][:, :], ACT.Silu).then_inc(s[b]["silu_ready"], 1)
                for b in range(NB):
                    act.wait_ge(full[2 + 2 * b], use(i, 2 + 2 * b, f"o{b}"))
                    for h in range(HEADS):
                        last = nc.scalar.activation(gated[b][:, h * DV:(h + 1) * DV], bank[2 + 2 * b][:, h * DV:(h + 1) * DV], ACT.Square,
                                                    accum_out=ssum[b][:, h:h + 1])
                    last.then_inc(s[b]["squared"], 1)
                if following is not None:
                    keep_inputs(following)
                for b in range(NB):
                    act.wait_ge(full[1], use(i, 1, f"oT{b}"))
                    nc.scalar.copy(gT[b][:, :, :].rearrange("p c t -> p (c t)"), bank[1][:, :])\
                        .then_inc(drained[1], 1)

            act.wait_ge(filled, 1)
            act.wait_ge(const_in, CONSTS)
            keep_inputs(0)
            with act.Fori(0, TILES - 1) as i:
                tile(i, i + 1)
            tile(TILES - 1, None)

        @block.gpsimd
        def _(pool):
            def roots(i):
                for b in range(NB):
                    pool.wait_ge(s[b]["ve_ready"], now(i))
                    nc.gpsimd.tensor_tensor(rstd[b][:, :], ve[b][:, :], minus_half[:, 0:1], ALU.pow)\
                        .then_inc(s[b]["rstd_ready"], 1)

            def keep_base(i):
                for b in range(NB):
                    pool.wait_ge(s[b]["h3_ready"], now(i - 1))
                    pool.wait_ge(s[b]["h2_ready"], now(i))
                    pool.sem_inc(pool_gate, 1)
                    nc.gpsimd.tensor_copy(base[b][:, :], h2[b][:, :]).then_inc(s[b]["base_ready"], 1)

            def tile(i, following):
                for b in range(NB):
                    pool.wait_ge(drained[5], use(i, 5, f"qk{b}"))
                    pool.wait_ge(drained[3], use(i, 3, f"decay{b}"))
                    for h in range(2):
                        rows = head_rows(h)
                        nc.gpsimd.tensor_tensor(
                            k[b][h][rows, 0:LEVELS, :], decay[b][h // 2][rows, 0:LEVELS, :],
                            k[b][h][rows, DIAG:DIAG + 1, :].to_broadcast([DK, LEVELS, P]), ALU.mult)\
                            .then_inc(s[b]["k_ready"], 1)
                        pool.wait_ge(s[b]["k_ready"], 2 * (i + 1) + h + 1)
                for b in range(NB):
                    pool.wait_ge(s[b]["silu_ready"], now(i))
                    pool.wait_ge(s[b]["gated_ready"], now(i - 1))
                    nc.gpsimd.tensor_tensor(out_gate[b][:, :].rearrange("p (h d) -> p h d", d=DV),
                                            silu[b][:, :].rearrange("p (h d) -> p h d", d=DV),
                                            norm_w[:, :].unsqueeze(1).to_broadcast([P, HEADS, DV]), ALU.mult)\
                        .then_inc(s[b]["out_gate_ready"], 1)
                if following is not None:
                    roots(following)
                for b in range(NB):
                    pool.wait_ge(s[b]["squared"], now(i))
                    pool.sem_inc(pool_gate, 1)
                    nc.gpsimd.tensor_scalar(meansq[b][:, :], ssum[b][:, :], 1.0 / DV, 1e-5, ALU.mult, ALU.add)\
                        .then_inc(s[b]["meansq_ready"], 1)
                    pool.wait_ge(s[b]["meansq_ready"], now(i))
                    nc.gpsimd.tensor_tensor(rms[b][:, :], meansq[b][:, :], minus_half[:, :], ALU.pow)\
                        .then_inc(s[b]["rms_ready"], 1)
                if following is not None:
                    keep_base(following)

            pool.wait_ge(filled, 1)
            pool.wait_ge(const_in, CONSTS)
            roots(0)
            keep_base(0)
            with pool.Fori(0, TILES - 1) as i:
                tile(i, i + 1)
            tile(TILES - 1, None)

        @block.vector
        def _(dve):
            def norms(i):
                for b in range(NB):
                    dve.wait_ge(h1_in[b], 16 * (i + 1))
                    dve.wait_ge(tower_in[b], 16 * (i + 1))
                    dve.wait_ge(s[b]["xn_ready"], now(i - 1))
                    dve.wait_ge(s[b]["base_ready"], now(i - 1))
                    nc.vector.tensor_tensor(h2[b][:, :], h1[b][:, :], tower[b][:, :], ALU.add)\
                        .then_inc(s[b]["h2_ready"], 1)
                for b in range(NB):
                    dve.wait_ge(s[b]["h2_ready"], now(i))
                    dve.sem_inc(dve_gate, 1)
                    nc.vector.bn_stats(stats[b][:, :], h2[b][:, :]).then_inc(s[b]["stats_ready"], 1)
                for b in range(NB):
                    dve.wait_ge(s[b]["stats_ready"], now(i))
                    dve.sem_inc(dve_gate, 1)
                    nc.vector.bn_aggr(mv[b][:, :], stats[b][:, :]).then_inc(s[b]["mv_ready"], 1)
                for b in range(NB):
                    dve.wait_ge(s[b]["mv_ready"], now(i))
                    nc.vector.tensor_scalar(ve[b][:, :], mv[b][:, 1:2], 1e-5, None, ALU.add)\
                        .then_inc(s[b]["ve_ready"], 1)
                for b in range(NB):
                    dve.wait_ge(s[b]["rstd_ready"], now(i))
                    nc.vector.tensor_scalar(xn[b][:, :], h2[b][:, :], mv[b][:, 0:1], rstd[b][:, :], ALU.subtract,
                                            ALU.mult).then_inc(s[b]["xn_ready"], 1)

            def tile(i, following):
                for b in range(NB):
                    dve.wait_ge(s[b]["gates_ready"], now(i - 1))
                    dve.wait_ge(full[1], use(i, 1, f"z{b}"))
                    nc.vector.tensor_tensor(z[b][:, :], bank[1][:, 0:HEADS * DK], gkb[:, :], ALU.add)\
                        .then_inc(drained[1], 1)
                    dve.wait_ge(drained[1], use(i, 1, f"z{b}"))
                    nc.vector.scalar_tensor_tensor(small[b][:, :], z[b][:, :], -1.0, z[b][:, :], ALU.mult, ALU.min)\
                        .then_inc(s[b]["small_ready"], 1)
                for b in range(NB):
                    dve.wait_ge(s[b]["soft_ready"], now(i))
                    dve.wait_ge(full[1], use(i - 1, 1, f"after{b}"))
                    nc.vector.scalar_tensor_tensor(gates[b][:, :], z[b][:, :], 0.0, soft[b][:, :], ALU.min,
                                                   ALU.subtract).then_inc(s[b]["gates_ready"], 1)
                for b in range(NB):
                    dve.wait_ge(drained[5], use(i, 5, f"qk{b}"))
                    for j in range(HALVES):
                        dve.wait_ge(drained[3 + 2 * j], use(i, 3 + 2 * j, f"decay{b}"))
                        nc.vector.tensor_tensor(q[b][j][:, 0:LEVELS, :], decay[b][j][:, 0:LEVELS, :],
                                                q[b][j][:, DIAG:DIAG + 1, :].to_broadcast([P, LEVELS, P]), ALU.mult)
                        nc.vector.tensor_tensor(q_carry[b][j][:, :], decay[b][j][:, CARRY, :], q[b][j][:, DIAG, :],
                                                ALU.mult)
                    for h in range(2, HEADS):
                        rows = head_rows(h)
                        last = nc.vector.tensor_tensor(
                            k[b][h][rows, 0:LEVELS, :], decay[b][h // 2][rows, 0:LEVELS, :],
                            k[b][h][rows, DIAG:DIAG + 1, :].to_broadcast([DK, LEVELS, P]), ALU.mult)
                    last.then_inc(s[b]["q_ready"], 1)
                    dve.wait_ge(drained[2], use(i, 2, f"k{b}"))
                    dve.wait_ge(drained[1], use(i, 1, f"after{b}"))
                    nc.vector.tensor_tensor(k_left[b][:, :], decay_left[b][:, :], k_rows[b][:, :], ALU.mult)\
                        .then_inc(s[b]["k_left_ready"], 1)
                for b in range(NB):
                    for l in range(LEVELS + 1):
                        j = 6 + l % 2
                        if l:
                            dve.wait_ge(drained[6 + (l - 1) % 2], use(i, 6 + (l - 1) % 2, f"pair{b}_{l - 1}"))
                        dve.wait_ge(full[j], use(i, j, f"pair{b}_{l}"))
                        dve.sem_inc(dve_gate, 1)
                        nc.vector.copy_predicated(weights[b][:, :, :],
                                                  pairs[:, l:l + 1, :].to_broadcast([P, HEADS, P]),
                                                  bank[j][:, :].rearrange("p (h t) -> p h t", t=P))\
                            .then_inc(drained[j], 1)
                if following is not None:
                    norms(following)
                for b in range(NB):
                    dve.wait_ge(s[b]["out_gate_ready"], now(i))
                    dve.wait_ge(s[b]["rms_ready"], now(i))
                    for h in range(HEADS):
                        cols = slice(h * DV, (h + 1) * DV)
                        last = nc.vector.scalar_tensor_tensor(gated[b][:, cols], bank[2 + 2 * b][:, cols],
                                                              rms[b][:, h:h + 1], out_gate[b][:, cols], ALU.mult,
                                                              ALU.mult)
                    last.then_inc(drained[2 + 2 * b], 1)
                    dve.wait_ge(drained[2 + 2 * b], use(i, 2 + 2 * b, f"o{b}"))
                    dve.sem_inc(s[b]["gated_ready"], 1)
                for b in range(NB):
                    dve.wait_ge(s[b]["state_ready"], now(i - 1))
                    dve.wait_ge(full[3 + 2 * b], use(i, 3 + 2 * b, f"kv{b}"))
                    for h in range(HEADS):
                        j, rows, cols = h // 2, head_rows(h), slice((h % 2) * DV, (h % 2 + 1) * DV)
                        last = nc.vector.scalar_tensor_tensor(
                            state[b][j][rows, cols], state[b][j][rows, cols], decay[b][j][rows, CARRY, P - 1:P],
                            bank[3 + 2 * b][rows, h * DV:(h + 1) * DV], ALU.mult, ALU.add)
                    last.then_inc(drained[3 + 2 * b], 1)
                    dve.wait_ge(drained[3 + 2 * b], use(i, 3 + 2 * b, f"kv{b}"))
                    dve.sem_inc(s[b]["state_ready"], 1)
                for b in range(NB):
                    dve.wait_ge(h3_stored[b], 16 * (i + 1))
                    dve.wait_ge(s[b]["base_ready"], now(i))
                    dve.wait_ge(full[2 + 2 * b], use(i, 2 + 2 * b, f"wo{b}"))
                    nc.vector.tensor_tensor(h3[b][:, :], bank[2 + 2 * b][:, 0:D], base[b][:, :], ALU.add)\
                        .then_inc(drained[2 + 2 * b], 1)
                    dve.wait_ge(drained[2 + 2 * b], use(i, 2 + 2 * b, f"wo{b}"))
                    dve.sem_inc(s[b]["h3_ready"], 1)

            for b in range(NB):
                for h in range(HEADS):
                    nc.vector.memset(k[b][h][:, :, :], 0.0)
                for j in range(HALVES):
                    nc.vector.memset(state[b][j][:, :], 0.0)
                nc.vector.memset(weights[b][:, :, :], 0.0)
            nc.vector.memset(minus_half[:, :], -0.5).then_inc(filled, 1)
            dve.wait_ge(const_in, CONSTS)
            dve.wait_ge(filled, 1)
            norms(0)
            with dve.Fori(0, TILES - 1) as i:
                tile(i, i + 1)
            tile(TILES - 1, None)


def gla_consts():
    import numpy as np
    N, LEVELS = 128, 7
    u = np.arange(N)[:, None]
    t = np.arange(N)[None, :]
    spans = np.zeros((N, LEVELS + 1, N), np.float32)
    pairs = np.zeros((N, LEVELS + 1, N), np.int32)
    for l in range(LEVELS):
        m = N >> (l + 1)
        middle = t // (2 * m) * (2 * m) + m
        right = t >= middle
        spans[:, l, :] = np.where(right, (u >= middle) & (u <= t), (u > t) & (u < middle))
        s = u
        pairs[:, l, :] = right & (s // (2 * m) == t // (2 * m)) & (s < middle)
    spans[:, LEVELS, :] = u <= t
    pairs[:, LEVELS, :] = u == t
    after = (u > t).astype(np.float32)
    return spans, after, pairs


def moe_route(nc, ident_dram, h3_dram, gate_w_dram, gate_b_dram, h3_all, xT_all, comb_all):
    NB, T, D = h3_dram.shape
    KC = D // P
    LANES = 4
    ITERS = NB * T // P // LANES
    EXPERTS = gate_w_dram.shape[1]
    TOP, WIDE = 4, 8
    SLOTS = EXPERTS + WIDE
    LOWEST, TAKEN = -3.0e38, 3.0e38
    ROUTE_SCALE = 2.5

    with ExitStack() as ctx:
        ctx.enter_context(nc.cleanup_on_exit())
        def sb(name, shape, dt=F32):
            return ctx.enter_context(nc.sbuf_tensor("mr_" + name, shape, dt))

        def sem(name):
            return nc.alloc_semaphore("mr_" + name)

        def each(name, shape):
            return [sb(f"{name}{b}", shape) for b in range(LANES)]

        ident = sb("ident", [P, P])
        gate_w = sb("gate_w", [P, KC, EXPERTS])
        gate_b = sb("gate_b", [P, EXPERTS])
        minus_half = sb("minus_half", [P, 1])
        stats, mv, ve, rstd = each("stats", [P, 6]), each("mv", [P, 2]), each("ve", [P, 1]), each("rstd", [P, 1])
        xn, xT = each("xn", [P, D]), each("xT", [P, KC, P])
        scores, biased = each("scores", [P, EXPERTS]), each("biased", [P, SLOTS])
        best, chosen = each("best", [P, WIDE]), each("chosen", [P, WIDE])
        marked, taken, total = each("marked", [P, SLOTS]), each("taken", [P, EXPERTS]), each("total", [P, 1])
        t_bank = [ctx.enter_context(nc.psum_tensor(f"mr_t{b}", [P, 512], F32)) for b in range(LANES)]
        g_bank = [ctx.enter_context(nc.psum_tensor(f"mr_g{b}", [P, 512], F32)) for b in range(LANES)]
        const_in, h3_in, filled = sem("const_in"), sem("h3_in"), sem("filled")
        NAMES = ["stats_ready", "mv_ready", "ve_ready", "rstd_ready", "xn_ready", "t_full", "xT_ready", "xT_kept",
                 "g_full", "scores_ready", "biased_ready", "best_ready", "chosen_ready", "marked_ready", "taken_ready",
                 "weights_ready", "total_ready", "inverse_ready", "comb_ready"]
        s = [{n: sem(f"{n}{b}") for n in NAMES} for b in range(LANES)]
        act_gate, dve_gate, pool_gate = sem("act_gate"), sem("dve_gate"), sem("pool_gate")

        def now(i):
            return i + 2

        def rows(b, i):
            return bass.ds(b * ITERS + i, 1)

        block = ctx.enter_context(nc.Block())

        @block.sync
        def _(sp):
            for b in range(LANES):
                for n in NAMES:
                    sp.sem_inc(s[b][n], 1)
            sp.dma_start(h3_all[:, :, :], h3_dram.rearrange("b (i p) d -> p (b i) d", p=P)).then_inc(h3_in, 16)
            for dst, src in ((ident[:, :], ident_dram), (gate_w[:, :, :], gate_w_dram.rearrange("(c p) n -> p c n", p=P)),
                             (gate_b[:, :], gate_b_dram.partition_broadcast(P))):
                sp.dma_start(dst, src).then_inc(const_in, 16)

        @block.vector
        def _(dve):
            nc.vector.memset(minus_half[:, :], -0.5)
            nc.vector.memset(comb_all[:, :, :], 1.0)
            for b in range(LANES):
                nc.vector.memset(biased[b][:, :], LOWEST)
                nc.vector.memset(chosen[b][:, :], LOWEST)
            nc.vector.memset(xn[0][:, :], 0.0).then_inc(filled, 1)
            dve.wait_ge(const_in, 48)
            dve.wait_ge(h3_in, 16)
            dve.wait_ge(filled, 1)
            with dve.Fori(0, ITERS) as i:
                for b in range(LANES):
                    nc.vector.bn_stats(stats[b][:, :], h3_all[:, rows(b, i), :].rearrange("p a d -> p (a d)"))\
                        .then_inc(s[b]["stats_ready"], 1)
                for b in range(LANES):
                    dve.wait_ge(s[b]["stats_ready"], now(i))
                    dve.sem_inc(dve_gate, 1)
                    nc.vector.bn_aggr(mv[b][:, :], stats[b][:, :]).then_inc(s[b]["mv_ready"], 1)
                for b in range(LANES):
                    dve.wait_ge(s[b]["mv_ready"], now(i))
                    nc.vector.tensor_scalar(ve[b][:, :], mv[b][:, 1:2], 1e-5, None, ALU.add)\
                        .then_inc(s[b]["ve_ready"], 1)
                for b in range(LANES):
                    dve.wait_ge(s[b]["rstd_ready"], now(i))
                    dve.wait_ge(s[b]["t_full"], now(i - 1))
                    dve.sem_inc(dve_gate, 1)
                    nc.vector.tensor_scalar(xn[b][:, :], h3_all[:, rows(b, i), :].rearrange("p a d -> p (a d)"),
                                            mv[b][:, 0:1], rstd[b][:, :], ALU.subtract, ALU.mult)\
                        .then_inc(s[b]["xn_ready"], 1)
                for b in range(LANES):
                    dve.wait_ge(s[b]["scores_ready"], now(i))
                    dve.wait_ge(s[b]["taken_ready"], now(i - 1))
                    nc.vector.tensor_tensor(biased[b][:, 0:EXPERTS], scores[b][:, :], gate_b[:, :], ALU.add)\
                        .then_inc(s[b]["biased_ready"], 1)
                for b in range(LANES):
                    dve.wait_ge(s[b]["biased_ready"], now(i))
                    dve.wait_ge(s[b]["chosen_ready"], now(i - 1))
                    dve.sem_inc(dve_gate, 1)
                    nc.vector.max(best[b][:, :], biased[b][:, :]).then_inc(s[b]["best_ready"], 1)
                for b in range(LANES):
                    dve.wait_ge(s[b]["best_ready"], now(i))
                    dve.wait_ge(s[b]["marked_ready"], now(i - 1))
                    nc.vector.tensor_copy(chosen[b][:, 0:TOP], best[b][:, 0:TOP]).then_inc(s[b]["chosen_ready"], 1)
                for b in range(LANES):
                    dve.wait_ge(s[b]["chosen_ready"], now(i))
                    dve.sem_inc(dve_gate, 1)
                    nc.vector.match_replace(marked[b][:, :], chosen[b][:, :], biased[b][:, :], TAKEN)\
                        .then_inc(s[b]["marked_ready"], 1)
                for b in range(LANES):
                    dve.wait_ge(s[b]["marked_ready"], now(i))
                    nc.vector.tensor_tensor(taken[b][:, :], marked[b][:, 0:EXPERTS], biased[b][:, 0:EXPERTS],
                                            ALU.not_equal).then_inc(s[b]["taken_ready"], 1)
                for b in range(LANES):
                    dve.wait_ge(s[b]["taken_ready"], now(i))
                    nc.vector.tensor_tensor(taken[b][:, :], taken[b][:, :], scores[b][:, :], ALU.mult)\
                        .then_inc(s[b]["weights_ready"], 1)
                for b in range(LANES):
                    dve.wait_ge(s[b]["weights_ready"], now(i))
                    nc.vector.tensor_reduce(total[b][:, :], taken[b][:, :], AX, ALU.add)\
                        .then_inc(s[b]["total_ready"], 1)
                for b in range(LANES):
                    dve.wait_ge(s[b]["total_ready"], now(i))
                    nc.vector.reciprocal(total[b][:, :], total[b][:, :]).then_inc(s[b]["inverse_ready"], 1)
                for b in range(LANES):
                    dve.wait_ge(s[b]["inverse_ready"], now(i))
                    dve.sem_inc(dve_gate, 1)
                    nc.vector.tensor_scalar(comb_all[:, rows(b, i), 0:EXPERTS].rearrange("p a d -> p (a d)"),
                                            taken[b][:, :], total[b][:, :], ROUTE_SCALE, ALU.mult, ALU.mult)\
                        .then_inc(s[b]["comb_ready"], 1)
                for b in range(LANES):
                    dve.wait_ge(s[b]["comb_ready"], now(i))

        @block.gpsimd
        def _(pool):
            pool.wait_ge(filled, 1)
            with pool.Fori(0, ITERS) as i:
                for b in range(LANES):
                    pool.wait_ge(s[b]["ve_ready"], now(i))
                    nc.gpsimd.tensor_tensor(rstd[b][:, :], ve[b][:, :], minus_half[:, :], ALU.pow)\
                        .then_inc(s[b]["rstd_ready"], 1)
                for b in range(LANES):
                    pool.wait_ge(s[b]["xT_ready"], now(i))
                    pool.sem_inc(pool_gate, 1)
                    nc.gpsimd.tensor_copy(xT_all[:, rows(b, i), :, :].rearrange("p a c t -> p (a c t)"),
                                          xT[b][:, :, :].rearrange("p c t -> p (c t)")).then_inc(s[b]["xT_kept"], 1)

        @block.tensor
        def _(pe):
            pe.wait_ge(const_in, 48)
            with pe.Fori(0, ITERS) as i:
                for b in range(LANES):
                    pe.wait_ge(s[b]["xn_ready"], now(i))
                    for c in range(KC):
                        last = nc.tensor.transpose(t_bank[b][:, c * P:(c + 1) * P], xn[b][:, c * P:(c + 1) * P],
                                                   ident[:, :])
                    last.then_inc(s[b]["t_full"], 1)
                for b in range(LANES):
                    pe.wait_ge(s[b]["scores_ready"], now(i - 1))
                    pe.wait_ge(s[b]["xT_ready"], now(i))
                    for c in range(KC):
                        last = nc.tensor.matmul(g_bank[b][:, 0:EXPERTS], xT[b][:, c, :], gate_w[:, c, :], start=c == 0,
                                                stop=c == KC - 1)
                    last.then_inc(s[b]["g_full"], 1)

        @block.scalar
        def _(act):
            with act.Fori(0, ITERS) as i:
                for b in range(LANES):
                    act.wait_ge(s[b]["xT_kept"], now(i - 1))
                    act.wait_ge(s[b]["t_full"], now(i))
                    nc.scalar.copy(xT[b][:, :, :].rearrange("p c t -> p (c t)"), t_bank[b][:, 0:D])\
                        .then_inc(s[b]["xT_ready"], 1)
                for b in range(LANES):
                    act.wait_ge(s[b]["g_full"], now(i))
                    act.wait_ge(s[b]["comb_ready"], now(i - 1))
                    nc.scalar.activation(scores[b][:, :], g_bank[b][:, 0:EXPERTS], ACT.Sigmoid)\
                        .then_inc(s[b]["scores_ready"], 1)


def moe_experts(nc, ident_dram, w13, w2, h3_all, xT_all, comb_all, out_dram):
    _, KC, EXPERTS, GU = w13.shape
    D = w2.shape[2]
    INTER = GU // 2
    NB, T, _ = out_dram.shape
    TILES = T // P
    PAIRS = (EXPERTS + 1) // 2
    STEPS = [(b, p) for b in range(NB) for p in range(PAIRS)]
    G_RING = 3
    G_USES = len(STEPS) // G_RING
    assert len(STEPS) % G_RING == 0 and len(STEPS) % 2 == 0 and INTER == P

    def experts(p):
        return range(2 * p, min(2 * p + 2, EXPERTS))

    with ExitStack() as ctx:
        ctx.enter_context(nc.cleanup_on_exit())
        def sb(name, shape, dt=F32):
            return ctx.enter_context(nc.sbuf_tensor("me_" + name, shape, dt))

        def sem(name):
            return nc.alloc_semaphore("me_" + name)

        def pb(name):
            return ctx.enter_context(nc.psum_tensor("me_bank_" + name, [P, 512], F32))

        ident = sb("ident", [P, P])
        xT = [sb(f"xT{b}", [P, KC, P]) for b in range(NB)]
        comb = [sb(f"comb{b}", [P, EXPERTS]) for b in range(NB)]
        silu = [sb(f"silu{r}", [P, 2, P]) for r in range(2)]
        hidden = [sb(f"hidden{r}", [P, 2, P]) for r in range(2)]
        hT = [sb(f"hT{r}", [P, 2, P]) for r in range(2)]
        y = [sb(f"y{b}", [P, D]) for b in range(NB)]
        g_bank = [pb(f"g{r}") for r in range(G_RING)]
        t_bank = [pb(f"t{r}") for r in range(2)]
        y_bank = [pb(f"y{b}") for b in range(NB)]
        const_in = sem("const_in")
        g_full, g_drained = [sem(f"g_full{r}") for r in range(G_RING)], [sem(f"g_drained{r}") for r in range(G_RING)]
        t_full, t_drained = [sem(f"t_full{r}") for r in range(2)], [sem(f"t_drained{r}") for r in range(2)]
        silu_ready = [sem(f"silu_ready{r}") for r in range(2)]
        y_full, y_ready = [sem(f"y_full{b}") for b in range(NB)], [sem(f"y_ready{b}") for b in range(NB)]
        xT_copied, comb_copied = [sem(f"xT_copied{b}") for b in range(NB)], [sem(f"comb_copied{b}") for b in range(NB)]
        y_stored = [sem(f"y_stored{b}") for b in range(NB)]
        act_gate, dve_gate, pool_gate, sp_gate = (sem("act_gate"), sem("dve_gate"), sem("pool_gate"), sem("sp_gate"))
        T_USES = len(STEPS) // 2

        def count(per, i, pos):
            return per * (i + 1) + pos + 1

        block = ctx.enter_context(nc.Block())

        @block.sync
        def _(sp):
            for r in range(G_RING):
                sp.sem_inc(g_full[r], G_USES)
                sp.sem_inc(g_drained[r], G_USES)
            for r in range(2):
                for x in (t_full[r], t_drained[r], silu_ready[r]):
                    sp.sem_inc(x, T_USES)
            for b in range(NB):
                for x in (y_full[b], y_ready[b], xT_copied[b], comb_copied[b]):
                    sp.sem_inc(x, 1)
                sp.sem_inc(y_stored[b], 16)
            sp.dma_start(ident[:, :], ident_dram).then_inc(const_in, 16)
            with sp.Fori(0, TILES) as i:
                for b in range(NB):
                    sp.wait_ge(y_stored[b], 16 * (i + 1))
                    sp.sem_inc(sp_gate, 1)
                    sp.wait_ge(y_ready[b], count(1, i, 0))
                    sp.sem_inc(sp_gate, 1)
                    sp.dma_start(out_dram[b, bass.ds(i * P, P), :], y[b][:, :]).then_inc(y_stored[b], 16)
            for b in range(NB):
                sp.wait_ge(y_stored[b], 16 * (TILES + 1))

        @block.gpsimd
        def _(pool):
            with pool.Fori(0, TILES) as i:
                for b in range(NB):
                    pool.wait_ge(y_full[b], count(1, i - 1, 0))
                    pool.sem_inc(pool_gate, 1)
                    nc.gpsimd.tensor_copy(xT[b][:, :, :].rearrange("p c t -> p (c t)"),
                                          xT_all[:, bass.ds(b * TILES + i, 1), :, :].rearrange("p a c t -> p (a c t)"))\
                        .then_inc(xT_copied[b], 1)
                    nc.gpsimd.tensor_copy(comb[b][:, :], comb_all[:, bass.ds(b * TILES + i, 1), :]
                                          .rearrange("p a e -> p (a e)")).then_inc(comb_copied[b], 1)

        @block.tensor
        def _(pe):
            def gate_up(i, n):
                b, p = STEPS[n]
                r, pos = n % G_RING, n // G_RING
                if p == 0:
                    pe.wait_ge(xT_copied[b], count(1, i, 0))
                pe.wait_ge(g_drained[r], count(G_USES, i, pos) - 1)
                cols = len(experts(p)) * GU
                for c in range(KC):
                    last = nc.tensor.matmul(g_bank[r][:, 0:cols], xT[b][:, c, :],
                                            w13[:, c, experts(p).start:experts(p).stop, :].rearrange("p e n -> p (e n)"),
                                            start=c == 0, stop=c == KC - 1)
                last.then_inc(g_full[r], 1)

            def turn(i, n):
                b, p = STEPS[n]
                pe.wait_ge(g_drained[n % G_RING], count(G_USES, i, n // G_RING))
                pe.wait_ge(t_drained[n % 2], count(T_USES, i, n // 2) - 1)
                for j in range(len(experts(p))):
                    last = nc.tensor.transpose(t_bank[n % 2][:, j * P:(j + 1) * P], hidden[n % 2][:, j, :], ident[:, :])
                last.then_inc(t_full[n % 2], 1)

            def down(i, n):
                b, p = STEPS[n]
                if p == 0:
                    pe.wait_ge(y_ready[b], count(1, i - 1, 0))
                pe.wait_ge(t_drained[n % 2], count(T_USES, i, n // 2))
                for j, e in enumerate(experts(p)):
                    last = nc.tensor.matmul(y_bank[b][:, 0:D], hT[n % 2][:, j, :], w2[:, e, :], start=e == 0,
                                            stop=e == EXPERTS - 1)
                if p == PAIRS - 1:
                    last.then_inc(y_full[b], 1)

            pe.wait_ge(const_in, 16)
            with pe.Fori(0, TILES) as i:
                for n in range(len(STEPS) + 3):
                    if n < len(STEPS):
                        gate_up(i, n)
                    if 0 <= n - 2 < len(STEPS):
                        turn(i, n - 2)
                    if 0 <= n - 3:
                        down(i, n - 3)

        @block.scalar
        def _(act):
            def gates(i, n):
                b, p = STEPS[n]
                m = len(experts(p))
                before = (i, n - 2) if n >= 2 else (i - 1, n - 2 + len(STEPS))
                act.wait_ge(g_drained[before[1] % G_RING], count(G_USES, before[0], before[1] // G_RING))
                act.wait_ge(g_full[n % G_RING], count(G_USES, i, n // G_RING))
                nc.scalar.activation(silu[n % 2][:, 0:m, :],
                                     g_bank[n % G_RING][:, 0:m * GU].rearrange("p (e g d) -> p e g d", e=m, g=2)[:, :, 0, :],
                                     ACT.Silu).then_inc(silu_ready[n % 2], 1)

            def keep(i, n):
                m = len(experts(STEPS[n][1]))
                act.wait_ge(t_full[n % 2], count(T_USES, i, n // 2))
                nc.scalar.copy(hT[n % 2][:, 0:m, :].rearrange("p e t -> p (e t)"), t_bank[n % 2][:, 0:m * P])\
                    .then_inc(t_drained[n % 2], 1)

            with act.Fori(0, TILES) as i:
                for n in range(len(STEPS) + 2):
                    if n < len(STEPS):
                        gates(i, n)
                    if 0 <= n - 2:
                        keep(i, n - 2)

        @block.vector
        def _(dve):
            def weigh(i, n):
                b, p = STEPS[n]
                if p == 0:
                    dve.wait_ge(comb_copied[b], count(1, i, 0))
                before = (i, n - 2) if n >= 2 else (i - 1, n - 2 + len(STEPS))
                dve.wait_ge(t_full[n % 2], count(T_USES, before[0], before[1] // 2))
                dve.wait_ge(silu_ready[n % 2], count(T_USES, i, n // 2))
                for j, e in enumerate(experts(p)):
                    last = nc.vector.scalar_tensor_tensor(
                        hidden[n % 2][:, j, :], g_bank[n % G_RING][:, j * GU + INTER:(j + 1) * GU], comb[b][:, e:e + 1],
                        silu[n % 2][:, j, :], ALU.mult, ALU.mult)
                last.then_inc(g_drained[n % G_RING], 1)

            def residual(i, b):
                dve.wait_ge(y_stored[b], 16 * (i + 1))
                dve.wait_ge(y_full[b], count(1, i, 0))
                nc.vector.tensor_tensor(y[b][:, :], y_bank[b][:, 0:D],
                                        h3_all[:, bass.ds(b * TILES + i, 1), :].rearrange("p a d -> p (a d)"), ALU.add)\
                    .then_inc(y_ready[b], 1)

            with dve.Fori(0, TILES) as i:
                for n in range(len(STEPS)):
                    weigh(i, n)
                    if n == PAIRS + 4:
                        residual(i, 0)
                residual(i, 1)


def moe_stage(nc, ident, gate_w, gate_b, w13, w2, h3_dram, out_dram):
    TILES = h3_dram.shape[0] * h3_dram.shape[1] // P
    with ExitStack() as ctx:
        h3_all = ctx.enter_context(nc.sbuf_tensor("h3_all", [P, TILES, 256], F32))
        xT_all = ctx.enter_context(nc.sbuf_tensor("xT_all", [P, TILES, 2, P], F32))
        comb_all = ctx.enter_context(nc.sbuf_tensor("comb_all", [P, TILES, 17], F32))
        moe_route(nc, ident, h3_dram, gate_w, gate_b, h3_all, xT_all, comb_all)
        moe_experts(nc, ident, w13, w2, h3_all, xT_all, comb_all, out_dram)


def second_layer(nc, gla_inputs, ident, gate_w, gate_b, w13_dram, w2_dram, h3_dram, out_dram):
    D, EXPERTS, GU = w13_dram.shape
    with ExitStack() as ctx:
        w13 = ctx.enter_context(nc.sbuf_tensor("w13", [P, D // P, EXPERTS, GU], F32))
        w2 = ctx.enter_context(nc.sbuf_tensor("w2", [P, EXPERTS, D], F32))
        gla_stage(nc, *gla_inputs, h3_dram, ((w13[:, :, :, :], w13_dram.rearrange("(c p) e n -> p c e n", p=P)), (w2[:, :, :], w2_dram)))
        moe_stage(nc, ident, gate_w, gate_b, w13, w2, h3_dram, out_dram)


def zero_rows(nc, h_versions):
    LAYERS, NB, _, D = h_versions.shape
    with ExitStack() as ctx:
        ctx.enter_context(nc.cleanup_on_exit())
        zeros = ctx.enter_context(nc.sbuf_tensor("zero_row", [1, LAYERS * NB * D], F32))
        filled = nc.alloc_semaphore("zero_filled")
        stored = nc.alloc_semaphore("zero_stored")
        block = ctx.enter_context(nc.Block())

        @block.vector
        def _(dve):
            nc.vector.memset(zeros[:, :], 0.0).then_inc(filled, 1)

        @block.sync
        def _(sp):
            sp.wait_ge(filled, 1)
            sp.dma_start(h_versions[:, :, 0:1, :].rearrange("l b t d -> t (l b) d"),
                         zeros[:, :].rearrange("p (a d) -> p a d", d=D)).then_inc(stored, 16)
            sp.wait_ge(stored, 16)


def program(nc, a, out):
    NB, T, D = out.shape
    LAYERS = a["ffn_wqkv"].shape[0]
    h1 = nc.dram_tensor("h1_rows", (NB, T, D), F32).ap()
    h3 = nc.dram_tensor("h3_rows", (NB, T, D), F32).ap()
    h_versions = nc.dram_tensor("tower_rows", (LAYERS + 1, NB, T + 1, D), F32).ap()
    zero_rows(nc, h_versions)
    mla_stage(nc, a["ids"], a["embedding"], a["ident"], a["rope"], a["causal"], a["mla_w_x"], a["mla_g_kv"],
              a["mla_w_kvdec"], a["mla_w_q"], a["mla_w_o"], h1, h_versions[0, :, 1:T + 1, :])
    local_tower(nc, a["ident"], a["trig"], a["band"], a["shift"], h_versions, a["qk_scale"], a["ffn_wqkv"],
                a["ffn_wo"], a["ffn_ln_g"], a["ffn_ln_b"], a["ffn_w1"], a["ffn_b1"], a["ffn_w2"], a["ffn_b2"])
    second_layer(nc, (a["ident"], a["spans"], a["after"], a["pairs"], a["gla_wqk"], a["gla_wk"], a["gla_wv"],
                      a["gla_wg"], a["gla_gk1"], a["gla_gk2"], a["gla_gkb"], a["gla_norm"], a["gla_wo"], h1,
                      h_versions[LAYERS, :, 1:T + 1, :]), a["ident"], a["gate_w"], a["gate_b"], a["w13"], a["w2"], h3,
                 out)


def kernel(x, L0_tok_embedding, L0_attn_W_kv, L0_attn_g_kv, L0_attn_W_kdec, L0_attn_W_vdec, L0_attn_W_q,
           L0_attn_W_qdec, L0_attn_W_krope, L0_attn_W_qrope, L0_attn_W_o, L0_ffn_Wqkv, L0_ffn_q_scale, L0_ffn_k_scale,
           L0_ffn_Wo, L0_ffn_ln_g, L0_ffn_ln_b, L0_ffn_W1, L0_ffn_b1, L0_ffn_W2, L0_ffn_b2, L1_attn_Wq, L1_attn_Wk,
           L1_attn_Wv, L1_attn_Wg, L1_attn_gk_w1, L1_attn_gk_w2, L1_attn_gk_b2, L1_attn_g_norm_w, L1_attn_Wo,
           L1_ffn_input_ids, L1_ffn_gate_w, L1_ffn_gate_b, L1_ffn_w13, L1_ffn_w2, L1_ffn_w13_s, L1_ffn_w2_s):
    import concourse.bacc as bacc
    import numpy as np
    from concourse.bass_utils import run_bass_kernel_spmd

    host = np.asarray
    NB, T = x.shape
    D = L0_tok_embedding.shape[1]
    ident, trig, band, shift = tower_consts(T // P)
    rope, causal = mla_consts(T)
    spans, after, pairs = gla_consts()
    a = dict(
        ident=ident, trig=trig, band=band, shift=shift, rope=rope, causal=causal, spans=spans, after=after,
        pairs=pairs,
        ids=host(x).reshape(NB * T // P, P).T,
        embedding=host(L0_tok_embedding),
        mla_w_x=np.concatenate([host(L0_attn_W_krope), host(L0_attn_W_kv), host(L0_attn_W_q)], 1),
        mla_g_kv=host(L0_attn_g_kv),
        mla_w_kvdec=np.concatenate([host(L0_attn_W_kdec), host(L0_attn_W_vdec)], 1),
        mla_w_q=np.concatenate([host(L0_attn_W_qrope), host(L0_attn_W_qdec)], 1),
        mla_w_o=host(L0_attn_W_o),
        qk_scale=np.stack([host(L0_ffn_q_scale), host(L0_ffn_k_scale)], 1),
        ffn_wqkv=host(L0_ffn_Wqkv), ffn_wo=host(L0_ffn_Wo), ffn_ln_g=host(L0_ffn_ln_g), ffn_ln_b=host(L0_ffn_ln_b),
        ffn_w1=host(L0_ffn_W1), ffn_b1=host(L0_ffn_b1), ffn_w2=host(L0_ffn_W2), ffn_b2=host(L0_ffn_b2),
        gla_wqk=np.concatenate([host(L1_attn_Wq), host(L1_attn_Wk)], 1),
        gla_wk=host(L1_attn_Wk), gla_wv=host(L1_attn_Wv), gla_wg=host(L1_attn_Wg), gla_gk1=host(L1_attn_gk_w1),
        gla_gk2=host(L1_attn_gk_w2), gla_gkb=host(L1_attn_gk_b2), gla_norm=host(L1_attn_g_norm_w),
        gla_wo=host(L1_attn_Wo),
        gate_w=host(L1_ffn_gate_w).T, gate_b=host(L1_ffn_gate_b),
        w13=np.concatenate([host(L1_ffn_w13), host(L1_ffn_w13_s)[None]]).transpose(2, 0, 1),
        w2=np.concatenate([host(L1_ffn_w2), host(L1_ffn_w2_s)[None]]).transpose(2, 0, 1),
    )
    a = {n: np.ascontiguousarray(v) for n, v in a.items()}

    nc = bacc.Bacc("TRN2", target_bir_lowering=False, num_devices=1)
    aps = {n: nc.dram_tensor("in_" + n, v.shape, mybir.dt.int32 if n in ("ids", "pairs") else F32,
                             kind="ExternalInput").ap() for n, v in a.items()}
    out = nc.dram_tensor("out_0", (NB, T, D), F32, kind="ExternalOutput").ap()
    program(nc, aps, out)
    result = run_bass_kernel_spmd(nc, [{"in_" + n: v for n, v in a.items()}], core_ids=[0])
    return result.results[0]["out_0"]
```
